# Optimizing a Trainium2 kernel written in Bass

```python
import numpy as np
import jax
import jax.numpy as jnp

def _softmax(x, axis=-1):
    return jax.nn.softmax(x, axis=axis)

def _gelu(x):
    return jax.nn.gelu(x, approximate=True)

def _silu(x):
    return jax.nn.silu(x)

def _sigmoid(x):
    return jax.nn.sigmoid(x)

def _layernorm(x, axis=-1, eps=1e-05):
    m = jnp.mean(x, axis=axis, keepdims=True)
    v = jnp.var(x, axis=axis, keepdims=True)
    return (x - m) / jnp.sqrt(v + eps)

def _scatter_add(tgt, idx, src, axis=0):
    return tgt.at[idx].add(src)

def _segment_sum(src, seg, n):
    return jax.ops.segment_sum(src, seg, n)
kernel_name = 'mk_hybrid_d1_jaxref_r4_d764dd'

def setup_inputs(seed: int=0):
    np.random.seed(seed)
    _w = jnp.asarray

    def _L0_attn_a_setup():
        import jax, jax.numpy as jnp
        import numpy as np
        N_EMBD = 256
        BLOCK_SIZE = 512
        ATTN_SPAN = 64
        LN_EPS = 1e-05

        def _band_mask(T, span, dtype):
            ones = jnp.ones((T, T), dtype=dtype)
            return jnp.tril(ones, 0) * (1.0 - jnp.tril(ones, -span))

        def _layer_norm(h, w, b):
            mu = jnp.mean(h, axis=-1, keepdims=True)
            var = jnp.var(h, axis=-1, keepdims=True)
            return (h - mu) * jax.lax.rsqrt(var + LN_EPS) * w + b
        key = jax.random.key(seed)
        k_x, k_w, k_b, k_lw = jax.random.split(key, 4)
        B, T, C = (4, BLOCK_SIZE, N_EMBD)
        x = jax.random.normal(k_x, (B, T, C), dtype=jnp.float32)
        lim = 1.0 / np.sqrt(C)
        W_qkv = jax.random.uniform(k_w, (C, 3 * C), minval=-lim, maxval=lim, dtype=jnp.float32)
        b_qkv = jax.random.uniform(k_b, (3 * C,), minval=-lim, maxval=lim, dtype=jnp.float32)
        ln_w = jnp.ones((C,), dtype=jnp.float32)
        ln_b = jnp.zeros((C,), dtype=jnp.float32)
        return {'x': x, 'W_qkv': W_qkv, 'b_qkv': b_qkv, 'ln_w': ln_w, 'ln_b': ln_b}
    _L0_attn_a_in = _L0_attn_a_setup()

    def _L0_attn_b_setup():
        import jax, jax.numpy as jnp
        import numpy as np
        EPS = 1e-06
        N_HEADS = 16

        def _heads(t, B, N, H, Dk):
            return t.reshape(B, N, H, Dk).transpose(0, 2, 1, 3)
        key = jax.random.key(seed)
        ks = jax.random.split(key, 5)
        B, N, D = (64, 128, 256)
        x = jax.random.normal(ks[0], (B, N, D), dtype=jnp.float32)
        s = 0.02
        W_q = jax.random.normal(ks[1], (D, D), dtype=jnp.float32) * s
        W_k = jax.random.normal(ks[2], (D, D), dtype=jnp.float32) * s
        W_v = jax.random.normal(ks[3], (D, D), dtype=jnp.float32) * s
        W_o = jax.random.normal(ks[4], (D, D), dtype=jnp.float32) * s
        z = jnp.zeros((D,), dtype=jnp.float32)
        return {'x': x, 'W_q': W_q, 'b_q': z, 'W_k': W_k, 'b_k': z, 'W_v': W_v, 'b_v': z, 'W_o': W_o, 'b_o': z}
    _L0_attn_b_in = _L0_attn_b_setup()

    def _L0_ffn_setup():
        import jax, jax.numpy as jnp
        import numpy as np
        B, S, D, H, E, K = (4, 512, 256, 512, 8, 2)
        TEMP = 5.0
        EPS = 1e-09
        key = jax.random.key(seed)
        k_x, k_wg, k_w1, k_w2 = jax.random.split(key, 4)
        scale = 0.02
        return {'x': jax.random.normal(k_x, (B, S, D), dtype=jnp.float32), 'Wg': jax.random.normal(k_wg, (D, E), dtype=jnp.float32) * scale, 'bg': jnp.zeros((E,), dtype=jnp.float32), 'W1': jax.random.normal(k_w1, (E, D, H), dtype=jnp.float32) * scale, 'b1': jnp.zeros((E, H), dtype=jnp.float32), 'W2': jax.random.normal(k_w2, (E, H, D), dtype=jnp.float32) * scale, 'b2': jnp.zeros((E, D), dtype=jnp.float32)}
    _L0_ffn_in = _L0_ffn_setup()
    _d = {'L0_attn_a_x': _L0_attn_a_in['x'], 'L0_attn_a_W_qkv': _L0_attn_a_in['W_qkv'], 'L0_attn_a_b_qkv': _L0_attn_a_in['b_qkv'], 'L0_attn_a_ln_w': _L0_attn_a_in['ln_w'], 'L0_attn_a_ln_b': _L0_attn_a_in['ln_b'], 'L0_attn_b_W_q': _L0_attn_b_in['W_q'], 'L0_attn_b_b_q': _L0_attn_b_in['b_q'], 'L0_attn_b_W_k': _L0_attn_b_in['W_k'], 'L0_attn_b_b_k': _L0_attn_b_in['b_k'], 'L0_attn_b_W_v': _L0_attn_b_in['W_v'], 'L0_attn_b_b_v': _L0_attn_b_in['b_v'], 'L0_attn_b_W_o': _L0_attn_b_in['W_o'], 'L0_attn_b_b_o': _L0_attn_b_in['b_o'], 'L0_ffn_Wg': _L0_ffn_in['Wg'], 'L0_ffn_bg': _L0_ffn_in['bg'], 'L0_ffn_W1': _L0_ffn_in['W1'], 'L0_ffn_b1': _L0_ffn_in['b1'], 'L0_ffn_W2': _L0_ffn_in['W2'], 'L0_ffn_b2': _L0_ffn_in['b2']}
    _x0 = _d['L0_attn_a_x']
    _d['L0_attn_a_x'] = jax.random.normal(jax.random.fold_in(jax.random.key(seed), 1), (2, 2048, 256), dtype=_x0.dtype)
    del _x0
    return _d

def reference(L0_attn_a_x, L0_attn_a_W_qkv, L0_attn_a_b_qkv, L0_attn_a_ln_w, L0_attn_a_ln_b, L0_attn_b_W_q, L0_attn_b_b_q, L0_attn_b_W_k, L0_attn_b_b_k, L0_attn_b_W_v, L0_attn_b_b_v, L0_attn_b_W_o, L0_attn_b_b_o, L0_ffn_Wg, L0_ffn_bg, L0_ffn_W1, L0_ffn_b1, L0_ffn_W2, L0_ffn_b2):

    def _L0_attn_a_ref(x, W_qkv, b_qkv, ln_w, ln_b):
        import jax, jax.numpy as jnp
        import numpy as np
        N_EMBD = 256
        BLOCK_SIZE = 512
        ATTN_SPAN = 64
        LN_EPS = 1e-05

        def _band_mask(T, span, dtype):
            ones = jnp.ones((T, T), dtype=dtype)
            return jnp.tril(ones, 0) * (1.0 - jnp.tril(ones, -span))

        def _layer_norm(h, w, b):
            mu = jnp.mean(h, axis=-1, keepdims=True)
            var = jnp.var(h, axis=-1, keepdims=True)
            return (h - mu) * jax.lax.rsqrt(var + LN_EPS) * w + b
        B, T, C = x.shape
        qkv = x @ W_qkv + b_qkv
        q, k, v = jnp.split(qkv, 3, axis=-1)
        scale = np.sqrt(C * ATTN_SPAN).astype(np.float32)
        scores = jnp.einsum('bid,bjd->bij', q, k) / scale
        scores = scores * _band_mask(T, ATTN_SPAN, x.dtype)[None, :, :]
        out = jnp.einsum('bij,bjd->bid', scores, v)
        return _layer_norm(out, ln_w, ln_b)

    def _L0_attn_b_ref(x, W_q, b_q, W_k, b_k, W_v, b_v, W_o, b_o):
        import jax, jax.numpy as jnp
        import numpy as np
        EPS = 1e-06
        N_HEADS = 16

        def _heads(t, B, N, H, Dk):
            return t.reshape(B, N, H, Dk).transpose(0, 2, 1, 3)
        B, N, Dm = x.shape
        H = N_HEADS
        Dk = Dm // H
        q = _heads(x @ W_q.T + b_q, B, N, H, Dk)
        k = _heads(x @ W_k.T + b_k, B, N, H, Dk)
        v = _heads(x @ W_v.T + b_v, B, N, H, Dk)
        dec = jnp.exp(-jnp.arange(N, dtype=jnp.float32) / N)[None, None, :, None]
        qf = jax.nn.relu(q) * dec
        kf = jax.nn.relu(k) * dec
        KV = jnp.einsum('bhnd,bhne->bhde', kf, v)
        Ksum = kf.sum(axis=2)
        denom = jnp.einsum('bhnd,bhd->bhn', qf, Ksum) + EPS
        out = jnp.einsum('bhnd,bhde->bhne', qf, KV) / denom[..., None]
        out = out.transpose(0, 2, 1, 3).reshape(B, N, Dm)
        return out @ W_o.T + b_o

    def _L0_ffn_ref(x, Wg, bg, W1, b1, W2, b2):
        import jax, jax.numpy as jnp
        import numpy as np
        B, S, D, H, E, K = (4, 512, 256, 512, 8, 2)
        TEMP = 5.0
        EPS = 1e-09
        logits = jnp.einsum('bsd,de->bse', x, Wg) + bg
        probs = jax.nn.softmax(logits / TEMP, axis=-1)
        vals, idx = jax.lax.top_k(probs, K)
        onehot = jax.nn.one_hot(idx, E, dtype=x.dtype)
        mask = jnp.einsum('bske,bsk->bse', onehot, vals)
        gates = mask / (jnp.sum(mask, axis=-1, keepdims=True) + EPS)
        h = jax.nn.gelu(jnp.einsum('bsd,edh->besh', x, W1) + b1[None, :, None, :], approximate=False)
        out = jnp.einsum('besh,ehd->besd', h, W2) + b2[None, :, None, :]
        y = jnp.einsum('bse,besd->bsd', gates, out)
        return y
    x = L0_attn_a_x
    x = x + _L0_attn_a_ref(_layernorm(x, axis=-1), L0_attn_a_W_qkv, L0_attn_a_b_qkv, L0_attn_a_ln_w, L0_attn_a_ln_b)
    x = x + _L0_ffn_ref(_layernorm(x, axis=-1), L0_ffn_Wg, L0_ffn_bg, L0_ffn_W1, L0_ffn_b1, L0_ffn_W2, L0_ffn_b2)
    x = x + _L0_attn_b_ref(_layernorm(x, axis=-1), L0_attn_b_W_q, L0_attn_b_b_q, L0_attn_b_W_k, L0_attn_b_b_k, L0_attn_b_W_v, L0_attn_b_b_v, L0_attn_b_W_o, L0_attn_b_b_o)
    x = x + _L0_ffn_ref(_layernorm(x, axis=-1), L0_ffn_Wg, L0_ffn_bg, L0_ffn_W1, L0_ffn_b1, L0_ffn_W2, L0_ffn_b2)
    return x

_drawn_inputs = setup_inputs


def setup_inputs(seed=0):
    import zlib

    import numpy as np

    out = dict(_drawn_inputs(seed))
    spreads = {'L0_attn_a_ln_w': (1.0, 0.2),
     'L0_attn_a_ln_b': (0.0, 0.1),
     'L0_attn_b_b_q': (0.0, 0.8),
     'L0_attn_b_b_k': (0.0, 0.8),
     'L0_attn_b_b_v': (0.0, 0.34),
     'L0_attn_b_b_o': (0.0, 0.1),
     'L0_ffn_bg': (0.0, 0.1),
     'L0_ffn_b1': (0.0, 0.317),
     'L0_ffn_b2': (0.0, 0.1)}
    factors = {'L0_attn_b_W_q': 8.0, 'L0_attn_b_W_k': 8.0, 'L0_attn_b_W_v': 6.839}
    for name, (base, spread) in spreads.items():
        noise = np.random.default_rng([zlib.crc32(name.encode()), seed]).standard_normal(out[name].shape)
        drawn = base * np.exp(spread * noise) if base else spread * noise
        out[name] = jnp.asarray(drawn.astype(out[name].dtype))
    for name, factor in factors.items():
        out[name] = (out[name] * factor).astype(out[name].dtype)
    return out
```

```python
from contextlib import ExitStack

import concourse.bass as bass
from concourse import mybir

F32 = mybir.dt.float32
BF16 = mybir.dt.bfloat16
I32 = mybir.dt.int32
U32 = mybir.dt.uint32
ALU = mybir.AluOpType
ACT = mybir.ActivationFunctionType
AX = mybir.AxisListType

P = 128
BATCH, SEQ, D = 2, 2048, 256
TOKENS = BATCH * SEQ
KC = D // P
TILES = TOKENS // P
GT = 4
GROUPS = TILES // GT
GN = GT * P
SPAN = 64
LN_EPS = 1e-5
EXPERTS, HID, TOPK = 8, 512, 2
HC = HID // P
TEMP = 5.0
GATE_EPS = 1e-9
ROW = D + EXPERTS
PAIRS = TILES * TOPK
SLOT_TILES = TOKENS * TOPK // P + EXPERTS - 1
SPARE = P
SLOT_PEEL = 4
assert (SLOT_TILES - 1 - SLOT_PEEL) % 3 == 0
HEADS = 16
DK = D // HEADS
DEN_EPS = 1e-6
VW = P + 2
RSQRT_MAGIC = 0x5F3759DF

CONST_COLS = {}


def _const_layout():
    at = 0
    for name, n in (("ident", P), ("mask_own", P), ("mask_prev", GROUPS * SPAN), ("before", P), ("ones", P),
                    ("dec", SEQ // P), ("rank_e", EXPERTS), ("seg", EXPERTS * TILES), ("iota", P),
                    ("token1", PAIRS), ("spare1", 1), ("head_block", P)):
        CONST_COLS[name] = (at, n)
        at += n
    return at


CONST_W = _const_layout()


class Steps:

    def __init__(self, eng, sem):
        self.eng, self.sem, self.base, self.n = eng, sem, 0, 0

    def did(self, ins):
        ins.then_inc(self.sem, 1)
        self.n += 1

    def wait(self):
        self.eng.wait_ge(self.sem, self.base + self.n)

    def chain(self, ins):
        self.did(ins)
        self.wait()


def over_groups(eng, step, unroll, steps=None, per_step=0):
    assert (GROUPS - 2) % unroll == 0
    step(0, 0)
    start, per = (steps.n if steps else 0), per_step * unroll
    with eng.Fori(0, (GROUPS - 2) // unroll) as i:
        if steps:
            steps.base, steps.n = start + i * per, 0
        for u in range(unroll):
            step(unroll * i + (1 + u), (1 + u) % unroll)
        assert not steps or steps.n == per, (steps.n, per)
    if steps:
        steps.base, steps.n = 0, start + per_step * (GROUPS - 2)
    step(GROUPS - 1, (GROUPS - 1) % unroll)
    step(GROUPS, GROUPS % unroll)


def program(nc, x, w_qkv, bqkv_cols, b_qkv, ln_w, ln_b, wq_t, bq_cols, wk_t, b_k, wv_t, b_v, wo_t, b_o,
            wg, bg, w1, b1, w2, b2, consts, dec_row, out):
    with ExitStack() as ctx:
        _program(nc, ctx, x, w_qkv, bqkv_cols, b_qkv, ln_w, ln_b, wq_t, bq_cols, wk_t, b_k, wv_t, b_v, wo_t, b_o,
                 wg, bg, w1, b1, w2, b2, consts, dec_row, out)


def _program(nc, ctx, x, w_qkv, bqkv_cols, b_qkv, ln_w, ln_b, wq_t, bq_cols, wk_t, b_k, wv_t, b_v, wo_t, b_o,
             wg, bg, w1, b1, w2, b2, consts, dec_row, out):
    ds = bass.ds

    def sb(name, shape, dt=F32, c=ctx):
        return c.enter_context(nc.sbuf_tensor(name, shape, dt))

    def sem(name, c=ctx):
        return c.enter_context(nc.semaphore(name))

    bank = [ctx.enter_context(nc.psum_tensor(f"bank{i}", [P, 512], F32)) for i in range(8)]

    x_sb = sb("x_sb", [P, TILES, D])
    w1_sb = sb("w1_sb", [P, EXPERTS, KC, HID])
    w2_sb = sb("w2_sb", [P, EXPERTS, HC, D])
    wg_sb = sb("wg_sb", [P, KC, EXPERTS])
    bg_sb = sb("bg_sb", [P, EXPERTS])
    cst = sb("cst", [P, CONST_W])
    rows = sb("rows", [P, 3, GT, ROW])
    xn_t = sb("xn_t", [P, KC, GN])
    st = sb("st", [P, GT, 6])
    mean = sb("mean", [P, GT])
    var = sb("var", [P, GT])
    half = sb("half", [P, GT], I32)
    rs = sb("rs", [P, GT])
    ra = sb("ra", [P, GT])
    rb = sb("rb", [P, GT])

    def const(name):
        at, n = CONST_COLS[name]
        return cst[:, at:at + n]

    ident = const("ident")

    table = nc.dram_tensor("row_table", [TOKENS + SPARE, ROW], F32).ap()
    acc1 = nc.dram_tensor("sum_1", [TOKENS + SPARE, D], F32).ap()

    def tiled(dram, g, width):
        return dram[ds(g * GN, GN), :].rearrange("(t p) n -> p t n", p=P) if not isinstance(g, int) else \
            dram[g * GN:(g + 1) * GN, :].rearrange("(t p) n -> p t n", p=P)

    def rsqrt(eng, steps):
        steps.chain(eng.tensor_scalar(var[:, :], var[:, :], LN_EPS, None, ALU.add))
        steps.chain(eng.tensor_scalar(half[:, :], var[:, :].bitcast(I32), 1, None, ALU.logical_shift_right))
        steps.chain(eng.tensor_scalar(rs[:, :].bitcast(I32), half[:, :], -1.0, float(RSQRT_MAGIC), ALU.mult, ALU.add))
        for _ in range(3):
            steps.chain(eng.scalar_tensor_tensor(ra[:, :], rs[:, :], -0.5, rs[:, :], ALU.mult, ALU.mult))
            steps.chain(eng.tensor_tensor(rb[:, :], ra[:, :], var[:, :], ALU.mult))
            steps.chain(eng.scalar_tensor_tensor(rs[:, :], rb[:, :], 1.5, rs[:, :], ALU.add, ALU.mult))

    RSQRT_STEPS = 12

    def stats(eng, steps, source):
        for t in range(GT):
            steps.did(eng.bn_stats(st[:, t, :], source(t)))
        steps.wait()
        mean_even, m2_even, mean_odd, m2_odd = (st[:, :, i] for i in (1, 2, 4, 5))
        steps.did(eng.tensor_tensor(ra[:, :], mean_even, mean_odd, ALU.add))
        steps.did(eng.tensor_tensor(rb[:, :], mean_even, mean_odd, ALU.subtract))
        steps.did(eng.tensor_tensor(var[:, :], m2_even, m2_odd, ALU.add))
        steps.wait()
        steps.did(eng.tensor_scalar(mean[:, :], ra[:, :], 0.5, None, ALU.mult))
        steps.chain(eng.scalar_tensor_tensor(rs[:, :], rb[:, :], 0.25, rb[:, :], ALU.mult, ALU.mult))
        steps.chain(eng.scalar_tensor_tensor(var[:, :], var[:, :], 1.0 / D, rs[:, :], ALU.mult, ALU.add))
        rsqrt(eng, steps)

    STATS_STEPS = GT + 6 + RSQRT_STEPS

    def normalise(eng, p, source, done):
        for t in range(GT):
            eng.tensor_scalar(rows[:, p, t, 0:D], source(t), mean[:, t:t + 1], rs[:, t:t + 1],
                              ALU.subtract, ALU.mult).then_inc(done, 1)

    def transpose_rows(eng, p, banks, done):
        for c in range(KC):
            for t in range(GT):
                mm = eng.transpose(banks[c][:, t * P:(t + 1) * P], rows[:, p, t, c * P:(c + 1) * P], ident)
        mm.then_inc(done, 1)

    def attention():
        with ExitStack() as c:
            w_sb = sb("wqkv_sb", [P, KC, 3 * D], c=c)
            bqk = sb("bqk", [P, 2 * KC], c=c)
            bv_sb = sb("bv_sb", [P, D], c=c)
            lw = sb("lw", [P, D], c=c)
            lb = sb("lb", [P, D], c=c)
            q_t = sb("q_t", [P, 3, KC, GN], c=c)
            k_t = sb("k_t", [P, 3, KC, GN], c=c)
            v_sb = sb("v_sb", [P, 3, GT, D], c=c)
            sc = sb("sc", [P, 2, 2 * P], c=c)
            o_sb = sb("o_sb", [P, GT, D], c=c)
            n_sb = sb("n_sb", [P, GT, D], c=c)
            zeros = sb("zeros", [P, ROW], c=c)

            s_x0, s_x1, s_x2 = (sem(f"a_x{i}", c) for i in range(3))
            s_w = sem("a_weights", c)
            s_big = sem("a_ffn_weights", c)
            s_zero = sem("a_zeroed", c)
            s_z = sem("a_zeros_out", c)
            s_dve = sem("a_dve_steps", c)
            s_pool = sem("a_pool_steps", c)
            s_rows = sem("a_rows", c)
            s_xt, s_xts = sem("a_xt_psum", c), sem("a_xt", c)
            s_qk, s_qks = sem("a_qk_psum", c), sem("a_qk", c)
            s_v, s_vs = sem("a_v_psum", c), sem("a_v", c)
            s_s, s_ss = sem("a_scores_psum", c), sem("a_scores", c)
            s_o, s_os = sem("a_out_psum", c), sem("a_out", c)
            s_n = sem("a_out_normalised", c)
            s_res = sem("a_residual", c)

            block = c.enter_context(nc.Block())

            @block.sync
            def _(sp):
                sp.dma_start(x_sb[:, 0:GT, :], tiled(x, 0, D)).then_inc(s_x0, 16)
                sp.dma_start(cst[:, :], consts).then_inc(s_w, 16)
                sp.dma_start(w_sb[:, :, :], w_qkv.rearrange("(c p) n -> p c n", p=P)).then_inc(s_w, 16)
                sp.dma_start(x_sb[:, GT:2 * GT, :], tiled(x, 1, D)).then_inc(s_x1, 16)
                for g in range(2, GROUPS):
                    sp.dma_start(x_sb[:, g * GT:(g + 1) * GT, :], tiled(x, g, D)).then_inc(s_x2, 16)
                for e in range(EXPERTS):
                    sp.dma_start(w1_sb[:, e, :, :], w1[e].rearrange("(c p) n -> p c n", p=P)).then_inc(s_big, 16)
                    sp.dma_start(w2_sb[:, e, :, :], w2[e].rearrange("(c p) n -> p c n", p=P)).then_inc(s_big, 16)
                sp.wait_ge(s_zero, 4)
                sp.dma_start(table[TOKENS:TOKENS + SPARE, :], zeros[:, :]).then_inc(s_z, 16)
                sp.dma_start(acc1[TOKENS:TOKENS + SPARE, :], zeros[:, 0:D]).then_inc(s_z, 16)
                sp.dma_start(out[TOKENS:TOKENS + SPARE, :], zeros[:, 0:D]).then_inc(s_z, 16)
                sp.wait_ge(s_z, 48)
                sp.wait_ge(s_big, 16 * (2 * EXPERTS))

            def evacuate_q_k(act, g, p):
                if not isinstance(g, int) or g >= 2:
                    act.wait_ge(s_s, GT * (g - 1))
                for m in range(2 * KC):
                    act.wait_ge(s_qk, 2 * KC * g + m + 1)
                    to = (q_t if m < KC else k_t)[:, p, m % KC, :]
                    act.activation(to, bank[2 + m % 2][:, :], ACT.Identity, bias=bqk[:, m:m + 1]).then_inc(s_qks, 1)

            @block.scalar
            def _(act):
                act.dma_start(bqk[:, :], bqkv_cols[:, 0:2 * KC]).then_inc(s_w, 16)
                act.dma_start(bv_sb[:, :], b_qkv[2 * D:3 * D].partition_broadcast(P)).then_inc(s_w, 16)
                act.dma_start(lw[:, :], ln_w.partition_broadcast(P)).then_inc(s_w, 16)
                act.dma_start(lb[:, :], ln_b.partition_broadcast(P)).then_inc(s_w, 16)
                act.dma_start(wg_sb[:, :, :], wg.rearrange("(c p) n -> p c n", p=P)).then_inc(s_w, 16)
                act.dma_start(bg_sb[:, :], bg.partition_broadcast(P)).then_inc(s_w, 16)
                act.wait_ge(s_w, 16 * 8)

                def step(g, p):
                    if g != GROUPS if isinstance(g, int) else True:
                        if not isinstance(g, int) or g >= 1:
                            act.wait_ge(s_v, 2 * g)
                        act.wait_ge(s_xt, g + 1)
                        for k in range(KC):
                            act.activation(xn_t[:, k, :], bank[k][:, :], ACT.Copy).then_inc(s_xts, 1)
                        evacuate_q_k(act, g, p)
                    if not isinstance(g, int) or g >= 1:
                        if not isinstance(g, int) or g >= 2:
                            act.wait_ge(s_n, GT * (g - 1))
                        for t in range(GT):
                            act.wait_ge(s_o, GT * (g - 1) + t + 1)
                            act.activation(o_sb[:, t, :], bank[6 + t % 2][:, 0:D], ACT.Copy).then_inc(s_os, 1)

                over_groups(act, step, 3)

            @block.vector
            def _(dve):
                steps = Steps(dve, s_dve)
                dve.memset(sc[:, :, P + SPAN:2 * P], 0.0).then_inc(s_zero, 1)
                dve.memset(k_t[:, 2, :, GN - P:GN], 0.0).then_inc(s_zero, 1)
                dve.memset(v_sb[:, 2, GT - 1, :], 0.0).then_inc(s_zero, 1)
                dve.memset(zeros[:, :], 0.0).then_inc(s_zero, 1)

                def front(g, p):
                    if not isinstance(g, int) or g >= 3:
                        dve.wait_ge(s_xt, g - 2)
                    stats(dve, steps, lambda t: x_sb[:, ds(g * GT + t, 1), :])
                    normalise(dve, p, lambda t: x_sb[:, ds(g * GT + t, 1), :], s_rows)

                def masked(g, t):
                    dve.wait_ge(s_s, GT * g + t + 1)
                    dve.tensor_tensor(sc[:, t % 2, 0:P], bank[t % 2][:, 0:P], const("mask_own"),
                                      ALU.mult).then_inc(s_ss, 1)
                    at = CONST_COLS["mask_prev"][0]
                    m = cst[:, ds(at + g * SPAN, SPAN)] if t == 0 else cst[:, at + SPAN:at + 2 * SPAN]
                    dve.tensor_tensor(sc[:, t % 2, P:P + SPAN], bank[t % 2][:, P:P + SPAN], m,
                                      ALU.mult).then_inc(s_ss, 1)

                def step(g, p):
                    static = isinstance(g, int)
                    if not static or g == 1:
                        dve.wait_ge(s_x2, 16 * (GROUPS - 2))
                    if static and g == 0:
                        dve.wait_ge(s_x0, 16)
                        front(0, 0)
                        dve.wait_ge(s_x1, 16)
                        dve.wait_ge(s_w, 16 * 8)
                    if not static or g < GROUPS:
                        if not static or g >= 2:
                            dve.wait_ge(s_o, GT * (g - 1))
                        for h in range(2):
                            dve.wait_ge(s_v, 2 * g + h + 1)
                            dve.tensor_tensor(v_sb[:, p, 2 * h:2 * h + 2, :],
                                              bank[4 + h][:, :].rearrange("p (t n) -> p t n", t=2),
                                              bv_sb[:, :].unsqueeze(1).to_broadcast([P, 2, D]),
                                              ALU.add).then_inc(s_vs, 1)
                    if not static or g < GROUPS - 1:
                        front(g + 1, (p + 1) % 3)
                    if not static or g >= 1:
                        for t in range(GT):
                            masked(g - 1, t)
                        dve.wait_ge(s_os, GT * g)
                        if not static or g >= 2:
                            dve.wait_ge(s_res, 3 * (g - 1))
                        stats(dve, steps, lambda t: o_sb[:, t, :])
                        for t in range(GT):
                            dve.tensor_scalar(n_sb[:, t, :], o_sb[:, t, :], mean[:, t:t + 1], rs[:, t:t + 1],
                                              ALU.subtract, ALU.mult).then_inc(s_n, 1)

                over_groups(dve, step, 3, steps, 2 * STATS_STEPS)

            @block.gpsimd
            def _(pool):
                pool.wait_ge(s_w, 16 * 8)
                with pool.Fori(0, GROUPS) as g:
                    pool.wait_ge(s_n, GT * g + GT)
                    pool.tensor_tensor(n_sb[:, :, :], n_sb[:, :, :], lw[:, :].unsqueeze(1).to_broadcast([P, GT, D]),
                                       ALU.mult).then_inc(s_res, 1)
                    pool.wait_ge(s_res, 3 * g + 1)
                    pool.tensor_tensor(n_sb[:, :, :], n_sb[:, :, :], lb[:, :].unsqueeze(1).to_broadcast([P, GT, D]),
                                       ALU.add).then_inc(s_res, 1)
                    pool.wait_ge(s_res, 3 * g + 2)
                    pool.tensor_tensor(x_sb[:, ds(g * GT, GT), :], x_sb[:, ds(g * GT, GT), :], n_sb[:, :, :],
                                       ALU.add).then_inc(s_res, 1)

            @block.tensor
            def _(pe):
                pe.wait_ge(s_w, 16 * 8)
                pe.wait_ge(s_zero, 3)

                def project(g, p):
                    pe.wait_ge(s_rows, GT * (g + 1))
                    transpose_rows(pe, p, bank[0:2], s_xt)
                    pe.wait_ge(s_xts, KC * (g + 1))
                    for m in range(2 * KC):
                        if not isinstance(g, int) or 2 * KC * g + m >= 2:
                            pe.wait_ge(s_qks, 2 * KC * g + m - 1)
                        for k in range(KC):
                            mm = pe.matmul(bank[2 + m % 2][:, :], w_sb[:, k, m * P:(m + 1) * P], xn_t[:, k, :],
                                           start=(k == 0), stop=(k == KC - 1))
                        mm.then_inc(s_qk, 1)
                    for h in range(2):
                        if not isinstance(g, int) or g >= 1:
                            pe.wait_ge(s_vs, 2 * g + h - 1)
                        for t in (2 * h, 2 * h + 1):
                            for k in range(KC):
                                mm = pe.matmul(bank[4 + h][:, (t % 2) * D:(t % 2 + 1) * D],
                                               xn_t[:, k, t * P:(t + 1) * P], w_sb[:, k, 2 * D:3 * D],
                                               start=(k == 0), stop=(k == KC - 1))
                        mm.then_inc(s_v, 1)

                def before(p, t):
                    return (p, t - 1) if t else ((p - 1) % 3, GT - 1)

                def scores(p, t):
                    for k in range(KC):
                        pe.matmul(bank[t % 2][:, 0:P], k_t[:, p, k, t * P:(t + 1) * P],
                                  q_t[:, p, k, t * P:(t + 1) * P], start=(k == 0), stop=(k == KC - 1))
                    pb, tb = before(p, t)
                    for k in range(KC):
                        mm = pe.matmul(bank[t % 2][:, P:P + SPAN], k_t[:, pb, k, tb * P:(tb + 1) * P],
                                       q_t[:, p, k, t * P:t * P + SPAN], start=(k == 0), stop=(k == KC - 1))
                    mm.then_inc(s_s, 1)

                def values(g, p, t):
                    pe.wait_ge(s_ss, 2 * (GT * g + t + 1))
                    if not isinstance(g, int) or GT * g + t >= 2:
                        pe.wait_ge(s_os, GT * g + t - 1 if t >= 2 else GT * g)
                    pb, tb = before(p, t)
                    pe.matmul(bank[6 + t % 2][:, 0:D], sc[:, t % 2, 0:P], v_sb[:, p, t, :], start=True, stop=False)
                    pe.matmul(bank[6 + t % 2][:, 0:D], sc[:, t % 2, P:2 * P], v_sb[:, pb, tb, :],
                              start=False, stop=True).then_inc(s_o, 1)

                def attend(g, p):
                    pe.wait_ge(s_qks, 2 * KC * (g + 1))
                    pe.wait_ge(s_vs, 2 * (g + 1))
                    scores(p, 0)
                    for t in range(1, GT):
                        scores(p, t)
                        values(g, p, t - 1)
                    values(g, p, GT - 1)

                def step(g, p):
                    if not isinstance(g, int) or g < GROUPS:
                        project(g, p)
                    if not isinstance(g, int) or g >= 1:
                        attend(g - 1, (p - 1) % 3)

                over_groups(pe, step, 3)

    def mixture(n, total):
        with ExitStack() as c:
            b1_sb = sb(f"m{n}_b1", [P, EXPERTS, HID], c=c)
            b2_sb = sb(f"m{n}_b2", [P, EXPERTS, D], c=c)
            logit = sb(f"m{n}_logit", [P, GT, EXPERTS], c=c)
            prob = sb(f"m{n}_prob", [P, GT, EXPERTS], c=c)
            tmp = sb(f"m{n}_tmp", [P, GT, EXPERTS], c=c)
            col = sb(f"m{n}_col", [P, 8, GT], c=c)
            first = sb(f"m{n}_first", [P, TILES, EXPERTS], c=c)
            second = sb(f"m{n}_second", [P, TILES, EXPERTS], c=c)
            either = sb(f"m{n}_either", [P, TILES, EXPERTS], BF16, c=c)
            cb = sb(f"m{n}_cb", [P, 2 * P], BF16, c=c)
            tot = sb(f"m{n}_tot", [P, EXPERTS, TILES], c=c)
            inc = sb(f"m{n}_inc", [P, EXPERTS, TILES], c=c)
            pos = sb(f"m{n}_pos", [P, TILES, EXPERTS], c=c)
            e8 = sb(f"m{n}_e8", [P, 4, EXPERTS], c=c)
            e8i = sb(f"m{n}_e8i", [P, 2, EXPERTS], I32, c=c)
            slot = sb(f"m{n}_slot", [P, 3, PAIRS], c=c)
            sloti = sb(f"m{n}_sloti", [P, 3, PAIRS], I32, c=c)
            in_tile = x_sb[:, :, :].rearrange("p t n -> p (t n)").rearrange("p (a b) -> p a b", b=P)
            of_tile = sb(f"m{n}_of_tile", [P, PAIRS, SLOT_TILES + 1], c=c)
            tile_e = sb(f"m{n}_tile_e", [P, SLOT_TILES + 1, EXPERTS], c=c)
            idxf = sb(f"m{n}_idxf", [P, 2, SLOT_TILES + 1], c=c)
            idx = sb(f"m{n}_idx", [P, SLOT_TILES + 1], U32, c=c)
            expert = sb(f"m{n}_expert", [P, SLOT_TILES + 1], I32, c=c)
            idxb = [sb(f"m{n}_idxb{r}", [P, 1], U32, c=c) for r in range(3)]
            xg = [sb(f"m{n}_xg{r}", [P, ROW], c=c) for r in range(3)]
            y_sc = [sb(f"m{n}_y_sc{r}", [P, D], c=c) for r in range(3)]
            xg_t = sb(f"m{n}_xg_t", [P, KC, P], c=c)
            h_sb = sb(f"m{n}_h", [P, HID], c=c)
            h_t = sb(f"m{n}_h_t", [P, HC, P], c=c)
            y_sb = sb(f"m{n}_y", [P, D], c=c)

            carry = sb(f"m{n}_carry", [P, 7], c=c)
            s_carry = sem(f"m{n}_carry_zeroed", c)
            s_bias = sem(f"m{n}_biases", c)
            s_dve = sem(f"m{n}_dve_steps", c)
            s_rows = sem(f"m{n}_rows", c)
            s_gates = sem(f"m{n}_gates", c)
            s_xt, s_xts = sem(f"m{n}_xt_psum", c), sem(f"m{n}_xt", c)
            s_lg, s_mx, s_ex = sem(f"m{n}_logits", c), sem(f"m{n}_shifted", c), sem(f"m{n}_exp", c)
            s_out = [sem(f"m{n}_rows_out{p}", c) for p in range(2)]
            s_xout = sem(f"m{n}_x_out", c)
            s_cnt, s_onehot, s_inv = sem(f"m{n}_counted", c), sem(f"m{n}_onehot", c), sem(f"m{n}_tokens", c)
            s_idx = sem(f"m{n}_indices", c)
            s_ib = sem(f"m{n}_index_copied", c)
            s_g = [sem(f"m{n}_gathered{r}", c) for r in range(3)]
            s_sum = sem(f"m{n}_summed", c)
            f_xt, f_xts = sem(f"m{n}_slot_xt_psum", c), sem(f"m{n}_slot_xt", c)
            f_h, f_hb = sem(f"m{n}_h_psum", c), sem(f"m{n}_h_biased", c)
            f_ht, f_gelu = sem(f"m{n}_h_t_psum", c), sem(f"m{n}_h_gelu", c)
            f_y, f_yb, f_ys = sem(f"m{n}_y_psum", c), sem(f"m{n}_y_biased", c), sem(f"m{n}_y_gated", c)

            block = c.enter_context(nc.Block())

            def over_slots(eng, step):
                for s in range(SLOT_PEEL):
                    step(s, s % 3)
                with eng.Fori(0, (SLOT_TILES - 1 - SLOT_PEEL) // 3) as i:
                    for u in range(3):
                        step(3 * i + (SLOT_PEEL + u), (SLOT_PEEL + u) % 3)
                step(SLOT_TILES - 1, (SLOT_TILES - 1) % 3)
                step(SLOT_TILES, SLOT_TILES % 3)


            @block.sync
            def _(sp):
                def store(g, p):
                    sp.wait_ge(s_gates, g + 1)
                    sp.dma_start(tiled(table, g, ROW), rows[:, p, :, :]).then_inc(s_out[p], 16)
                    sp.dma_start(tiled(total, g, D), x_sb[:, ds(g * GT, GT), :]).then_inc(s_xout, 16)
                sp.dma_start(b1_sb[:, :, :], b1.partition_broadcast(P)).then_inc(s_bias, 16)
                sp.dma_start(b2_sb[:, :, :], b2.partition_broadcast(P)).then_inc(s_bias, 16)
                with sp.Fori(0, GROUPS // 2) as i:
                    store(2 * i, 0)
                    store(2 * i + 1, 1)

            @block.gpsimd
            def _(pool):
                pool.wait_ge(s_idx, 2)
                for p in range(2):
                    pool.wait_ge(s_out[p], 16 * GROUPS // 2)
                pool.wait_ge(s_xout, 16 * GROUPS)

                pool.memset(carry[:, :], 0.0).then_inc(s_carry, 1)
                pool.wait_ge(s_carry, 1)

                def carry_wait(place):
                    pool.tensor_tensor(carry[:, place:place + 1], carry[:, 6:7], carry[:, 6:7], ALU.add)

                def gather(s, r):
                    pool.tensor_copy(idxb[r][:, :], idx[:, ds(s, 1)]).then_inc(s_ib, 1)
                    pool.wait_ge(s_ib, s + 1)
                    carry_wait(r)
                    pool.indirect_dma_start(xg[r][:, :], None, table,
                                            bass.IndirectOffsetOnAxis(idxb[r][:, 0:1], 0)).then_inc(s_g[r], 16)

                def step(s, r):
                    if isinstance(s, int) and s == SLOT_TILES:
                        return
                    if not isinstance(s, int) or s >= 1:
                        pool.wait_ge(s_sum, 16 * s)
                    if not isinstance(s, int) or s < SLOT_TILES - 2:
                        gather(s + 2, (r + 2) % 3)
                    pool.wait_ge(f_ys, s + 1)
                    carry_wait(3 + r)
                    pool.indirect_dma_start(total, bass.IndirectOffsetOnAxis(idxb[r][:, 0:1], 0), y_sc[r][:, :], None,
                                            compute_op=ALU.add).then_inc(s_sum, 16)

                gather(0, 0)
                gather(1, 1)
                step(0, 0)
                with pool.Fori(0, (SLOT_TILES - 5) // 3) as i:
                    for u in range(3):
                        step(3 * i + (1 + u), (1 + u) % 3)
                for s in range(SLOT_TILES - 4, SLOT_TILES):
                    step(s, s % 3)
                pool.wait_ge(s_sum, 16 * SLOT_TILES)

            @block.scalar
            def _(act):
                def copy_rows(g, p):
                    if not isinstance(g, int) or g >= 1:
                        act.wait_ge(s_lg, g)
                    act.wait_ge(s_xt, g + 1)
                    for k in range(KC):
                        act.activation(xn_t[:, k, :], bank[k][:, :], ACT.Copy).then_inc(s_xts, 1)
                    act.wait_ge(s_mx, g + 1)
                    act.activation(prob[:, :, :], logit[:, :, :], ACT.Exp, scale=1.0 / TEMP).then_inc(s_ex, 1)

                copy_rows(0, 0)
                with act.Fori(1, GROUPS) as g:
                    copy_rows(g, None)

                act.wait_ge(s_idx, 2)

                def copy_slots(s, r):
                    act.wait_ge(f_xt, s + 1)
                    if not isinstance(s, int) or s >= 1:
                        act.wait_ge(f_h, s)
                    act.activation(xg_t[:, :, :], bank[0][:, 0:D].rearrange("p (c n) -> p c n", c=KC),
                                   ACT.Copy).then_inc(f_xts, 1)

                def step(s, r):
                    if not isinstance(s, int) or s < SLOT_TILES - 1:
                        copy_slots(s + 1, (r + 1) % 3)
                    if not isinstance(s, int) or s >= 1:
                        if not isinstance(s, int) or s >= 4:
                            act.wait_ge(s_sum, 16 * (s - 3))
                        act.wait_ge(f_yb, s)
                        q = (r - 1) % 3
                        e = act.value_load(expert[0:1, ds(s - 1, 1)], min_val=0, max_val=EXPERTS - 1)
                        act.activation(y_sc[q][:, :], y_sb[:, :], ACT.Copy,
                                       scale=xg[q][:, ds(e + D, 1)]).then_inc(f_ys, 1)
                    if not isinstance(s, int) or s < SLOT_TILES:
                        act.wait_ge(f_ht, s + 1)
                        if not isinstance(s, int) or s >= 1:
                            act.wait_ge(f_y, s)
                        act.activation(h_t[:, :, :], bank[2][:, :].rearrange("p (c n) -> p c n", c=HC),
                                       ACT.Gelu).then_inc(f_gelu, 1)

                copy_slots(0, 0)
                over_slots(act, step)

            @block.vector
            def _(dve):
                steps = Steps(dve, s_dve)
                steps.chain(dve.tensor_copy(cb[:, 0:P], const("before")))
                steps.chain(dve.tensor_copy(cb[:, P:2 * P], const("ones")))

                def wide(c4):
                    return c4.unsqueeze(2).to_broadcast([P, GT, EXPERTS])

                def router(g, p):
                    tiles = ds(g * GT, GT)
                    rank = const("rank_e").unsqueeze(1).to_broadcast([P, GT, EXPERTS])
                    dve.wait_ge(s_lg, g + 1)
                    lg = bank[2][:, 0:GT * EXPERTS].rearrange("p (t e) -> p t e", t=GT)
                    steps.chain(dve.tensor_tensor(logit[:, :, :], lg, bg_sb[:, :].unsqueeze(1).to_broadcast([P, GT, EXPERTS]), ALU.add))
                    steps.chain(dve.tensor_reduce(col[:, 0, :], logit[:, :, :], AX.X, ALU.max))
                    dve.tensor_tensor(logit[:, :, :], logit[:, :, :], wide(col[:, 0, :]), ALU.subtract).then_inc(s_mx, 1)
                    dve.wait_ge(s_ex, g + 1)
                    steps.chain(dve.tensor_reduce(col[:, 1, :], prob[:, :, :], AX.X, ALU.add))
                    steps.chain(dve.reciprocal(col[:, 2, :], col[:, 1, :]))
                    steps.chain(dve.tensor_tensor(prob[:, :, :], prob[:, :, :], wide(col[:, 2, :]), ALU.mult))
                    for k, hot in ((0, first), (1, second)):
                        steps.chain(dve.tensor_reduce(col[:, 3 + k, :], prob[:, :, :], AX.X, ALU.max))
                        steps.chain(dve.tensor_tensor(tmp[:, :, :], prob[:, :, :], wide(col[:, 3 + k, :]), ALU.is_equal))
                        steps.chain(dve.tensor_tensor(tmp[:, :, :], tmp[:, :, :], rank, ALU.mult))
                        steps.chain(dve.tensor_reduce(col[:, 5, :], tmp[:, :, :], AX.X, ALU.max))
                        steps.chain(dve.tensor_tensor(hot[:, tiles, :], tmp[:, :, :], wide(col[:, 5, :]), ALU.is_equal))
                        if k == 0:
                            steps.chain(dve.scalar_tensor_tensor(prob[:, :, :], hot[:, tiles, :], -2.0, prob[:, :, :],
                                                                 ALU.mult, ALU.add))
                    steps.did(dve.tensor_tensor(either[:, tiles, :], first[:, tiles, :], second[:, tiles, :], ALU.add))
                    steps.chain(dve.scalar_tensor_tensor(col[:, 6, :], col[:, 3, :], GATE_EPS, col[:, 4, :], ALU.add, ALU.add))
                    steps.chain(dve.reciprocal(col[:, 7, :], col[:, 6, :]))
                    steps.chain(dve.tensor_tensor(col[:, 3:5, :], col[:, 3:5, :],
                                                  col[:, 7:8, :].to_broadcast([P, 2, GT]), ALU.mult))
                    steps.chain(dve.tensor_tensor(tmp[:, :, :], first[:, tiles, :], wide(col[:, 3, :]), ALU.mult))
                    steps.chain(dve.tensor_tensor(prob[:, :, :], second[:, tiles, :], wide(col[:, 4, :]), ALU.mult))
                    dve.tensor_tensor(rows[:, p, :, D:ROW], tmp[:, :, :], prob[:, :, :], ALU.add).then_inc(s_gates, 1)

                ROUTER_STEPS = 22

                def step(g, p):
                    static = isinstance(g, int)
                    if not static or g < GROUPS:
                        if static and g >= 2:
                            dve.wait_ge(s_out[p], 16 * ((g - p) // 2))
                        elif not static:
                            dve.wait_ge(s_out[p], step.stored)
                        stats(dve, steps, lambda t: x_sb[:, ds(g * GT + t, 1), :])
                        normalise(dve, p, lambda t: x_sb[:, ds(g * GT + t, 1), :], s_rows)
                    if not static or g >= 1:
                        router(g - 1, 1 - p)

                step(0, 0)
                step(1, 1)
                start, per = steps.n, 2 * (STATS_STEPS + ROUTER_STEPS)
                with dve.Fori(1, GROUPS // 2) as i:
                    steps.base, steps.n = start + (i - 1) * per, 0
                    step.stored = 16 * i
                    step(2 * i, 0)
                    step(2 * i + 1, 1)
                    assert steps.n == per, (steps.n, per)
                steps.base, steps.n = 0, start + (GROUPS // 2 - 1) * per
                step(GROUPS, 0)

                dve.wait_ge(s_cnt, 1)
                steps.chain(dve.tensor_copy(tot[:, :, :], bank[1][:, 0:TILES * EXPERTS].rearrange("p (t e) -> p e t", t=TILES)))
                flat = lambda a: a[:, :, :].rearrange("p a b -> p (a b)")
                steps.chain(dve.tensor_tensor_scan(flat(inc), const("seg"), flat(tot), 0.0, ALU.mult, ALU.add))
                steps.chain(dve.tensor_scalar(e8i[:, 0, :], inc[:, :, TILES - 1], float(P - 1), None, ALU.add))
                steps.chain(dve.tensor_scalar(e8i[:, 1, :], e8i[:, 0, :], 7, None, ALU.logical_shift_right))
                steps.chain(dve.tensor_copy(e8[:, 0, :], e8i[:, 1, :]))
                steps.chain(dve.tensor_tensor_scan(e8[:, 1, :], const("ones")[:, 0:EXPERTS], e8[:, 0, :], 0.0, ALU.mult, ALU.add))
                steps.chain(dve.tensor_tensor(e8[:, 2, :], e8[:, 1, :], e8[:, 0, :], ALU.subtract))
                steps.chain(dve.tensor_scalar(e8[:, 3, :], e8[:, 2, :], float(P), None, ALU.mult))
                steps.chain(dve.tensor_tensor(inc[:, :, :], inc[:, :, :], tot[:, :, :], ALU.subtract))
                steps.chain(dve.tensor_tensor(inc[:, :, :], inc[:, :, :], e8[:, 3, :].unsqueeze(2).to_broadcast([P, EXPERTS, TILES]), ALU.add))
                steps.chain(dve.tensor_tensor(pos[:, :, :], bank[0][:, 0:TILES * EXPERTS].rearrange("p (t e) -> p t e", t=TILES),
                                              inc[:, :, :].rearrange("p e t -> p t e"), ALU.add))
                for k, hot in ((0, first), (1, second)):
                    steps.chain(dve.tensor_tensor(hot[:, :, :], hot[:, :, :], pos[:, :, :], ALU.mult))
                    steps.chain(dve.tensor_reduce(slot[:, 0, k * TILES:(k + 1) * TILES], hot[:, :, :], AX.X, ALU.add))
                steps.chain(dve.tensor_copy(sloti[:, 0, :], slot[:, 0, :]))
                steps.chain(dve.tensor_scalar(sloti[:, 1, :], sloti[:, 0, :], 7, None, ALU.logical_shift_right))
                steps.chain(dve.tensor_scalar(sloti[:, 2, :], sloti[:, 0, :], P - 1, None, ALU.bitwise_and))
                steps.chain(dve.tensor_copy(slot[:, 1:3, :], sloti[:, 1:3, :]))
                iota = const("iota")
                NS1 = SLOT_TILES + 1
                steps.chain(dve.tensor_tensor(of_tile[:, :, :], iota[:, 0:NS1].unsqueeze(1).to_broadcast([P, PAIRS, NS1]),
                                              slot[:, 1, :].unsqueeze(2).to_broadcast([P, PAIRS, NS1]), ALU.is_equal))
                steps.chain(dve.tensor_tensor(of_tile[:, :, :], of_tile[:, :, :],
                                              const("token1").unsqueeze(2).to_broadcast([P, PAIRS, NS1]), ALU.mult))
                dve.wait_ge(s_xout, 16 * GROUPS)
                for q in range(4):
                    a = slice(q * PAIRS // 4, (q + 1) * PAIRS // 4)
                    dve.tensor_tensor(in_tile[:, a, :], iota.unsqueeze(1).to_broadcast([P, PAIRS // 4, P]),
                                      slot[:, 2, a].unsqueeze(2).to_broadcast([P, PAIRS // 4, P]),
                                      ALU.is_equal).then_inc(s_onehot, 1)
                steps.chain(dve.tensor_tensor(tile_e[:, :, :], e8[:, 1, :].unsqueeze(1).to_broadcast([P, NS1, EXPERTS]),
                                              iota[:, 0:NS1].unsqueeze(2).to_broadcast([P, NS1, EXPERTS]), ALU.is_le))
                steps.chain(dve.tensor_reduce(idxf[:, 0, :], tile_e[:, :, :], AX.X, ALU.add))
                steps.chain(dve.tensor_scalar(expert[:, :], idxf[:, 0, :], float(EXPERTS - 1), None, ALU.min))
                dve.wait_ge(s_inv, 1)
                steps.chain(dve.tensor_scalar(idxf[:, 0, :], bank[3][:, 0:NS1], 0.0, const("spare1"), ALU.is_equal, ALU.mult))
                steps.chain(dve.scalar_tensor_tensor(idxf[:, 1, :], bank[3][:, 0:NS1], -1.0, idxf[:, 0, :], ALU.add, ALU.add))
                dve.tensor_copy(idx[:, :], idxf[:, 1, :]).then_inc(s_idx, 2)

                dve.wait_ge(s_bias, 32)

                def bias_step(s, r):
                    if not isinstance(s, int) or s < SLOT_TILES:
                        e = dve.value_load(expert[0:1, ds(s, 1)], min_val=0, max_val=EXPERTS - 1)
                        dve.wait_ge(f_h, s + 1)
                        if not isinstance(s, int) or s >= 1:
                            dve.wait_ge(f_ht, s)
                        dve.tensor_tensor(h_sb[:, :], bank[1][:, :], b1_sb[:, ds(e, 1), :].rearrange("p a n -> p (a n)"), ALU.add).then_inc(f_hb, 1)
                    if not isinstance(s, int) or s >= 1:
                        e = dve.value_load(expert[0:1, ds(s - 1, 1)], min_val=0, max_val=EXPERTS - 1)
                        dve.wait_ge(f_y, s)
                        if not isinstance(s, int) or s >= 2:
                            dve.wait_ge(f_ys, s - 1)
                        dve.tensor_tensor(y_sb[:, :], bank[3][:, 0:D], b2_sb[:, ds(e, 1), :].rearrange("p a n -> p (a n)"), ALU.add).then_inc(f_yb, 1)

                over_slots(dve, bias_step)

            @block.tensor
            def _(pe):
                def logits(g, p):
                    pe.wait_ge(s_xts, KC * (g + 1))
                    if not isinstance(g, int) or g >= 1:
                        pe.wait_ge(s_mx, g)
                    for t in range(GT):
                        for k in range(KC):
                            mm = pe.matmul(bank[2][:, t * EXPERTS:(t + 1) * EXPERTS], xn_t[:, k, t * P:(t + 1) * P],
                                           wg_sb[:, k, :], start=(k == 0), stop=(k == KC - 1))
                    mm.then_inc(s_lg, 1)

                def front(g, p):
                    pe.wait_ge(s_rows, GT * (g + 1))
                    transpose_rows(pe, p, bank[0:2], s_xt)
                    logits(g, p)

                front(0, 0)
                front(1, 1)
                with pe.Fori(1, GROUPS // 2) as i:
                    front(2 * i, 0)
                    front(2 * i + 1, 1)
                pe.wait_ge(s_gates, GROUPS)
                flat = either[:, :, :].rearrange("p t e -> p (t e)")
                pe.matmul(bank[0][:, 0:TILES * EXPERTS], cb[:, 0:P], flat, start=True, stop=True)
                pe.matmul(bank[1][:, 0:TILES * EXPERTS], cb[:, P:2 * P], flat, start=True, stop=True).then_inc(s_cnt, 1)
                for q in range(4):
                    pe.wait_ge(s_onehot, q + 1)
                    for a in range(q * PAIRS // 4, (q + 1) * PAIRS // 4):
                        mm = pe.matmul(bank[3][:, 0:SLOT_TILES + 1], in_tile[:, a, :], of_tile[:, a, :],
                                       start=(a == 0), stop=(a == PAIRS - 1))
                mm.then_inc(s_inv, 1)
                pe.wait_ge(s_idx, 2)

                def turn(s, r, filled):
                    pe.wait_ge(s_g[r], 16 * filled)
                    if not isinstance(s, int) or s >= 1:
                        pe.wait_ge(f_xts, s)
                    for k in range(KC):
                        mm = pe.transpose(bank[0][:, k * P:(k + 1) * P], xg[r][:, k * P:(k + 1) * P], ident)
                    mm.then_inc(f_xt, 1)

                def step(s, r):
                    static = isinstance(s, int)
                    if not static or s < SLOT_TILES:
                        e = pe.value_load(expert[0:1, ds(s, 1)], min_val=0, max_val=EXPERTS - 1)
                        pe.wait_ge(f_xts, s + 1)
                        if not static or s >= 1:
                            pe.wait_ge(f_hb, s)
                        for k in range(KC):
                            mm = pe.matmul(bank[1][:, :], xg_t[:, k, :], w1_sb[:, ds(e, 1), k, :].rearrange("p a n -> p (a n)"),
                                           start=(k == 0), stop=(k == KC - 1))
                        mm.then_inc(f_h, 1)
                    if not static or s < SLOT_TILES - 1:
                        nxt = (s + 1) // 3 + 1 if static else step.filled(r)
                        turn(s + 1, (r + 1) % 3, nxt)
                    if not static or s >= 1:
                        e = pe.value_load(expert[0:1, ds(s - 1, 1)], min_val=0, max_val=EXPERTS - 1)
                        pe.wait_ge(f_gelu, s)
                        if not static or s >= 2:
                            pe.wait_ge(f_yb, s - 1)
                        for k in range(HC):
                            mm = pe.matmul(bank[3][:, 0:D], h_t[:, k, :], w2_sb[:, ds(e, 1), k, :].rearrange("p a n -> p (a n)"),
                                           start=(k == 0), stop=(k == HC - 1))
                        mm.then_inc(f_y, 1)
                    if not static or s < SLOT_TILES:
                        pe.wait_ge(f_hb, s + 1)
                        if not static or s >= 1:
                            pe.wait_ge(f_gelu, s)
                        for k in range(HC):
                            mm = pe.transpose(bank[2][:, k * P:(k + 1) * P], h_sb[:, k * P:(k + 1) * P], ident)
                        mm.then_inc(f_ht, 1)

                turn(0, 0, 1)
                for s in range(SLOT_PEEL):
                    step(s, s % 3)
                with pe.Fori(0, (SLOT_TILES - 1 - SLOT_PEEL) // 3) as i:
                    step.filled = lambda r: i + 2 if (r + 1) % 3 == 2 else i + 3
                    for u in range(3):
                        step(3 * i + (SLOT_PEEL + u), (SLOT_PEEL + u) % 3)
                step(SLOT_TILES - 1, (SLOT_TILES - 1) % 3)
                step(SLOT_TILES, SLOT_TILES % 3)

    def linear_attention():
        with ExitStack() as c:
            wq_sb = sb("wq_sb", [P, KC, D], c=c)
            wkv_sb = sb("wkv_sb", [P, KC, 2 * D], c=c)
            wo_sb = sb("wo_sb", [P, KC, D], c=c)
            bq_sb = sb("bq_sb", [P, KC], c=c)
            bk_sb = sb("bk_sb", [P, D], c=c)
            bv_sb = sb("bv2_sb", [P, D], c=c)
            bo_sb = sb("bo_sb", [P, D], c=c)
            decr = sb("decr", [P, SEQ], c=c)
            q_t = sb("q2_t", [P, KC, BATCH, SEQ], c=c)
            q_flat = q_t[:, :, :, :].rearrange("p c b n -> p c (b n)")
            k_sb = sb("k2_sb", [P, 2, D], c=c)
            kf = sb("kf", [P, 2, GT, D], c=c)
            v1 = sb("v1", [P, 2, GT, KC, VW], c=c)
            part = sb("part", [P, GROUPS, KC, VW], c=c)
            kv = sb("kv", [P, KC, VW], c=c)
            kvm = sb("kvm", [P, BATCH, KC, 2, P], c=c)
            den = xn_t
            o_t = sb("o2_t", [P, KC, GN], c=c)

            s_w = sem("b_weights", c)
            s_x = sem("b_x", c)
            s_ones = sem("b_ones", c)
            s_dve = sem("b_dve_steps", c)
            s_bo = sem("b_x_biased", c)
            s_rows = sem("b_rows", c)
            s_xt, s_xts = sem("b_xt_psum", c), sem("b_xt", c)
            s_kv, s_k, s_v = sem("b_kv_psum", c), sem("b_k", c), sem("b_v", c)
            s_kf = sem("b_kf", c)
            s_q, s_qs, s_qd = sem("b_q_psum", c), sem("b_q", c), sem("b_q_decayed", c)
            s_kvp, s_part = sem("b_part_psum", c), sem("b_part", c)
            s_kvm = sem("b_kv_masked", c)
            s_od, s_ot = sem("b_out_psum", c), sem("b_out", c)
            s_y, s_ys = sem("b_y_psum", c), sem("b_y", c)

            block = c.enter_context(nc.Block())

            @block.sync
            def _(sp):
                sp.dma_start(x_sb[:, 0:GT, :], tiled(acc1, 0, D)).then_inc(s_x, 16)
                with sp.Fori(1, GROUPS) as g:
                    sp.wait_ge(s_x, 16 * g)
                    sp.dma_start(x_sb[:, ds(g * GT, GT), :], tiled(acc1, g, D)).then_inc(s_x, 16)

            @block.scalar
            def _(act):
                for to, of in ((wkv_sb[:, :, 0:D], wk_t), (wkv_sb[:, :, D:2 * D], wv_t), (wq_sb[:, :, :], wq_t), (wo_sb[:, :, :], wo_t)):
                    act.dma_start(to, of.rearrange("(c p) n -> p c n", p=P)).then_inc(s_w, 16)
                act.dma_start(bq_sb[:, :], bq_cols).then_inc(s_w, 16)
                for to, of in ((bk_sb, b_k), (bv_sb, b_v), (bo_sb, b_o), (decr, dec_row)):
                    act.dma_start(to[:, :], of.partition_broadcast(P)).then_inc(s_w, 16)
                act.wait_ge(s_w, 16 * 9)

                def step(g, p):
                    static = isinstance(g, int)
                    if static and g == GROUPS:
                        return
                    if not static or g >= 1:
                        act.wait_ge(s_q, KC * g)
                    act.wait_ge(s_xt, g + 1)
                    for k in range(KC):
                        act.activation(xn_t[:, k, :], bank[k][:, :], ACT.Copy).then_inc(s_xts, 1)
                    if not static or g >= 2:
                        act.wait_ge(s_kvp, g - 1)
                    for t in range(GT):
                        act.wait_ge(s_k, GT * g + t + 1)
                        at = CONST_COLS["dec"][0]
                        tile = (g % (GROUPS // BATCH)) * GT + t if static else act_tile(g, t)
                        act.activation(kf[:, p, t, :], k_sb[:, t % 2, :], ACT.Relu,
                                       scale=cst[:, ds(at + tile, 1)]).then_inc(s_kf, 1)
                    for m in range(KC):
                        act.wait_ge(s_q, KC * g + m + 1)
                        act.activation(q_flat[:, m, ds(g * GN, GN)], bank[2 + m][:, :], ACT.Relu,
                                       bias=bq_sb[:, m:m + 1]).then_inc(s_qs, 1)

                def act_tile(g, t):
                    return (g % (GROUPS // BATCH)) * GT + t

                over_groups(act, step, 2)

            @block.gpsimd
            def _(pool):
                pool.memset(v1[:, :, :, :, P:VW], 1.0).then_inc(s_ones, 1)
                pool.wait_ge(s_w, 16 * 9)
                with pool.Fori(0, GROUPS) as g:
                    pool.wait_ge(s_rows, GT * g + GT)
                    pool.tensor_tensor(x_sb[:, ds(g * GT, GT), :], x_sb[:, ds(g * GT, GT), :],
                                       bo_sb[:, :].unsqueeze(1).to_broadcast([P, GT, D]), ALU.add).then_inc(s_bo, 1)

            @block.vector
            def _(dve):
                steps = Steps(dve, s_dve)
                dve.wait_ge(s_w, 16 * 9)
                dve.wait_ge(s_ones, 1)

                def front(g, p):
                    dve.wait_ge(s_x, 16 * g + 16)
                    if not isinstance(g, int) or g >= 2:
                        dve.wait_ge(s_xt, g - 1)
                    stats(dve, steps, lambda t: x_sb[:, ds(g * GT + t, 1), :])
                    normalise(dve, p, lambda t: x_sb[:, ds(g * GT + t, 1), :], s_rows)

                def step(g, p):
                    static = isinstance(g, int)
                    if static and g == 0:
                        front(0, 0)
                    if not static or g < GROUPS:
                        if not static or g >= 2:
                            dve.wait_ge(s_kvp, g - 1)
                        for t in range(GT):
                            dve.wait_ge(s_kv, GT * g + t + 1)
                            if not static or GT * g + t >= 2:
                                dve.wait_ge(s_kf, GT * g + t - 1)
                            b = bank[4 + t % 2]
                            dve.tensor_tensor(k_sb[:, t % 2, :], b[:, 0:D], bk_sb[:, :], ALU.add).then_inc(s_k, 1)
                            dve.tensor_tensor(v1[:, p, t, :, 0:P], b[:, D:2 * D].rearrange("p (c n) -> p c n", c=KC),
                                              bv_sb[:, :].rearrange("p (c n) -> p c n", c=KC), ALU.add).then_inc(s_v, 1)
                    if not static or g < GROUPS - 1:
                        front(g + 1, 1 - p)
                    if not static or g < GROUPS:
                        dve.wait_ge(s_qs, KC * g + KC)
                        at = (g % (GROUPS // BATCH)) * GN
                        q = q_flat[:, :, ds(g * GN, GN)]
                        dve.tensor_tensor(q, q, decr[:, ds(at, GN)].unsqueeze(1).to_broadcast([P, KC, GN]),
                                          ALU.mult).then_inc(s_qd, 1)
                    if not static or g >= 1:
                        for k in range(KC):
                            dve.wait_ge(s_kvp, g)
                            dve.tensor_copy(part[:, ds(g - 1, 1), k, :].rearrange("p a n -> p (a n)"), bank[6 + k][:, 0:VW]).then_inc(s_part, 1)

                over_groups(dve, step, 2, steps, STATS_STEPS)
                dve.wait_ge(s_part, KC * GROUPS)
                GB = GROUPS // BATCH
                block_mask = const("head_block").unsqueeze(1).to_broadcast([P, KC, P])
                for b in range(BATCH):
                    steps.chain(dve.tensor_tensor(kv[:, :, :], part[:, b * GB, :, :], part[:, b * GB + 1, :, :], ALU.add))
                    for a in range(2, GB):
                        steps.chain(dve.tensor_tensor(kv[:, :, :], kv[:, :, :], part[:, b * GB + a, :, :], ALU.add))
                    dve.tensor_tensor(kvm[:, b, :, 0, :], kv[:, :, 0:P], block_mask, ALU.mult).then_inc(s_kvm, 1)
                    steps.chain(dve.tensor_tensor(kvm[:, b, :, 1, :], kv[:, :, P:P + 1].to_broadcast([P, KC, P]), block_mask, ALU.mult))

                def divide(g):
                    for k in range(KC):
                        dve.wait_ge(s_od, KC * g + k + 1)
                        steps.chain(dve.tensor_scalar(den[:, k, :], bank[2 * k + 1][:, :], DEN_EPS, None, ALU.add))
                        steps.chain(dve.reciprocal(den[:, k, :], den[:, k, :]))
                        if k == 0 and (not isinstance(g, int) or g >= 1):
                            dve.wait_ge(s_y, 2 * g)
                        dve.tensor_tensor(o_t[:, k, :], bank[2 * k][:, :], den[:, k, :], ALU.mult).then_inc(s_ot, 1)

                def residual(g):
                    for h in range(2):
                        dve.wait_ge(s_y, 2 * g + h + 1)
                        xs = x_sb[:, ds(g * GT + 2 * h, 2), :]
                        dve.tensor_tensor(xs, bank[4 + h][:, :].rearrange("p (t n) -> p t n", t=2), xs, ALU.add).then_inc(s_ys, 1)

                dve.wait_ge(s_bo, GROUPS)
                divide(0)
                residual(0)
                start, per = steps.n, 2 * KC
                with dve.Fori(1, GROUPS) as g:
                    steps.base, steps.n = start + (g - 1) * per, 0
                    divide(g)
                    residual(g)

            @block.tensor
            def _(pe):
                pe.wait_ge(s_w, 16 * 9)

                def project(g, p):
                    static = isinstance(g, int)
                    pe.wait_ge(s_rows, GT * (g + 1))
                    transpose_rows(pe, p, bank[0:2], s_xt)
                    pe.wait_ge(s_xts, KC * (g + 1))
                    for t in range(GT):
                        if not static or GT * g + t >= 2:
                            pe.wait_ge(s_v, GT * g + t - 1)
                        for k in range(KC):
                            mm = pe.matmul(bank[4 + t % 2][:, :], xn_t[:, k, t * P:(t + 1) * P], wkv_sb[:, k, :],
                                           start=(k == 0), stop=(k == KC - 1))
                        mm.then_inc(s_kv, 1)
                    for m in range(KC):
                        if not static or g >= 1:
                            pe.wait_ge(s_qs, KC * (g - 1) + m + 1)
                        for k in range(KC):
                            mm = pe.matmul(bank[2 + m][:, :], wq_sb[:, k, m * P:(m + 1) * P], xn_t[:, k, :],
                                           start=(k == 0), stop=(k == KC - 1))
                        mm.then_inc(s_q, 1)

                def parts(g, p):
                    static = isinstance(g, int)
                    pe.wait_ge(s_kf, GT * (g + 1))
                    pe.wait_ge(s_v, GT * (g + 1))
                    if not static or g >= 1:
                        pe.wait_ge(s_part, KC * g)
                    for k in range(KC):
                        for t in range(GT):
                            mm = pe.matmul(bank[6 + k][:, 0:VW], kf[:, p, t, k * P:(k + 1) * P], v1[:, p, t, k, :],
                                           start=(t == 0), stop=(t == GT - 1))
                    mm.then_inc(s_kvp, 1)

                def step(g, p):
                    if not isinstance(g, int) or g < GROUPS:
                        project(g, p)
                    if not isinstance(g, int) or g >= 1:
                        parts(g - 1, 1 - p)

                over_groups(pe, step, 2)

                pe.wait_ge(s_kvm, BATCH)
                pe.wait_ge(s_dve, GROUPS * STATS_STEPS + BATCH * (GROUPS // BATCH))
                pe.wait_ge(s_qd, GROUPS)

                def outputs(g, b):
                    static = isinstance(g, int)
                    for k in range(KC):
                        if not static or g >= 1:
                            pe.wait_ge(s_ot, KC * (g - 1) + k + 1)
                        for a in range(2):
                            mm = pe.matmul(bank[2 * k + a][:, :], kvm[:, b, k, a, :], q_flat[:, k, ds(g * GN, GN)],
                                           start=True, stop=True)
                        mm.then_inc(s_od, 1)

                def mix(g):
                    static = isinstance(g, int)
                    pe.wait_ge(s_ot, KC * (g + 1))
                    for h in range(2):
                        if not static or g >= 1:
                            pe.wait_ge(s_ys, 2 * (g - 1) + h + 1)
                        for t in (2 * h, 2 * h + 1):
                            for k in range(KC):
                                mm = pe.matmul(bank[4 + h][:, (t % 2) * D:(t % 2 + 1) * D], o_t[:, k, t * P:(t + 1) * P],
                                               wo_sb[:, k, :], start=(k == 0), stop=(k == KC - 1))
                        mm.then_inc(s_y, 1)

                GB = GROUPS // BATCH
                outputs(0, 0)
                mix(0)
                for b in range(BATCH):
                    with pe.Fori(b * GB + (b == 0), (b + 1) * GB) as g:
                        outputs(g, b)
                        mix(g)

    attention()
    mixture(1, acc1)
    linear_attention()
    mixture(2, out)


def constants():
    import numpy as np
    p = np.arange(P)[:, None]
    i = np.arange(P)[None, :]
    scale = 1.0 / np.sqrt(D * SPAN)
    own = ((p <= i) & (i - p < SPAN)) * scale
    prev = (p > i[:, 0:SPAN] + P - SPAN) * scale
    prev = np.concatenate([prev * (g % (GROUPS // BATCH) != 0) for g in range(GROUPS)], axis=1)
    decay = np.exp(-(np.arange(SEQ) / SEQ))
    pair_tile = np.arange(PAIRS) % TILES
    parts = {
        "ident": p == i, "mask_own": own, "mask_prev": prev, "before": p < i, "ones": np.ones((P, P)),
        "dec": decay.reshape(SEQ // P, P).T, "rank_e": EXPERTS - np.arange(EXPERTS)[None, :] + 0 * p,
        "seg": (np.arange(EXPERTS * TILES) % TILES != 0)[None, :] + 0 * p, "iota": i + 0 * p,
        "token1": pair_tile[None, :] * P + p + 1, "spare1": TOKENS + 1 + p, "head_block": p // DK == i // DK,
    }
    table = np.zeros((P, CONST_W), np.float32)
    for name, a in parts.items():
        at, n = CONST_COLS[name]
        table[:, at:at + n] = a
    return table, decay.astype(np.float32)


def kernel(L0_attn_a_x, L0_attn_a_W_qkv, L0_attn_a_b_qkv, L0_attn_a_ln_w, L0_attn_a_ln_b, L0_attn_b_W_q, L0_attn_b_b_q,
           L0_attn_b_W_k, L0_attn_b_b_k, L0_attn_b_W_v, L0_attn_b_b_v, L0_attn_b_W_o, L0_attn_b_b_o, L0_ffn_Wg, L0_ffn_bg,
           L0_ffn_W1, L0_ffn_b1, L0_ffn_W2, L0_ffn_b2):
    import numpy as np
    import concourse.bacc as bacc
    from concourse.bass_utils import run_bass_kernel_spmd

    table, decay = constants()
    a = np.asarray
    arrays = {
        "x": a(L0_attn_a_x).reshape(TOKENS, D), "w_qkv": a(L0_attn_a_W_qkv), "bqkv_cols": a(L0_attn_a_b_qkv).reshape(3 * KC, P).T,
        "b_qkv": a(L0_attn_a_b_qkv),
        "ln_w": a(L0_attn_a_ln_w), "ln_b": a(L0_attn_a_ln_b),
        "wq_t": a(L0_attn_b_W_q).T, "bq_cols": a(L0_attn_b_b_q).reshape(KC, P).T, "wk_t": a(L0_attn_b_W_k).T, "b_k": a(L0_attn_b_b_k),
        "wv_t": a(L0_attn_b_W_v).T, "b_v": a(L0_attn_b_b_v), "wo_t": a(L0_attn_b_W_o).T, "b_o": a(L0_attn_b_b_o),
        "wg": a(L0_ffn_Wg), "bg": a(L0_ffn_bg), "w1": a(L0_ffn_W1), "b1": a(L0_ffn_b1), "w2": a(L0_ffn_W2),
        "b2": a(L0_ffn_b2), "consts": table, "dec_row": decay,
    }
    arrays = {n: np.ascontiguousarray(v) for n, v in arrays.items()}
    nc = bacc.Bacc("TRN2", target_bir_lowering=False, num_devices=1)
    args = [nc.dram_tensor(f"in_{n}", v.shape, mybir.dt.from_np(v.dtype), kind="ExternalInput").ap()
            for n, v in arrays.items()]
    out = nc.dram_tensor("out_x", (TOKENS + SPARE, D), F32, kind="ExternalOutput").ap()
    program(nc, *args, out)
    r = run_bass_kernel_spmd(nc, [{f"in_{n}": v for n, v in arrays.items()}], core_ids=[0])
    return np.asarray(r.results[0]["out_x"])[0:TOKENS].reshape(BATCH, SEQ, D)
```

```python
from contextlib import ExitStack

import concourse.bass as bass
from concourse import mybir

F32 = mybir.dt.float32
BF16 = mybir.dt.bfloat16
I32 = mybir.dt.int32
U32 = mybir.dt.uint32
ALU = mybir.AluOpType
ACT = mybir.ActivationFunctionType
AX = mybir.AxisListType

P = 128
BATCH, SEQ, D = 2, 2048, 256
TOKENS = BATCH * SEQ
KC = D // P
TILES = TOKENS // P
GT = 4
GROUPS = TILES // GT
GN = GT * P
SPAN = 64
LN_EPS = 1e-5
EXPERTS, HID, TOPK = 8, 512, 2
HC = HID // P
TEMP = 5.0
GATE_EPS = 1e-9
ROW = D + EXPERTS
PAIRS = TILES * TOPK
SLOT_TILES = TOKENS * TOPK // P + EXPERTS - 1
SPARE = P
RING = 5
assert (SLOT_TILES - 1) % RING == 0
HEADS = 16
DK = D // HEADS
DEN_EPS = 1e-6
VW = P + 2
RSQRT_MAGIC = 0x5F3759DF

CONST_COLS = {}


def _const_layout():
    at = 0
    for name, n in (("ident", P), ("mask_own", P), ("mask_prev", GROUPS * SPAN), ("before", P), ("ones", P),
                    ("dec", SEQ // P), ("rank_e", EXPERTS), ("seg", EXPERTS * TILES), ("iota", P),
                    ("token1", PAIRS), ("spare1", 1), ("head_block", P)):
        CONST_COLS[name] = (at, n)
        at += n
    return at


CONST_W = _const_layout()


class Steps:

    def __init__(self, eng, sem):
        self.eng, self.sem, self.base, self.n = eng, sem, 0, 0

    def did(self, ins):
        ins.then_inc(self.sem, 1)
        self.n += 1

    def wait(self):
        self.eng.wait_ge(self.sem, self.base + self.n)

    def chain(self, ins):
        self.did(ins)
        self.wait()


def over_groups(eng, step, unroll, steps=None, per_step=0):
    assert (GROUPS - 2) % unroll == 0
    step(0, 0)
    start, per = (steps.n if steps else 0), per_step * unroll
    with eng.Fori(0, (GROUPS - 2) // unroll) as i:
        if steps:
            steps.base, steps.n = start + i * per, 0
        for u in range(unroll):
            step(unroll * i + (1 + u), (1 + u) % unroll)
        assert not steps or steps.n == per, (steps.n, per)
    if steps:
        steps.base, steps.n = 0, start + per_step * (GROUPS - 2)
    step(GROUPS - 1, (GROUPS - 1) % unroll)
    step(GROUPS, GROUPS % unroll)


def program(nc, x, w_qkv, bqkv_cols, b_qkv, ln_w, ln_b, wq_t, bq_cols, wk_t, b_k, wv_t, b_v, wo_t, b_o,
            wg, bg, w1, b1, w2, b2, consts, dec_row, out):
    with ExitStack() as ctx:
        _program(nc, ctx, x, w_qkv, bqkv_cols, b_qkv, ln_w, ln_b, wq_t, bq_cols, wk_t, b_k, wv_t, b_v, wo_t, b_o,
                 wg, bg, w1, b1, w2, b2, consts, dec_row, out)


def _program(nc, ctx, x, w_qkv, bqkv_cols, b_qkv, ln_w, ln_b, wq_t, bq_cols, wk_t, b_k, wv_t, b_v, wo_t, b_o,
             wg, bg, w1, b1, w2, b2, consts, dec_row, out):
    ds = bass.ds

    def sb(name, shape, dt=F32, c=ctx):
        return c.enter_context(nc.sbuf_tensor(name, shape, dt))

    def sem(name, c=ctx):
        return c.enter_context(nc.semaphore(name))

    bank = [ctx.enter_context(nc.psum_tensor(f"bank{i}", [P, 512], F32)) for i in range(8)]

    x_sb = sb("x_sb", [P, TILES, D])
    w1_sb = sb("w1_sb", [P, EXPERTS, KC, HID])
    w2_sb = sb("w2_sb", [P, EXPERTS, HC, D])
    wg_sb = sb("wg_sb", [P, KC, EXPERTS])
    bg_sb = sb("bg_sb", [P, EXPERTS])
    cst = sb("cst", [P, CONST_W])
    rows = sb("rows", [P, 3, GT, D])
    xn_t = sb("xn_t", [P, KC, GN])
    st = sb("st", [P, TILES, 6])
    mean = sb("mean", [P, TILES])
    var = sb("var", [P, TILES])
    half = sb("half", [P, TILES], I32)
    rs = sb("rs", [P, TILES])
    ra = sb("ra", [P, TILES])
    rb = sb("rb", [P, TILES])

    def const(name):
        at, n = CONST_COLS[name]
        return cst[:, at:at + n]

    ident = const("ident")

    table = nc.dram_tensor("row_table", [TOKENS + SPARE, ROW], F32).ap()
    acc1 = nc.dram_tensor("sum_1", [TOKENS + SPARE, D], F32).ap()

    def tiled(dram, g, width):
        return dram[ds(g * GN, GN), :].rearrange("(t p) n -> p t n", p=P) if not isinstance(g, int) else \
            dram[g * GN:(g + 1) * GN, :].rearrange("(t p) n -> p t n", p=P)

    def moments(eng, steps, n):
        v, m, r, a, b, h = (t[:, 0:n] for t in (var, mean, rs, ra, rb, half))
        mean_even, m2_even, mean_odd, m2_odd = (st[:, 0:n, i] for i in (1, 2, 4, 5))
        steps.did(eng.tensor_tensor(a, mean_even, mean_odd, ALU.add))
        steps.did(eng.tensor_tensor(b, mean_even, mean_odd, ALU.subtract))
        steps.did(eng.tensor_tensor(v, m2_even, m2_odd, ALU.add))
        steps.wait()
        steps.did(eng.tensor_scalar(m, a, 0.5, None, ALU.mult))
        steps.did(eng.tensor_scalar(v, v, 1.0 / D, LN_EPS, ALU.mult, ALU.add))
        steps.chain(eng.scalar_tensor_tensor(r, b, 0.25, b, ALU.mult, ALU.mult))
        steps.chain(eng.tensor_tensor(v, v, r, ALU.add))
        steps.chain(eng.tensor_scalar(h, v.bitcast(I32), 1, None, ALU.logical_shift_right))
        steps.chain(eng.tensor_scalar(r.bitcast(I32), h, -1.0, float(RSQRT_MAGIC), ALU.mult, ALU.add))
        for _ in range(3):
            steps.chain(eng.scalar_tensor_tensor(a, r, -0.5, r, ALU.mult, ALU.mult))
            steps.chain(eng.tensor_tensor(b, a, v, ALU.mult))
            steps.chain(eng.scalar_tensor_tensor(r, b, 1.5, r, ALU.add, ALU.mult))

    MOMENT_STEPS = 18

    def stats(eng, steps, source):
        for t in range(GT):
            steps.did(eng.bn_stats(st[:, t, :], source(t)))
        steps.wait()
        moments(eng, steps, GT)

    STATS_STEPS = GT + MOMENT_STEPS

    def normalise(eng, p, source, done, at=0):
        for t in range(GT):
            eng.tensor_scalar(rows[:, p, t, 0:D], source(t), mean[:, ds(at + t, 1)], rs[:, ds(at + t, 1)],
                              ALU.subtract, ALU.mult).then_inc(done, 1)

    def transpose_rows(eng, p, banks, done):
        for c in range(KC):
            for t in range(GT):
                mm = eng.transpose(banks[c][:, t * P:(t + 1) * P], rows[:, p, t, c * P:(c + 1) * P], ident)
        mm.then_inc(done, 1)

    def attention():
        with ExitStack() as c:
            w_sb = sb("wqkv_sb", [P, KC, 3 * D], c=c)
            bqk = sb("bqk", [P, 2 * KC], c=c)
            bv_sb = sb("bv_sb", [P, D], c=c)
            lw = sb("lw", [P, D], c=c)
            lb = sb("lb", [P, D], c=c)
            q_t = sb("q_t", [P, 3, KC, GN], c=c)
            k_t = sb("k_t", [P, 3, KC, GN], c=c)
            v_sb = sb("v_sb", [P, 3, GT, D], c=c)
            sc = sb("sc", [P, 2, 2 * P], c=c)
            o_sb = sb("o_sb", [P, GT, D], c=c)
            n_sb = sb("n_sb", [P, GT, D], c=c)
            zeros = sb("zeros", [P, ROW], c=c)

            s_x0, s_x1, s_x2 = (sem(f"a_x{i}", c) for i in range(3))
            s_w = sem("a_weights", c)
            s_big = sem("a_ffn_weights", c)
            s_zero = sem("a_zeroed", c)
            s_z = sem("a_zeros_out", c)
            s_dve = sem("a_dve_steps", c)
            s_pool = sem("a_pool_steps", c)
            s_rows = sem("a_rows", c)
            s_xt, s_xts = sem("a_xt_psum", c), sem("a_xt", c)
            s_qk, s_qks = sem("a_qk_psum", c), sem("a_qk", c)
            s_v, s_vs = sem("a_v_psum", c), sem("a_v", c)
            s_s, s_ss = sem("a_scores_psum", c), sem("a_scores", c)
            s_o, s_os = sem("a_out_psum", c), sem("a_out", c)
            s_n = sem("a_out_normalised", c)
            s_res = sem("a_residual", c)

            block = c.enter_context(nc.Block())

            @block.sync
            def _(sp):
                sp.dma_start(x_sb[:, 0:GT, :], tiled(x, 0, D)).then_inc(s_x0, 16)
                sp.dma_start(cst[:, :], consts).then_inc(s_w, 16)
                sp.dma_start(w_sb[:, :, :], w_qkv.rearrange("(c p) n -> p c n", p=P)).then_inc(s_w, 16)
                sp.dma_start(x_sb[:, GT:2 * GT, :], tiled(x, 1, D)).then_inc(s_x1, 16)
                for g in range(2, GROUPS):
                    sp.dma_start(x_sb[:, g * GT:(g + 1) * GT, :], tiled(x, g, D)).then_inc(s_x2, 16)
                for e in range(EXPERTS):
                    sp.dma_start(w1_sb[:, e, :, :], w1[e].rearrange("(c p) n -> p c n", p=P)).then_inc(s_big, 16)
                    sp.dma_start(w2_sb[:, e, :, :], w2[e].rearrange("(c p) n -> p c n", p=P)).then_inc(s_big, 16)
                sp.wait_ge(s_zero, 4)
                sp.dma_start(table[TOKENS:TOKENS + SPARE, :], zeros[:, :]).then_inc(s_z, 16)
                sp.dma_start(acc1[TOKENS:TOKENS + SPARE, :], zeros[:, 0:D]).then_inc(s_z, 16)
                sp.dma_start(out[TOKENS:TOKENS + SPARE, :], zeros[:, 0:D]).then_inc(s_z, 16)
                sp.wait_ge(s_z, 48)
                sp.wait_ge(s_big, 16 * (2 * EXPERTS))

            def evacuate_q_k(act, g, p):
                if not isinstance(g, int) or g >= 2:
                    act.wait_ge(s_s, GT * (g - 1))
                for m in range(2 * KC):
                    act.wait_ge(s_qk, 2 * KC * g + m + 1)
                    to = (q_t if m < KC else k_t)[:, p, m % KC, :]
                    act.activation(to, bank[2 + m % 2][:, :], ACT.Identity, bias=bqk[:, m:m + 1]).then_inc(s_qks, 1)

            @block.scalar
            def _(act):
                act.dma_start(bqk[:, :], bqkv_cols[:, 0:2 * KC]).then_inc(s_w, 16)
                act.dma_start(bv_sb[:, :], b_qkv[2 * D:3 * D].partition_broadcast(P)).then_inc(s_w, 16)
                act.dma_start(lw[:, :], ln_w.partition_broadcast(P)).then_inc(s_w, 16)
                act.dma_start(lb[:, :], ln_b.partition_broadcast(P)).then_inc(s_w, 16)
                act.dma_start(wg_sb[:, :, :], wg.rearrange("(c p) n -> p c n", p=P)).then_inc(s_w, 16)
                act.dma_start(bg_sb[:, :], bg.partition_broadcast(P)).then_inc(s_w, 16)
                act.wait_ge(s_w, 16 * 8)

                def step(g, p):
                    if g != GROUPS if isinstance(g, int) else True:
                        if not isinstance(g, int) or g >= 1:
                            act.wait_ge(s_v, 2 * g)
                        act.wait_ge(s_xt, g + 1)
                        for k in range(KC):
                            act.activation(xn_t[:, k, :], bank[k][:, :], ACT.Copy).then_inc(s_xts, 1)
                        evacuate_q_k(act, g, p)
                    if not isinstance(g, int) or g >= 1:
                        if not isinstance(g, int) or g >= 2:
                            act.wait_ge(s_n, GT * (g - 1))
                        for t in range(GT):
                            act.wait_ge(s_o, GT * (g - 1) + t + 1)
                            act.activation(o_sb[:, t, :], bank[6 + t % 2][:, 0:D], ACT.Copy).then_inc(s_os, 1)

                over_groups(act, step, 3)

            @block.vector
            def _(dve):
                steps = Steps(dve, s_dve)
                dve.memset(sc[:, :, P + SPAN:2 * P], 0.0).then_inc(s_zero, 1)
                dve.memset(k_t[:, 2, :, GN - P:GN], 0.0).then_inc(s_zero, 1)
                dve.memset(v_sb[:, 2, GT - 1, :], 0.0).then_inc(s_zero, 1)
                dve.memset(zeros[:, :], 0.0).then_inc(s_zero, 1)

                def front(g, p):
                    if not isinstance(g, int) or g >= 3:
                        dve.wait_ge(s_xt, g - 2)
                    stats(dve, steps, lambda t: x_sb[:, ds(g * GT + t, 1), :])
                    normalise(dve, p, lambda t: x_sb[:, ds(g * GT + t, 1), :], s_rows)

                def masked(g, t):
                    dve.wait_ge(s_s, GT * g + t + 1)
                    dve.tensor_tensor(sc[:, t % 2, 0:P], bank[t % 2][:, 0:P], const("mask_own"),
                                      ALU.mult).then_inc(s_ss, 1)
                    at = CONST_COLS["mask_prev"][0]
                    m = cst[:, ds(at + g * SPAN, SPAN)] if t == 0 else cst[:, at + SPAN:at + 2 * SPAN]
                    dve.tensor_tensor(sc[:, t % 2, P:P + SPAN], bank[t % 2][:, P:P + SPAN], m,
                                      ALU.mult).then_inc(s_ss, 1)

                def step(g, p):
                    static = isinstance(g, int)
                    if not static or g == 1:
                        dve.wait_ge(s_x2, 16 * (GROUPS - 2))
                    if static and g == 0:
                        dve.wait_ge(s_x0, 16)
                        front(0, 0)
                        dve.wait_ge(s_x1, 16)
                        dve.wait_ge(s_w, 16 * 8)
                    if not static or g < GROUPS:
                        if not static or g >= 2:
                            dve.wait_ge(s_o, GT * (g - 1))
                        for h in range(2):
                            dve.wait_ge(s_v, 2 * g + h + 1)
                            dve.tensor_tensor(v_sb[:, p, 2 * h:2 * h + 2, :],
                                              bank[4 + h][:, :].rearrange("p (t n) -> p t n", t=2),
                                              bv_sb[:, :].unsqueeze(1).to_broadcast([P, 2, D]),
                                              ALU.add).then_inc(s_vs, 1)
                    if not static or g < GROUPS - 1:
                        front(g + 1, (p + 1) % 3)
                    if not static or g >= 1:
                        for t in range(GT):
                            masked(g - 1, t)
                        dve.wait_ge(s_os, GT * g)
                        if not static or g >= 2:
                            dve.wait_ge(s_res, 3 * (g - 1))
                        stats(dve, steps, lambda t: o_sb[:, t, :])
                        for t in range(GT):
                            dve.tensor_scalar(n_sb[:, t, :], o_sb[:, t, :], mean[:, t:t + 1], rs[:, t:t + 1],
                                              ALU.subtract, ALU.mult).then_inc(s_n, 1)

                over_groups(dve, step, 3, steps, 2 * STATS_STEPS)

            @block.gpsimd
            def _(pool):
                pool.wait_ge(s_w, 16 * 8)
                with pool.Fori(0, GROUPS) as g:
                    pool.wait_ge(s_n, GT * g + GT)
                    pool.tensor_tensor(n_sb[:, :, :], n_sb[:, :, :], lw[:, :].unsqueeze(1).to_broadcast([P, GT, D]),
                                       ALU.mult).then_inc(s_res, 1)
                    pool.wait_ge(s_res, 3 * g + 1)
                    pool.tensor_tensor(n_sb[:, :, :], n_sb[:, :, :], lb[:, :].unsqueeze(1).to_broadcast([P, GT, D]),
                                       ALU.add).then_inc(s_res, 1)
                    pool.wait_ge(s_res, 3 * g + 2)
                    pool.tensor_tensor(x_sb[:, ds(g * GT, GT), :], x_sb[:, ds(g * GT, GT), :], n_sb[:, :, :],
                                       ALU.add).then_inc(s_res, 1)

            @block.tensor
            def _(pe):
                pe.wait_ge(s_w, 16 * 8)
                pe.wait_ge(s_zero, 3)

                def project(g, p):
                    pe.wait_ge(s_rows, GT * (g + 1))
                    transpose_rows(pe, p, bank[0:2], s_xt)
                    pe.wait_ge(s_xts, KC * (g + 1))
                    for m in range(2 * KC):
                        if not isinstance(g, int) or 2 * KC * g + m >= 2:
                            pe.wait_ge(s_qks, 2 * KC * g + m - 1)
                        for k in range(KC):
                            mm = pe.matmul(bank[2 + m % 2][:, :], w_sb[:, k, m * P:(m + 1) * P], xn_t[:, k, :],
                                           start=(k == 0), stop=(k == KC - 1))
                        mm.then_inc(s_qk, 1)
                    for h in range(2):
                        if not isinstance(g, int) or g >= 1:
                            pe.wait_ge(s_vs, 2 * g + h - 1)
                        for t in (2 * h, 2 * h + 1):
                            for k in range(KC):
                                mm = pe.matmul(bank[4 + h][:, (t % 2) * D:(t % 2 + 1) * D],
                                               xn_t[:, k, t * P:(t + 1) * P], w_sb[:, k, 2 * D:3 * D],
                                               start=(k == 0), stop=(k == KC - 1))
                        mm.then_inc(s_v, 1)

                def before(p, t):
                    return (p, t - 1) if t else ((p - 1) % 3, GT - 1)

                def scores(p, t):
                    for k in range(KC):
                        pe.matmul(bank[t % 2][:, 0:P], k_t[:, p, k, t * P:(t + 1) * P],
                                  q_t[:, p, k, t * P:(t + 1) * P], start=(k == 0), stop=(k == KC - 1))
                    pb, tb = before(p, t)
                    for k in range(KC):
                        mm = pe.matmul(bank[t % 2][:, P:P + SPAN], k_t[:, pb, k, tb * P:(tb + 1) * P],
                                       q_t[:, p, k, t * P:t * P + SPAN], start=(k == 0), stop=(k == KC - 1))
                    mm.then_inc(s_s, 1)

                def values(g, p, t):
                    pe.wait_ge(s_ss, 2 * (GT * g + t + 1))
                    if not isinstance(g, int) or GT * g + t >= 2:
                        pe.wait_ge(s_os, GT * g + t - 1 if t >= 2 else GT * g)
                    pb, tb = before(p, t)
                    pe.matmul(bank[6 + t % 2][:, 0:D], sc[:, t % 2, 0:P], v_sb[:, p, t, :], start=True, stop=False)
                    pe.matmul(bank[6 + t % 2][:, 0:D], sc[:, t % 2, P:2 * P], v_sb[:, pb, tb, :],
                              start=False, stop=True).then_inc(s_o, 1)

                def attend(g, p):
                    pe.wait_ge(s_qks, 2 * KC * (g + 1))
                    pe.wait_ge(s_vs, 2 * (g + 1))
                    scores(p, 0)
                    for t in range(1, GT):
                        scores(p, t)
                        values(g, p, t - 1)
                    values(g, p, GT - 1)

                def step(g, p):
                    if not isinstance(g, int) or g < GROUPS:
                        project(g, p)
                    if not isinstance(g, int) or g >= 1:
                        attend(g - 1, (p - 1) % 3)

                over_groups(pe, step, 3)

    def mixture(n, total):
        with ExitStack() as c:
            b1_sb = sb(f"m{n}_b1", [P, EXPERTS, HID], c=c)
            b2_sb = sb(f"m{n}_b2", [P, EXPERTS, D], c=c)
            logit = sb(f"m{n}_logit", [P, TILES, EXPERTS], c=c)
            prob = sb(f"m{n}_prob", [P, TILES, EXPERTS], c=c)
            tmp = sb(f"m{n}_tmp", [P, TILES, EXPERTS], c=c)
            col = sb(f"m{n}_col", [P, 8, TILES], c=c)
            first = sb(f"m{n}_first", [P, TILES, EXPERTS], c=c)
            second = sb(f"m{n}_second", [P, TILES, EXPERTS], c=c)
            either = sb(f"m{n}_either", [P, TILES, EXPERTS], BF16, c=c)
            cb = sb(f"m{n}_cb", [P, 2 * P], BF16, c=c)
            tot = sb(f"m{n}_tot", [P, EXPERTS, TILES], c=c)
            inc = sb(f"m{n}_inc", [P, EXPERTS, TILES], c=c)
            pos = sb(f"m{n}_pos", [P, TILES, EXPERTS], c=c)
            e8 = sb(f"m{n}_e8", [P, 4, EXPERTS], c=c)
            e8i = sb(f"m{n}_e8i", [P, 2, EXPERTS], I32, c=c)
            slot = sb(f"m{n}_slot", [P, 3, PAIRS], c=c)
            sloti = sb(f"m{n}_sloti", [P, 3, PAIRS], I32, c=c)
            in_tile = x_sb[:, :, :].rearrange("p t n -> p (t n)").rearrange("p (a b) -> p a b", b=P)
            of_tile = sb(f"m{n}_of_tile", [P, PAIRS, SLOT_TILES + 1], c=c)
            tile_e = sb(f"m{n}_tile_e", [P, SLOT_TILES + 1, EXPERTS], c=c)
            idxf = sb(f"m{n}_idxf", [P, 2, SLOT_TILES + 1], c=c)
            idx = sb(f"m{n}_idx", [P, SLOT_TILES + 1], U32, c=c)
            expert = sb(f"m{n}_expert", [P, SLOT_TILES + 1], I32, c=c)
            gather_i = [sb(f"m{n}_gather_i{r}", [P, 1], U32, c=c) for r in range(RING)]
            sum_i = [sb(f"m{n}_sum_i{r}", [P, 1], U32, c=c) for r in range(RING)]
            xg = [sb(f"m{n}_xg{r}", [P, ROW], c=c) for r in range(RING)]
            y_sc = [sb(f"m{n}_y_sc{r}", [P, D], c=c) for r in range(RING)]
            xg_t = sb(f"m{n}_xg_t", [P, KC, P], c=c)
            h_sb = sb(f"m{n}_h", [P, HID], c=c)
            h_t = sb(f"m{n}_h_t", [P, HC, P], c=c)
            y_sb = sb(f"m{n}_y", [P, D], c=c)

            carry = sb(f"m{n}_carry", [P, 2 * RING + 1], c=c)
            s_carry = sem(f"m{n}_carry_zeroed", c)
            s_bias = sem(f"m{n}_biases", c)
            s_dve = sem(f"m{n}_dve_steps", c)
            s_st, s_rows = sem(f"m{n}_statistics", c), sem(f"m{n}_rows", c)
            s_either = sem(f"m{n}_chosen", c)
            s_gates = sem(f"m{n}_gates", c)
            s_xt, s_xts = sem(f"m{n}_xt_psum", c), sem(f"m{n}_xt", c)
            s_lg, s_mx, s_ex = sem(f"m{n}_logits", c), sem(f"m{n}_shifted", c), sem(f"m{n}_exp", c)
            s_out = [sem(f"m{n}_rows_out{p}", c) for p in range(2)]
            s_xout, s_gout = sem(f"m{n}_x_out", c), sem(f"m{n}_gates_out", c)
            s_cnt, s_onehot, s_inv = sem(f"m{n}_counted", c), sem(f"m{n}_onehot", c), sem(f"m{n}_tokens", c)
            s_idx = sem(f"m{n}_indices", c)
            s_ib = sem(f"m{n}_index_copied", c)
            s_g = [sem(f"m{n}_gathered{r}", c) for r in range(RING)]
            s_sum = sem(f"m{n}_summed", c)
            f_xt, f_xts = sem(f"m{n}_slot_xt_psum", c), sem(f"m{n}_slot_xt", c)
            f_h, f_hb = sem(f"m{n}_h_psum", c), sem(f"m{n}_h_biased", c)
            f_ht, f_gelu = sem(f"m{n}_h_t_psum", c), sem(f"m{n}_h_gelu", c)
            f_y, f_yb, f_ys = sem(f"m{n}_y_psum", c), sem(f"m{n}_y_biased", c), sem(f"m{n}_y_gated", c)

            block = c.enter_context(nc.Block())

            def over_slots(eng, step):
                for s in range(RING):
                    step(s, s)
                with eng.Fori(1, (SLOT_TILES - 1) // RING) as i:
                    step.turn = i
                    for u in range(RING):
                        step(RING * i + u, u)
                step(SLOT_TILES - 1, (SLOT_TILES - 1) % RING)
                step(SLOT_TILES, SLOT_TILES % RING)


            @block.sync
            def _(sp):
                def store(g, p):
                    sp.wait_ge(s_rows, GT * g + GT)
                    sp.dma_start(tiled(table, g, ROW)[:, :, 0:D], rows[:, p, :, :]).then_inc(s_out[p], 16)
                    sp.dma_start(tiled(total, g, D), x_sb[:, ds(g * GT, GT), :]).then_inc(s_xout, 16)
                sp.dma_start(b1_sb[:, :, :], b1.partition_broadcast(P)).then_inc(s_bias, 16)
                sp.dma_start(b2_sb[:, :, :], b2.partition_broadcast(P)).then_inc(s_bias, 16)
                with sp.Fori(0, GROUPS // 2) as i:
                    store(2 * i, 0)
                    store(2 * i + 1, 1)
                sp.wait_ge(s_gates, 1)
                sp.dma_start(table[0:TOKENS, D:ROW].rearrange("(t p) n -> p t n", p=P), tmp[:, :, :]).then_inc(s_gout, 16)

            @block.gpsimd
            def _(pool):
                pool.wait_ge(s_idx, 2)
                for p in range(2):
                    pool.wait_ge(s_out[p], 16 * GROUPS // 2)
                pool.wait_ge(s_xout, 16 * GROUPS)
                pool.wait_ge(s_gout, 16)

                pool.memset(carry[:, :], 0.0).then_inc(s_carry, 1)
                pool.wait_ge(s_carry, 1)

                def carry_wait(place):
                    pool.tensor_tensor(carry[:, place:place + 1], carry[:, 2 * RING:], carry[:, 2 * RING:], ALU.add)

                def gather(s, r, copies):
                    pool.tensor_copy(gather_i[r][:, :], idx[:, ds(s, 1)]).then_inc(s_ib, 1)
                    pool.wait_ge(s_ib, copies)
                    carry_wait(r)
                    pool.indirect_dma_start(xg[r][:, :], None, table,
                                            bass.IndirectOffsetOnAxis(gather_i[r][:, 0:1], 0)).then_inc(s_g[r], 16)

                def step(s, r):
                    if isinstance(s, int) and s == SLOT_TILES:
                        return
                    ahead = not isinstance(s, int) or s + RING < SLOT_TILES
                    copies = (2 * s if not isinstance(s, int) or s + RING < SLOT_TILES else SLOT_TILES - RING + s) + RING
                    pool.tensor_copy(sum_i[r][:, :], idx[:, ds(s, 1)]).then_inc(s_ib, 1)
                    pool.wait_ge(s_ib, copies + 1)
                    pool.wait_ge(f_ys, s + 1)
                    if not isinstance(s, int) or s >= 1:
                        pool.wait_ge(s_sum, 16 * s)
                    carry_wait(RING + r)
                    pool.indirect_dma_start(total, bass.IndirectOffsetOnAxis(sum_i[r][:, 0:1], 0), y_sc[r][:, :], None,
                                            compute_op=ALU.add).then_inc(s_sum, 16)
                    if ahead:
                        gather(s + RING, r, copies + 2)

                for s in range(RING):
                    gather(s, s, s + 1)
                for s in range(RING):
                    step(s, s)
                with pool.Fori(1, (SLOT_TILES - 1) // RING - 1) as i:
                    for u in range(RING):
                        step(RING * i + u, u)
                for s in range(SLOT_TILES - 1 - RING, SLOT_TILES):
                    step(s, s % RING)
                pool.wait_ge(s_sum, 16 * SLOT_TILES)

            @block.scalar
            def _(act):
                def copy_rows(g, p):
                    if not isinstance(g, int) or g >= 1:
                        act.wait_ge(s_lg, g)
                    act.wait_ge(s_xt, g + 1)
                    for k in range(KC):
                        act.activation(xn_t[:, k, :], bank[k][:, :], ACT.Copy).then_inc(s_xts, 1)

                copy_rows(0, 0)
                with act.Fori(1, GROUPS) as g:
                    copy_rows(g, None)
                act.wait_ge(s_mx, 1)
                act.activation(prob[:, :, :], logit[:, :, :], ACT.Exp, scale=1.0 / TEMP).then_inc(s_ex, 1)

                act.wait_ge(s_idx, 2)

                def copy_slots(s, r):
                    act.wait_ge(f_xt, s + 1)
                    if not isinstance(s, int) or s >= 1:
                        act.wait_ge(f_h, s)
                    act.activation(xg_t[:, :, :], bank[0][:, 0:D].rearrange("p (c n) -> p c n", c=KC),
                                   ACT.Copy).then_inc(f_xts, 1)

                def step(s, r):
                    if not isinstance(s, int) or s < SLOT_TILES - 1:
                        copy_slots(s + 1, (r + 1) % RING)
                    if not isinstance(s, int) or s >= 1:
                        if not isinstance(s, int) or s >= RING + 1:
                            act.wait_ge(s_sum, 16 * (s - RING))
                        act.wait_ge(f_yb, s)
                        q = (r - 1) % RING
                        e = act.value_load(expert[0:1, ds(s - 1, 1)], min_val=0, max_val=EXPERTS - 1)
                        act.activation(y_sc[q][:, :], y_sb[:, :], ACT.Copy,
                                       scale=xg[q][:, ds(e + D, 1)]).then_inc(f_ys, 1)
                    if not isinstance(s, int) or s < SLOT_TILES:
                        act.wait_ge(f_ht, s + 1)
                        if not isinstance(s, int) or s >= 1:
                            act.wait_ge(f_y, s)
                        act.activation(h_t[:, :, :], bank[2][:, :].rearrange("p (c n) -> p c n", c=HC),
                                       ACT.Gelu).then_inc(f_gelu, 1)

                copy_slots(0, 0)
                over_slots(act, step)

            @block.vector
            def _(dve):
                steps = Steps(dve, s_dve)
                steps.chain(dve.tensor_copy(cb[:, 0:P], const("before")))
                steps.chain(dve.tensor_copy(cb[:, P:2 * P], const("ones")))

                def wide(c4):
                    return c4.unsqueeze(2).to_broadcast([P, TILES, EXPERTS])

                def by_expert(c8):
                    return c8.unsqueeze(1).to_broadcast([P, TILES, EXPERTS])

                with dve.Fori(0, GROUPS) as g:
                    for t in range(GT):
                        dve.bn_stats(st[:, ds(g * GT + t, 1), :].rearrange("p a n -> p (a n)"),
                                     x_sb[:, ds(g * GT + t, 1), :].rearrange("p a n -> p (a n)")).then_inc(s_st, 1)
                dve.wait_ge(s_st, TILES)
                moments(dve, steps, TILES)

                def row_step(g, p):
                    normalise(dve, p, lambda t: x_sb[:, ds(g * GT + t, 1), :], s_rows, g * GT)

                row_step(0, 0)
                row_step(1, 1)
                with dve.Fori(1, GROUPS // 2) as i:
                    for p in range(2):
                        dve.wait_ge(s_out[p], 16 * i)
                        dve.wait_ge(s_xt, 2 * i + p - 1)
                        row_step(2 * i + p, p)

                dve.wait_ge(s_lg, GROUPS)
                lg = bank[2][:, 0:TILES * EXPERTS].rearrange("p (t e) -> p t e", t=TILES)
                steps.chain(dve.tensor_tensor(logit[:, :, :], lg, by_expert(bg_sb[:, :]), ALU.add))
                steps.chain(dve.tensor_reduce(col[:, 0, :], logit[:, :, :], AX.X, ALU.max))
                dve.tensor_tensor(logit[:, :, :], logit[:, :, :], wide(col[:, 0, :]), ALU.subtract).then_inc(s_mx, 1)
                dve.wait_ge(s_ex, 1)
                steps.chain(dve.tensor_reduce(col[:, 1, :], prob[:, :, :], AX.X, ALU.add))
                steps.chain(dve.reciprocal(col[:, 2, :], col[:, 1, :]))
                steps.chain(dve.tensor_tensor(prob[:, :, :], prob[:, :, :], wide(col[:, 2, :]), ALU.mult))
                for k, hot in ((0, first), (1, second)):
                    steps.chain(dve.tensor_reduce(col[:, 3 + k, :], prob[:, :, :], AX.X, ALU.max))
                    steps.chain(dve.tensor_tensor(tmp[:, :, :], prob[:, :, :], wide(col[:, 3 + k, :]), ALU.is_equal))
                    steps.chain(dve.tensor_tensor(tmp[:, :, :], tmp[:, :, :], by_expert(const("rank_e")), ALU.mult))
                    steps.chain(dve.tensor_reduce(col[:, 5, :], tmp[:, :, :], AX.X, ALU.max))
                    steps.chain(dve.tensor_tensor(hot[:, :, :], tmp[:, :, :], wide(col[:, 5, :]), ALU.is_equal))
                    if k == 0:
                        steps.chain(dve.scalar_tensor_tensor(prob[:, :, :], hot[:, :, :], -2.0, prob[:, :, :],
                                                             ALU.mult, ALU.add))
                dve.tensor_tensor(either[:, :, :], first[:, :, :], second[:, :, :], ALU.add).then_inc(s_either, 1)
                steps.chain(dve.scalar_tensor_tensor(col[:, 6, :], col[:, 3, :], GATE_EPS, col[:, 4, :], ALU.add, ALU.add))
                steps.chain(dve.reciprocal(col[:, 7, :], col[:, 6, :]))
                steps.chain(dve.tensor_tensor(col[:, 3:5, :], col[:, 3:5, :],
                                              col[:, 7:8, :].to_broadcast([P, 2, TILES]), ALU.mult))
                steps.did(dve.tensor_tensor(tmp[:, :, :], first[:, :, :], wide(col[:, 3, :]), ALU.mult))
                steps.chain(dve.tensor_tensor(prob[:, :, :], second[:, :, :], wide(col[:, 4, :]), ALU.mult))
                dve.tensor_tensor(tmp[:, :, :], tmp[:, :, :], prob[:, :, :], ALU.add).then_inc(s_gates, 1)

                dve.wait_ge(s_cnt, 1)
                steps.chain(dve.tensor_copy(tot[:, :, :], bank[1][:, 0:TILES * EXPERTS].rearrange("p (t e) -> p e t", t=TILES)))
                flat = lambda a: a[:, :, :].rearrange("p a b -> p (a b)")
                steps.chain(dve.tensor_tensor_scan(flat(inc), const("seg"), flat(tot), 0.0, ALU.mult, ALU.add))
                steps.chain(dve.tensor_scalar(e8i[:, 0, :], inc[:, :, TILES - 1], float(P - 1), None, ALU.add))
                steps.chain(dve.tensor_scalar(e8i[:, 1, :], e8i[:, 0, :], 7, None, ALU.logical_shift_right))
                steps.chain(dve.tensor_copy(e8[:, 0, :], e8i[:, 1, :]))
                steps.chain(dve.tensor_tensor_scan(e8[:, 1, :], const("ones")[:, 0:EXPERTS], e8[:, 0, :], 0.0, ALU.mult, ALU.add))
                steps.chain(dve.tensor_tensor(e8[:, 2, :], e8[:, 1, :], e8[:, 0, :], ALU.subtract))
                steps.chain(dve.tensor_scalar(e8[:, 3, :], e8[:, 2, :], float(P), None, ALU.mult))
                steps.chain(dve.tensor_tensor(inc[:, :, :], inc[:, :, :], tot[:, :, :], ALU.subtract))
                steps.chain(dve.tensor_tensor(inc[:, :, :], inc[:, :, :], e8[:, 3, :].unsqueeze(2).to_broadcast([P, EXPERTS, TILES]), ALU.add))
                steps.chain(dve.tensor_tensor(pos[:, :, :], bank[0][:, 0:TILES * EXPERTS].rearrange("p (t e) -> p t e", t=TILES),
                                              inc[:, :, :].rearrange("p e t -> p t e"), ALU.add))
                for k, hot in ((0, first), (1, second)):
                    steps.chain(dve.tensor_tensor(hot[:, :, :], hot[:, :, :], pos[:, :, :], ALU.mult))
                    steps.chain(dve.tensor_reduce(slot[:, 0, k * TILES:(k + 1) * TILES], hot[:, :, :], AX.X, ALU.add))
                steps.chain(dve.tensor_copy(sloti[:, 0, :], slot[:, 0, :]))
                steps.chain(dve.tensor_scalar(sloti[:, 1, :], sloti[:, 0, :], 7, None, ALU.logical_shift_right))
                steps.chain(dve.tensor_scalar(sloti[:, 2, :], sloti[:, 0, :], P - 1, None, ALU.bitwise_and))
                steps.chain(dve.tensor_copy(slot[:, 1:3, :], sloti[:, 1:3, :]))
                iota = const("iota")
                NS1 = SLOT_TILES + 1
                steps.chain(dve.tensor_tensor(of_tile[:, :, :], iota[:, 0:NS1].unsqueeze(1).to_broadcast([P, PAIRS, NS1]),
                                              slot[:, 1, :].unsqueeze(2).to_broadcast([P, PAIRS, NS1]), ALU.is_equal))
                steps.chain(dve.tensor_tensor(of_tile[:, :, :], of_tile[:, :, :],
                                              const("token1").unsqueeze(2).to_broadcast([P, PAIRS, NS1]), ALU.mult))
                dve.wait_ge(s_xout, 16 * GROUPS)
                for q in range(4):
                    a = slice(q * PAIRS // 4, (q + 1) * PAIRS // 4)
                    dve.tensor_tensor(in_tile[:, a, :], iota.unsqueeze(1).to_broadcast([P, PAIRS // 4, P]),
                                      slot[:, 2, a].unsqueeze(2).to_broadcast([P, PAIRS // 4, P]),
                                      ALU.is_equal).then_inc(s_onehot, 1)
                steps.chain(dve.tensor_tensor(tile_e[:, :, :], e8[:, 1, :].unsqueeze(1).to_broadcast([P, NS1, EXPERTS]),
                                              iota[:, 0:NS1].unsqueeze(2).to_broadcast([P, NS1, EXPERTS]), ALU.is_le))
                steps.chain(dve.tensor_reduce(idxf[:, 0, :], tile_e[:, :, :], AX.X, ALU.add))
                steps.chain(dve.tensor_scalar(expert[:, :], idxf[:, 0, :], float(EXPERTS - 1), None, ALU.min))
                dve.wait_ge(s_inv, 1)
                steps.chain(dve.tensor_scalar(idxf[:, 0, :], bank[3][:, 0:NS1], 0.0, const("spare1"), ALU.is_equal, ALU.mult))
                steps.chain(dve.scalar_tensor_tensor(idxf[:, 1, :], bank[3][:, 0:NS1], -1.0, idxf[:, 0, :], ALU.add, ALU.add))
                dve.tensor_copy(idx[:, :], idxf[:, 1, :]).then_inc(s_idx, 2)

                dve.wait_ge(s_bias, 32)

                def bias_step(s, r):
                    if not isinstance(s, int) or s < SLOT_TILES:
                        e = dve.value_load(expert[0:1, ds(s, 1)], min_val=0, max_val=EXPERTS - 1)
                        dve.wait_ge(f_h, s + 1)
                        if not isinstance(s, int) or s >= 1:
                            dve.wait_ge(f_ht, s)
                        dve.tensor_tensor(h_sb[:, :], bank[1][:, :], b1_sb[:, ds(e, 1), :].rearrange("p a n -> p (a n)"), ALU.add).then_inc(f_hb, 1)
                    if not isinstance(s, int) or s >= 1:
                        e = dve.value_load(expert[0:1, ds(s - 1, 1)], min_val=0, max_val=EXPERTS - 1)
                        dve.wait_ge(f_y, s)
                        if not isinstance(s, int) or s >= 2:
                            dve.wait_ge(f_ys, s - 1)
                        dve.tensor_tensor(y_sb[:, :], bank[3][:, 0:D], b2_sb[:, ds(e, 1), :].rearrange("p a n -> p (a n)"), ALU.add).then_inc(f_yb, 1)

                over_slots(dve, bias_step)

            @block.tensor
            def _(pe):
                def logits(g, p):
                    pe.wait_ge(s_xts, KC * (g + 1))
                    for t in range(GT):
                        for k in range(KC):
                            mm = pe.matmul(bank[2][:, ds((g * GT + t) * EXPERTS, EXPERTS)], xn_t[:, k, t * P:(t + 1) * P],
                                           wg_sb[:, k, :], start=(k == 0), stop=(k == KC - 1))
                    mm.then_inc(s_lg, 1)

                def front(g, p):
                    pe.wait_ge(s_rows, GT * (g + 1))
                    transpose_rows(pe, p, bank[0:2], s_xt)
                    logits(g, p)

                front(0, 0)
                front(1, 1)
                with pe.Fori(1, GROUPS // 2) as i:
                    front(2 * i, 0)
                    front(2 * i + 1, 1)
                pe.wait_ge(s_either, 1)
                flat = either[:, :, :].rearrange("p t e -> p (t e)")
                pe.matmul(bank[0][:, 0:TILES * EXPERTS], cb[:, 0:P], flat, start=True, stop=True)
                pe.matmul(bank[1][:, 0:TILES * EXPERTS], cb[:, P:2 * P], flat, start=True, stop=True).then_inc(s_cnt, 1)
                for q in range(4):
                    pe.wait_ge(s_onehot, q + 1)
                    for a in range(q * PAIRS // 4, (q + 1) * PAIRS // 4):
                        mm = pe.matmul(bank[3][:, 0:SLOT_TILES + 1], in_tile[:, a, :], of_tile[:, a, :],
                                       start=(a == 0), stop=(a == PAIRS - 1))
                mm.then_inc(s_inv, 1)
                pe.wait_ge(s_idx, 2)

                def turn(s, r, filled):
                    pe.wait_ge(s_g[r], 16 * filled)
                    if not isinstance(s, int) or s >= 1:
                        pe.wait_ge(f_xts, s)
                    for k in range(KC):
                        mm = pe.transpose(bank[0][:, k * P:(k + 1) * P], xg[r][:, k * P:(k + 1) * P], ident)
                    mm.then_inc(f_xt, 1)

                def step(s, r):
                    static = isinstance(s, int)
                    if not static or s < SLOT_TILES:
                        e = pe.value_load(expert[0:1, ds(s, 1)], min_val=0, max_val=EXPERTS - 1)
                        pe.wait_ge(f_xts, s + 1)
                        if not static or s >= 1:
                            pe.wait_ge(f_hb, s)
                        for k in range(KC):
                            mm = pe.matmul(bank[1][:, :], xg_t[:, k, :], w1_sb[:, ds(e, 1), k, :].rearrange("p a n -> p (a n)"),
                                           start=(k == 0), stop=(k == KC - 1))
                        mm.then_inc(f_h, 1)
                    if not static or s < SLOT_TILES - 1:
                        turned = s // RING if static else step.turn
                        turn(s + 1, (r + 1) % RING, turned + (2 if r == RING - 1 else 1))
                    if not static or s >= 1:
                        e = pe.value_load(expert[0:1, ds(s - 1, 1)], min_val=0, max_val=EXPERTS - 1)
                        pe.wait_ge(f_gelu, s)
                        if not static or s >= 2:
                            pe.wait_ge(f_yb, s - 1)
                        for k in range(HC):
                            mm = pe.matmul(bank[3][:, 0:D], h_t[:, k, :], w2_sb[:, ds(e, 1), k, :].rearrange("p a n -> p (a n)"),
                                           start=(k == 0), stop=(k == HC - 1))
                        mm.then_inc(f_y, 1)
                    if not static or s < SLOT_TILES:
                        pe.wait_ge(f_hb, s + 1)
                        if not static or s >= 1:
                            pe.wait_ge(f_gelu, s)
                        for k in range(HC):
                            mm = pe.transpose(bank[2][:, k * P:(k + 1) * P], h_sb[:, k * P:(k + 1) * P], ident)
                        mm.then_inc(f_ht, 1)

                turn(0, 0, 1)
                over_slots(pe, step)

    def linear_attention():
        with ExitStack() as c:
            wq_sb = sb("wq_sb", [P, KC, D], c=c)
            wkv_sb = sb("wkv_sb", [P, KC, 2 * D], c=c)
            wo_sb = sb("wo_sb", [P, KC, D], c=c)
            bq_sb = sb("bq_sb", [P, KC], c=c)
            bk_sb = sb("bk_sb", [P, D], c=c)
            bv_sb = sb("bv2_sb", [P, D], c=c)
            bo_sb = sb("bo_sb", [P, D], c=c)
            decr = sb("decr", [P, SEQ], c=c)
            q_t = sb("q2_t", [P, KC, BATCH, SEQ], c=c)
            q_flat = q_t[:, :, :, :].rearrange("p c b n -> p c (b n)")
            k_sb = sb("k2_sb", [P, 2, D], c=c)
            kf = sb("kf", [P, 2, GT, D], c=c)
            v1 = sb("v1", [P, 2, GT, KC, VW], c=c)
            part = sb("part", [P, GROUPS, KC, VW], c=c)
            kv = sb("kv", [P, KC, VW], c=c)
            kvm = sb("kvm", [P, BATCH, KC, 2, P], c=c)
            den = xn_t
            o_t = sb("o2_t", [P, KC, GN], c=c)

            s_w = sem("b_weights", c)
            s_x = sem("b_x", c)
            s_ones = sem("b_ones", c)
            s_dve = sem("b_dve_steps", c)
            s_bo = sem("b_x_biased", c)
            s_rows = sem("b_rows", c)
            s_xt, s_xts = sem("b_xt_psum", c), sem("b_xt", c)
            s_kv, s_k, s_v = sem("b_kv_psum", c), sem("b_k", c), sem("b_v", c)
            s_kf = sem("b_kf", c)
            s_q, s_qs, s_qd = sem("b_q_psum", c), sem("b_q", c), sem("b_q_decayed", c)
            s_kvp, s_part = sem("b_part_psum", c), sem("b_part", c)
            s_kvm = sem("b_kv_masked", c)
            s_od, s_ot = sem("b_out_psum", c), sem("b_out", c)
            s_y, s_ys = sem("b_y_psum", c), sem("b_y", c)

            block = c.enter_context(nc.Block())

            @block.sync
            def _(sp):
                sp.dma_start(x_sb[:, 0:GT, :], tiled(acc1, 0, D)).then_inc(s_x, 16)
                with sp.Fori(1, GROUPS) as g:
                    sp.wait_ge(s_x, 16 * g)
                    sp.dma_start(x_sb[:, ds(g * GT, GT), :], tiled(acc1, g, D)).then_inc(s_x, 16)

            @block.scalar
            def _(act):
                for to, of in ((wkv_sb[:, :, 0:D], wk_t), (wkv_sb[:, :, D:2 * D], wv_t), (wq_sb[:, :, :], wq_t), (wo_sb[:, :, :], wo_t)):
                    act.dma_start(to, of.rearrange("(c p) n -> p c n", p=P)).then_inc(s_w, 16)
                act.dma_start(bq_sb[:, :], bq_cols).then_inc(s_w, 16)
                for to, of in ((bk_sb, b_k), (bv_sb, b_v), (bo_sb, b_o), (decr, dec_row)):
                    act.dma_start(to[:, :], of.partition_broadcast(P)).then_inc(s_w, 16)
                act.wait_ge(s_w, 16 * 9)

                def step(g, p):
                    static = isinstance(g, int)
                    if static and g == GROUPS:
                        return
                    if not static or g >= 1:
                        act.wait_ge(s_q, KC * g)
                    act.wait_ge(s_xt, g + 1)
                    for k in range(KC):
                        act.activation(xn_t[:, k, :], bank[k][:, :], ACT.Copy).then_inc(s_xts, 1)
                    if not static or g >= 2:
                        act.wait_ge(s_kvp, g - 1)
                    for t in range(GT):
                        act.wait_ge(s_k, GT * g + t + 1)
                        at = CONST_COLS["dec"][0]
                        tile = (g % (GROUPS // BATCH)) * GT + t if static else act_tile(g, t)
                        act.activation(kf[:, p, t, :], k_sb[:, t % 2, :], ACT.Relu,
                                       scale=cst[:, ds(at + tile, 1)]).then_inc(s_kf, 1)
                    for m in range(KC):
                        act.wait_ge(s_q, KC * g + m + 1)
                        act.activation(q_flat[:, m, ds(g * GN, GN)], bank[2 + m][:, :], ACT.Relu,
                                       bias=bq_sb[:, m:m + 1]).then_inc(s_qs, 1)

                def act_tile(g, t):
                    return (g % (GROUPS // BATCH)) * GT + t

                over_groups(act, step, 2)

            @block.gpsimd
            def _(pool):
                pool.memset(v1[:, :, :, :, P:VW], 1.0).then_inc(s_ones, 1)
                pool.wait_ge(s_w, 16 * 9)
                with pool.Fori(0, GROUPS) as g:
                    pool.wait_ge(s_rows, GT * g + GT)
                    pool.tensor_tensor(x_sb[:, ds(g * GT, GT), :], x_sb[:, ds(g * GT, GT), :],
                                       bo_sb[:, :].unsqueeze(1).to_broadcast([P, GT, D]), ALU.add).then_inc(s_bo, 1)

            @block.vector
            def _(dve):
                steps = Steps(dve, s_dve)
                dve.wait_ge(s_w, 16 * 9)
                dve.wait_ge(s_ones, 1)

                def front(g, p):
                    dve.wait_ge(s_x, 16 * g + 16)
                    if not isinstance(g, int) or g >= 2:
                        dve.wait_ge(s_xt, g - 1)
                    stats(dve, steps, lambda t: x_sb[:, ds(g * GT + t, 1), :])
                    normalise(dve, p, lambda t: x_sb[:, ds(g * GT + t, 1), :], s_rows)

                def step(g, p):
                    static = isinstance(g, int)
                    if static and g == 0:
                        front(0, 0)
                    if not static or g < GROUPS:
                        if not static or g >= 2:
                            dve.wait_ge(s_kvp, g - 1)
                        for t in range(GT):
                            dve.wait_ge(s_kv, GT * g + t + 1)
                            if not static or GT * g + t >= 2:
                                dve.wait_ge(s_kf, GT * g + t - 1)
                            b = bank[4 + t % 2]
                            dve.tensor_tensor(k_sb[:, t % 2, :], b[:, 0:D], bk_sb[:, :], ALU.add).then_inc(s_k, 1)
                            dve.tensor_tensor(v1[:, p, t, :, 0:P], b[:, D:2 * D].rearrange("p (c n) -> p c n", c=KC),
                                              bv_sb[:, :].rearrange("p (c n) -> p c n", c=KC), ALU.add).then_inc(s_v, 1)
                    if not static or g < GROUPS - 1:
                        front(g + 1, 1 - p)
                    if not static or g < GROUPS:
                        dve.wait_ge(s_qs, KC * g + KC)
                        at = (g % (GROUPS // BATCH)) * GN
                        q = q_flat[:, :, ds(g * GN, GN)]
                        dve.tensor_tensor(q, q, decr[:, ds(at, GN)].unsqueeze(1).to_broadcast([P, KC, GN]),
                                          ALU.mult).then_inc(s_qd, 1)
                    if not static or g >= 1:
                        for k in range(KC):
                            dve.wait_ge(s_kvp, g)
                            dve.tensor_copy(part[:, ds(g - 1, 1), k, :].rearrange("p a n -> p (a n)"), bank[6 + k][:, 0:VW]).then_inc(s_part, 1)

                over_groups(dve, step, 2, steps, STATS_STEPS)
                dve.wait_ge(s_part, KC * GROUPS)
                GB = GROUPS // BATCH
                block_mask = const("head_block").unsqueeze(1).to_broadcast([P, KC, P])
                for b in range(BATCH):
                    steps.chain(dve.tensor_tensor(kv[:, :, :], part[:, b * GB, :, :], part[:, b * GB + 1, :, :], ALU.add))
                    for a in range(2, GB):
                        steps.chain(dve.tensor_tensor(kv[:, :, :], kv[:, :, :], part[:, b * GB + a, :, :], ALU.add))
                    dve.tensor_tensor(kvm[:, b, :, 0, :], kv[:, :, 0:P], block_mask, ALU.mult).then_inc(s_kvm, 1)
                    steps.chain(dve.tensor_tensor(kvm[:, b, :, 1, :], kv[:, :, P:P + 1].to_broadcast([P, KC, P]), block_mask, ALU.mult))

                def divide(g):
                    for k in range(KC):
                        dve.wait_ge(s_od, KC * g + k + 1)
                        steps.chain(dve.tensor_scalar(den[:, k, :], bank[2 * k + 1][:, :], DEN_EPS, None, ALU.add))
                        steps.chain(dve.reciprocal(den[:, k, :], den[:, k, :]))
                        if k == 0 and (not isinstance(g, int) or g >= 1):
                            dve.wait_ge(s_y, 2 * g)
                        dve.tensor_tensor(o_t[:, k, :], bank[2 * k][:, :], den[:, k, :], ALU.mult).then_inc(s_ot, 1)

                def residual(g):
                    for h in range(2):
                        dve.wait_ge(s_y, 2 * g + h + 1)
                        xs = x_sb[:, ds(g * GT + 2 * h, 2), :]
                        dve.tensor_tensor(xs, bank[4 + h][:, :].rearrange("p (t n) -> p t n", t=2), xs, ALU.add).then_inc(s_ys, 1)

                dve.wait_ge(s_bo, GROUPS)
                divide(0)
                residual(0)
                start, per = steps.n, 2 * KC
                with dve.Fori(1, GROUPS) as g:
                    steps.base, steps.n = start + (g - 1) * per, 0
                    divide(g)
                    residual(g)

            @block.tensor
            def _(pe):
                pe.wait_ge(s_w, 16 * 9)

                def project(g, p):
                    static = isinstance(g, int)
                    pe.wait_ge(s_rows, GT * (g + 1))
                    transpose_rows(pe, p, bank[0:2], s_xt)
                    pe.wait_ge(s_xts, KC * (g + 1))
                    for t in range(GT):
                        if not static or GT * g + t >= 2:
                            pe.wait_ge(s_v, GT * g + t - 1)
                        for k in range(KC):
                            mm = pe.matmul(bank[4 + t % 2][:, :], xn_t[:, k, t * P:(t + 1) * P], wkv_sb[:, k, :],
                                           start=(k == 0), stop=(k == KC - 1))
                        mm.then_inc(s_kv, 1)
                    for m in range(KC):
                        if not static or g >= 1:
                            pe.wait_ge(s_qs, KC * (g - 1) + m + 1)
                        for k in range(KC):
                            mm = pe.matmul(bank[2 + m][:, :], wq_sb[:, k, m * P:(m + 1) * P], xn_t[:, k, :],
                                           start=(k == 0), stop=(k == KC - 1))
                        mm.then_inc(s_q, 1)

                def parts(g, p):
                    static = isinstance(g, int)
                    pe.wait_ge(s_kf, GT * (g + 1))
                    pe.wait_ge(s_v, GT * (g + 1))
                    if not static or g >= 1:
                        pe.wait_ge(s_part, KC * g)
                    for k in range(KC):
                        for t in range(GT):
                            mm = pe.matmul(bank[6 + k][:, 0:VW], kf[:, p, t, k * P:(k + 1) * P], v1[:, p, t, k, :],
                                           start=(t == 0), stop=(t == GT - 1))
                    mm.then_inc(s_kvp, 1)

                def step(g, p):
                    if not isinstance(g, int) or g < GROUPS:
                        project(g, p)
                    if not isinstance(g, int) or g >= 1:
                        parts(g - 1, 1 - p)

                over_groups(pe, step, 2)

                pe.wait_ge(s_kvm, BATCH)
                pe.wait_ge(s_dve, GROUPS * STATS_STEPS + BATCH * (GROUPS // BATCH))
                pe.wait_ge(s_qd, GROUPS)

                def outputs(g, b):
                    static = isinstance(g, int)
                    for k in range(KC):
                        if not static or g >= 1:
                            pe.wait_ge(s_ot, KC * (g - 1) + k + 1)
                        for a in range(2):
                            mm = pe.matmul(bank[2 * k + a][:, :], kvm[:, b, k, a, :], q_flat[:, k, ds(g * GN, GN)],
                                           start=True, stop=True)
                        mm.then_inc(s_od, 1)

                def mix(g):
                    static = isinstance(g, int)
                    pe.wait_ge(s_ot, KC * (g + 1))
                    for h in range(2):
                        if not static or g >= 1:
                            pe.wait_ge(s_ys, 2 * (g - 1) + h + 1)
                        for t in (2 * h, 2 * h + 1):
                            for k in range(KC):
                                mm = pe.matmul(bank[4 + h][:, (t % 2) * D:(t % 2 + 1) * D], o_t[:, k, t * P:(t + 1) * P],
                                               wo_sb[:, k, :], start=(k == 0), stop=(k == KC - 1))
                        mm.then_inc(s_y, 1)

                GB = GROUPS // BATCH
                outputs(0, 0)
                mix(0)
                for b in range(BATCH):
                    with pe.Fori(b * GB + (b == 0), (b + 1) * GB) as g:
                        outputs(g, b)
                        mix(g)

    attention()
    mixture(1, acc1)
    linear_attention()
    mixture(2, out)


def constants():
    import numpy as np
    p = np.arange(P)[:, None]
    i = np.arange(P)[None, :]
    scale = 1.0 / np.sqrt(D * SPAN)
    own = ((p <= i) & (i - p < SPAN)) * scale
    prev = (p > i[:, 0:SPAN] + P - SPAN) * scale
    prev = np.concatenate([prev * (g % (GROUPS // BATCH) != 0) for g in range(GROUPS)], axis=1)
    decay = np.exp(-(np.arange(SEQ) / SEQ))
    pair_tile = np.arange(PAIRS) % TILES
    parts = {
        "ident": p == i, "mask_own": own, "mask_prev": prev, "before": p < i, "ones": np.ones((P, P)),
        "dec": decay.reshape(SEQ // P, P).T, "rank_e": EXPERTS - np.arange(EXPERTS)[None, :] + 0 * p,
        "seg": (np.arange(EXPERTS * TILES) % TILES != 0)[None, :] + 0 * p, "iota": i + 0 * p,
        "token1": pair_tile[None, :] * P + p + 1, "spare1": TOKENS + 1 + p, "head_block": p // DK == i // DK,
    }
    table = np.zeros((P, CONST_W), np.float32)
    for name, a in parts.items():
        at, n = CONST_COLS[name]
        table[:, at:at + n] = a
    return table, decay.astype(np.float32)


def kernel(L0_attn_a_x, L0_attn_a_W_qkv, L0_attn_a_b_qkv, L0_attn_a_ln_w, L0_attn_a_ln_b, L0_attn_b_W_q, L0_attn_b_b_q,
           L0_attn_b_W_k, L0_attn_b_b_k, L0_attn_b_W_v, L0_attn_b_b_v, L0_attn_b_W_o, L0_attn_b_b_o, L0_ffn_Wg, L0_ffn_bg,
           L0_ffn_W1, L0_ffn_b1, L0_ffn_W2, L0_ffn_b2):
    import numpy as np
    import concourse.bacc as bacc
    from concourse.bass_utils import run_bass_kernel_spmd

    table, decay = constants()
    a = np.asarray
    arrays = {
        "x": a(L0_attn_a_x).reshape(TOKENS, D), "w_qkv": a(L0_attn_a_W_qkv), "bqkv_cols": a(L0_attn_a_b_qkv).reshape(3 * KC, P).T,
        "b_qkv": a(L0_attn_a_b_qkv),
        "ln_w": a(L0_attn_a_ln_w), "ln_b": a(L0_attn_a_ln_b),
        "wq_t": a(L0_attn_b_W_q).T, "bq_cols": a(L0_attn_b_b_q).reshape(KC, P).T, "wk_t": a(L0_attn_b_W_k).T, "b_k": a(L0_attn_b_b_k),
        "wv_t": a(L0_attn_b_W_v).T, "b_v": a(L0_attn_b_b_v), "wo_t": a(L0_attn_b_W_o).T, "b_o": a(L0_attn_b_b_o),
        "wg": a(L0_ffn_Wg), "bg": a(L0_ffn_bg), "w1": a(L0_ffn_W1), "b1": a(L0_ffn_b1), "w2": a(L0_ffn_W2),
        "b2": a(L0_ffn_b2), "consts": table, "dec_row": decay,
    }
    arrays = {n: np.ascontiguousarray(v) for n, v in arrays.items()}
    nc = bacc.Bacc("TRN2", target_bir_lowering=False, num_devices=1)
    args = [nc.dram_tensor(f"in_{n}", v.shape, mybir.dt.from_np(v.dtype), kind="ExternalInput").ap()
            for n, v in arrays.items()]
    out = nc.dram_tensor("out_x", (TOKENS + SPARE, D), F32, kind="ExternalOutput").ap()
    program(nc, *args, out)
    r = run_bass_kernel_spmd(nc, [{f"in_{n}": v for n, v in arrays.items()}], core_ids=[0])
    return np.asarray(r.results[0]["out_x"])[0:TOKENS].reshape(BATCH, SEQ, D)
```

```python
from contextlib import ExitStack

import concourse.bass as bass
from concourse import mybir

F32 = mybir.dt.float32
F32R = mybir.dt.float32r
BF16 = mybir.dt.bfloat16
I32 = mybir.dt.int32
U32 = mybir.dt.uint32
ALU = mybir.AluOpType
ACT = mybir.ActivationFunctionType
AX = mybir.AxisListType

P = 128
BATCH, SEQ, D = 2, 2048, 256
TOKENS = BATCH * SEQ
KC = D // P
TILES = TOKENS // P
GT = 4
GROUPS = TILES // GT
GN = GT * P
SPAN = 64
LN_EPS = 1e-5
EXPERTS, HID, TOPK = 8, 512, 2
HC = HID // P
TEMP = 5.0
GATE_EPS = 1e-9
ROW = D + EXPERTS
PAIRS = TILES * TOPK
SLOT_TILES = TOKENS * TOPK // P + EXPERTS - 1
SPARE = P
RING = 5
TURN = 2 * RING
assert (SLOT_TILES - 1) % TURN == 0
HEADS = 16
DK = D // HEADS
HG = HEADS // KC
NW = P + HG
DEN_EPS = 1e-6
VW = P + 2
RSQRT_MAGIC = 0x5F3759DF

CONST_COLS = {}


def _const_layout():
    at = 0
    for name, n in (("ident", P), ("mask_own", P), ("mask_prev", SPAN), ("mask_first", GROUPS * SPAN), ("before", P), ("ones", P),
                    ("dec", SEQ // P), ("rank_e", EXPERTS), ("seg", EXPERTS * TILES), ("iota", P),
                    ("tile1", PAIRS), ("place", 1), ("spare1", 1), ("head_block", P + HG)):
        CONST_COLS[name] = (at, n)
        at += n
    return at


CONST_W = _const_layout()


class Steps:

    def __init__(self, eng, sem):
        self.eng, self.sem, self.base, self.n = eng, sem, 0, 0

    def did(self, ins):
        ins.then_inc(self.sem, 1)
        self.n += 1

    def wait(self):
        self.eng.wait_ge(self.sem, self.base + self.n)

    def chain(self, ins):
        self.did(ins)
        self.wait()


def over_groups(eng, step, unroll, steps=None, per_step=0):
    assert (GROUPS - 2) % unroll == 0
    step(0, 0)
    start, per = (steps.n if steps else 0), per_step * unroll
    with eng.Fori(0, (GROUPS - 2) // unroll) as i:
        if steps:
            steps.base, steps.n = start + i * per, 0
        for u in range(unroll):
            step(unroll * i + (1 + u), (1 + u) % unroll)
        assert not steps or steps.n == per, (steps.n, per)
    if steps:
        steps.base, steps.n = 0, start + per_step * (GROUPS - 2)
    step(GROUPS - 1, (GROUPS - 1) % unroll)
    step(GROUPS, GROUPS % unroll)


def program(nc, x, w_qkv, bqkv_cols, b_qkv, ln_w, ln_b, wq_t, bq_cols, wk_t, b_k, wv_t, b_v, wo_t, b_o,
            wg, bg, w1, b1, w2, b2, consts, out):
    with ExitStack() as ctx:
        _program(nc, ctx, x, w_qkv, bqkv_cols, b_qkv, ln_w, ln_b, wq_t, bq_cols, wk_t, b_k, wv_t, b_v, wo_t, b_o,
                 wg, bg, w1, b1, w2, b2, consts, out)


def _program(nc, ctx, x, w_qkv, bqkv_cols, b_qkv, ln_w, ln_b, wq_t, bq_cols, wk_t, b_k, wv_t, b_v, wo_t, b_o,
             wg, bg, w1, b1, w2, b2, consts, out):
    ds = bass.ds

    def sb(name, shape, dt=F32, c=ctx):
        return c.enter_context(nc.sbuf_tensor(name, shape, dt))

    def sem(name):
        return nc.alloc_semaphore(name=name)

    bank = [ctx.enter_context(nc.psum_tensor(f"bank{i}", [P, 512], F32)) for i in range(8)]

    w1_hi = sb("w1_hi", [P, EXPERTS, KC, HID], F32R)
    w2_hi = sb("w2_hi", [P, EXPERTS, HC, D], F32R)
    wg_sb = sb("wg_sb", [P, KC, EXPERTS])
    bg_sb = sb("bg_sb", [P, EXPERTS])
    cst = sb("cst", [P, CONST_W])
    st = sb("st", [P, 2 * GT, 6])
    st_x = sb("st_x", [P, TILES, 6])
    mean = sb("mean", [P, TILES])
    var = sb("var", [P, TILES])
    half = sb("half", [P, TILES], I32)
    rs = sb("rs", [P, TILES])
    ra = sb("ra", [P, TILES])
    rb = sb("rb", [P, TILES])

    def const(name):
        at, n = CONST_COLS[name]
        return cst[:, at:at + n]

    ident = const("ident")

    table = nc.dram_tensor("row_table", [TOKENS + SPARE, ROW], F32).ap()
    acc1 = nc.dram_tensor("sum_1", [TOKENS + SPARE, D], F32).ap()

    def tiled(dram, g, width):
        return dram[ds(g * GN, GN), :].rearrange("(t p) n -> p t n", p=P) if not isinstance(g, int) else \
            dram[g * GN:(g + 1) * GN, :].rearrange("(t p) n -> p t n", p=P)

    def moments(eng, steps, n, of=None, between=()):
        of = of or st
        between = list(between)

        def pause():
            if between:
                between.pop(0)()

        v, m, r, a, b, h = (t[:, 0:n] for t in (var, mean, rs, ra, rb, half))
        mean_even, m2_even, mean_odd, m2_odd = (of[:, 0:n, i] for i in (1, 2, 4, 5))
        steps.did(eng.tensor_tensor(a, mean_even, mean_odd, ALU.add))
        steps.did(eng.tensor_tensor(b, mean_even, mean_odd, ALU.subtract))
        steps.did(eng.tensor_tensor(v, m2_even, m2_odd, ALU.add))
        steps.wait()
        steps.did(eng.tensor_scalar(m, a, 0.5, None, ALU.mult))
        steps.did(eng.tensor_scalar(v, v, 1.0 / D, LN_EPS, ALU.mult, ALU.add))
        steps.chain(eng.scalar_tensor_tensor(r, b, 0.25, b, ALU.mult, ALU.mult))
        steps.chain(eng.tensor_tensor(v, v, r, ALU.add))
        steps.chain(eng.tensor_scalar(h, v.bitcast(I32), 1, None, ALU.logical_shift_right))
        steps.chain(eng.tensor_scalar(r.bitcast(I32), h, -1.0, float(RSQRT_MAGIC), ALU.mult, ALU.add))
        for _ in range(3):
            pause()
            steps.chain(eng.scalar_tensor_tensor(a, r, -0.5, r, ALU.mult, ALU.mult))
            pause()
            steps.chain(eng.tensor_tensor(b, a, v, ALU.mult))
            steps.chain(eng.scalar_tensor_tensor(r, b, 1.5, r, ALU.add, ALU.mult))
        for rest in between:
            rest()

    MOMENT_STEPS = 18

    def measure(eng, steps, source, at=0):
        for t in range(GT):
            steps.did(eng.bn_stats(st[:, at + t, :], source(t)))

    def tile_of(x_sb, g, t):
        return x_sb[:, ds(g * GT + t, 1), :].rearrange("p a n -> p (a n)")

    def measure_x_tile(eng, x_sb, g, t, done):
        eng.bn_stats(st_x[:, ds(g * GT + t, 1), :].rearrange("p a n -> p (a n)"), tile_of(x_sb, g, t)).then_inc(done, 1)

    def measure_x(eng, x_sb, g, done):
        for t in range(GT):
            measure_x_tile(eng, x_sb, g, t, done)

    def normalise(eng, rows, p, source, done, at=0):
        for t in range(GT):
            to = rows[:, p, t, :] if isinstance(p, int) else \
                rows[:, ds(p, 1), t, :].rearrange("p a n -> p (a n)")
            eng.tensor_scalar(to, source(t), mean[:, ds(at + t, 1)], rs[:, ds(at + t, 1)],
                              ALU.subtract, ALU.mult).then_inc(done, 1)

    def transpose_rows(eng, rows, p, banks, done):
        for c in range(KC):
            for t in range(GT):
                mm = eng.transpose(banks[c][:, t * P:(t + 1) * P], rows[:, p, t, c * P:(c + 1) * P], ident)
        mm.then_inc(done, 1)

    PIECE = KC * HID

    def of_expert(w, e):
        return w[:, ds(e, 1), :, :].rearrange("p a c n -> p (a c n)")

    def stage_weights(eng, stage, p, w, e, done):
        chunks = w.shape[1] // P
        eng.dma_start(stage[:, p, :].rearrange("p (c n) -> p c n", c=chunks),
                      w[ds(e, 1), :, :].rearrange("a (c p) n -> p (a c) n", p=P)).then_inc(done, 16)

    def multiply(pe, to, hi, lo, w_hi, w_lo, chunks, lo_is_ready, done):
        for k in range(chunks):
            pe.matmul(to, hi(k), w_hi(k), start=(k == 0), stop=False)
        for k in range(chunks):
            pe.matmul(to, hi(k), w_lo(k), start=False, stop=False)
        lo_is_ready()
        for k in range(chunks):
            mm = pe.matmul(to, lo(k), w_hi(k), start=False, stop=(k == chunks - 1))
        if done:
            mm.then_inc(done, 1)

    def attention():
        with ExitStack() as c:
            x_sb = sb("a_x_sb", [P, TILES, D], c=c)
            rows = sb("a_rows_sb", [P, 3, GT, D], c=c)
            xn_hi, xn_lo = (sb(f"a_xn_{part}", [P, KC, GN], F32R, c=c) for part in ("hi", "lo"))
            w_hi, w_lo = (sb(f"a_w_{part}", [P, KC, 3 * D], F32R, c=c) for part in ("hi", "lo"))
            stage = sb("a_stage", [P, 2, PIECE], c=c)
            w_sb = sb("wqkv_sb", [P, KC, 3 * D], c=c)
            bqk = sb("bqk", [P, 2 * KC], c=c)
            bv_sb = sb("bv_sb", [P, D], c=c)
            lw = sb("lw", [P, D], c=c)
            lb = sb("lb", [P, D], c=c)
            q_t = sb("q_t", [P, 3, KC, GN], c=c)
            k_t = sb("k_t", [P, 3, KC, GN], c=c)
            v_sb = sb("v_sb", [P, 3, GT, D], c=c)
            sc = sb("sc", [P, 2, 2 * P], c=c)
            o_sb = sb("o_sb", [P, 2, GT, D], c=c)
            n_sb = sb("n_sb", [P, GT, D], c=c)
            zeros = sb("zeros", [P, ROW], c=c)

            s_x0, s_x1, s_x2 = (sem(f"a_x{i}") for i in range(3))
            s_w = sem("a_weights")
            s_stage = [sem(f"a_staged{p}") for p in range(2)]
            s_hi = sem("a_weights_rounded")
            s_zero = sem("a_zeroed")
            s_z = sem("a_zeros_out")
            s_dve = sem("a_dve_steps")
            s_rows = sem("a_rows")
            s_whi, s_wlo = sem("a_w_hi_ready"), sem("a_w_lo_ready")
            s_xt, s_xhi, s_xlo = sem("a_xt_psum"), sem("a_xn_hi_ready"), sem("a_xn_lo_ready")
            s_qk, s_qks = sem("a_qk_psum"), sem("a_qk")
            s_v, s_va, s_vs = sem("a_v_psum"), sem("a_v_copied"), sem("a_v")
            s_s, s_ss = sem("a_scores_psum"), sem("a_scores")
            s_o, s_os = sem("a_out_psum"), sem("a_out")
            s_xout = sem("a_x_out")
            s_st = sem("a_x_statistics")
            s_n = sem("a_out_used")
            s_xb = sem("a_x_and_bias")
            s_res = sem("a_residual")

            block = c.enter_context(nc.Block())

            @block.sync
            def _(sp):
                sp.dma_start(x_sb[:, 0:GT, :], tiled(x, 0, D)).then_inc(s_x0, 16)
                sp.dma_start(cst[:, :], consts).then_inc(s_w, 16)
                sp.dma_start(w_sb[:, :, :], w_qkv.rearrange("(c p) n -> p c n", p=P)).then_inc(s_w, 16)
                sp.dma_start(x_sb[:, GT:2 * GT, :], tiled(x, 1, D)).then_inc(s_x1, 16)
                sp.wait_ge(s_w, 16 * 8)
                for g in range(2, GROUPS):
                    sp.dma_start(x_sb[:, g * GT:(g + 1) * GT, :], tiled(x, g, D)).then_inc(s_x2, 16)
                stage_weights(sp, stage, 0, w1, 0, s_stage[0])
                stage_weights(sp, stage, 1, w2, 0, s_stage[1])
                with sp.Fori(1, EXPERTS) as e:
                    for p, w in ((0, w1), (1, w2)):
                        sp.wait_ge(s_hi, 2 * e + p - 1)
                        stage_weights(sp, stage, p, w, e, s_stage[p])
                sp.wait_ge(s_zero, 4)
                sp.dma_start(table[TOKENS:TOKENS + SPARE, :], zeros[:, :]).then_inc(s_z, 16)
                sp.dma_start(acc1[TOKENS:TOKENS + SPARE, :], zeros[:, 0:D]).then_inc(s_z, 16)
                sp.dma_start(out[TOKENS:TOKENS + SPARE, :], zeros[:, 0:D]).then_inc(s_z, 16)
                with sp.Fori(0, GROUPS) as g:
                    sp.wait_ge(s_res, 2 * g + 2)
                    sp.dma_start(tiled(acc1, g, D), x_sb[:, ds(g * GT, GT), :]).then_inc(s_xout, 16)
                sp.wait_ge(s_xout, 16 * GROUPS)
                sp.wait_ge(s_z, 48)

            def o_tile(g, t):
                return o_sb[:, ds(g % 2, 1), t, :].rearrange("p a n -> p (a n)")

            def evacuate_q_k(act, g, p):
                if not isinstance(g, int) or g >= 2:
                    act.wait_ge(s_s, GT * (g - 1))
                for m in range(2 * KC):
                    act.wait_ge(s_qk, 2 * KC * g + m + 1)
                    to = (q_t if m < KC else k_t)[:, p, m % KC, :]
                    act.activation(to, bank[2 + m % 2][:, :], ACT.Identity, bias=bqk[:, m:m + 1]).then_inc(s_qks, 1)

            @block.scalar
            def _(act):
                act.dma_start(bqk[:, :], bqkv_cols[:, 0:2 * KC]).then_inc(s_w, 16)
                act.dma_start(bv_sb[:, :], b_qkv[2 * D:3 * D].partition_broadcast(P)).then_inc(s_w, 16)
                act.dma_start(lw[:, :], ln_w.partition_broadcast(P)).then_inc(s_w, 16)
                act.dma_start(lb[:, :], ln_b.partition_broadcast(P)).then_inc(s_w, 16)
                act.dma_start(wg_sb[:, :, :], wg.rearrange("(c p) n -> p c n", p=P)).then_inc(s_w, 16)
                act.dma_start(bg_sb[:, :], bg.partition_broadcast(P)).then_inc(s_w, 16)
                act.wait_ge(s_w, 16 * 8)

                def copy_rows(g):
                    if not isinstance(g, int) or g >= 1:
                        act.wait_ge(s_v, 2 * g)
                    act.wait_ge(s_xt, g + 1)
                    for k in range(KC):
                        act.activation(xn_hi[:, k, :], bank[2 + k][:, :], ACT.Copy).then_inc(s_xhi, 1)

                def round_weights(e):
                    for q, hi in ((0, w1_hi), (1, w2_hi)):
                        act.wait_ge(s_stage[q], 16 * e + 16)
                        act.activation(of_expert(hi, e), stage[:, q, :], ACT.Copy).then_inc(s_hi, 1)

                assert EXPERTS == GROUPS

                def step(g, p):
                    if not isinstance(g, int) or g < GROUPS:
                        evacuate_q_k(act, g, p)
                        if not isinstance(g, int) or g >= 2:
                            act.wait_ge(s_o, GT * (g - 1))
                        for h in range(2):
                            act.wait_ge(s_v, 2 * g + h + 1)
                            act.activation(v_sb[:, p, 2 * h:2 * h + 2, :], bank[4 + h][:, :].rearrange("p (t n) -> p t n", t=2),
                                           ACT.Copy).then_inc(s_va, 1)
                    if not isinstance(g, int) or g < GROUPS - 1:
                        copy_rows(g + 1)
                    if not isinstance(g, int) or g < GROUPS:
                        round_weights(g)
                    if not isinstance(g, int) or g >= 1:
                        act.wait_ge(s_n, GT * g)
                        for t in range(GT):
                            act.wait_ge(s_o, GT * (g - 1) + t + 1)
                            act.activation(o_tile(g - 1, t), bank[6 + t % 2][:, 0:D], ACT.Copy).then_inc(s_os, 1)

                act.activation(w_hi[:, :, :], w_sb[:, :, :], ACT.Copy).then_inc(s_whi, 1)
                copy_rows(0)
                over_groups(act, step, 3)

            @block.vector
            def _(dve):
                steps = Steps(dve, s_dve)
                dve.memset(sc[:, :, P + SPAN:2 * P], 0.0).then_inc(s_zero, 1)
                dve.memset(k_t[:, 2, :, GN - P:GN], 0.0).then_inc(s_zero, 1)
                dve.memset(v_sb[:, 2, GT - 1, :], 0.0).then_inc(s_zero, 1)
                dve.memset(zeros[:, :], 0.0).then_inc(s_zero, 1)
                dve.memset(o_sb[:, :, 0, 0:1], 0.0).then_inc(s_n, 2 * GT)

                def x_rows(g):
                    return lambda t: tile_of(x_sb, g, t)

                def front(g, at=0):
                    if not isinstance(g, int) or g >= 3:
                        dve.wait_ge(s_xt, g - 2)
                    normalise(dve, rows, g % 3, x_rows(g), s_rows, at)

                def out_rows(g, at):
                    if not isinstance(g, int) or g >= 1:
                        dve.wait_ge(s_res, 2 * g)
                    for t in range(GT):
                        dve.tensor_scalar(n_sb[:, t, :], o_tile(g, t), mean[:, at + t:at + t + 1], rs[:, at + t:at + t + 1],
                                          ALU.subtract, ALU.mult).then_inc(s_n, 1)

                def left(g):
                    for k in range(KC):
                        dve.wait_ge(s_xhi, KC * g + k + 1)
                        dve.tensor_tensor(xn_lo[:, k, :], bank[2 + k][:, :], xn_hi[:, k, :].bitcast(F32),
                                          ALU.subtract).then_inc(s_xlo, 1)

                def masked(g, t):
                    dve.wait_ge(s_s, GT * g + t + 1)
                    if t:
                        at = CONST_COLS["mask_own"][0]
                        dve.tensor_tensor(sc[:, t % 2, 0:P + SPAN], bank[t % 2][:, 0:P + SPAN],
                                          cst[:, at:at + P + SPAN], ALU.mult).then_inc(s_ss, 2)
                        return
                    dve.tensor_tensor(sc[:, t % 2, 0:P], bank[t % 2][:, 0:P], const("mask_own"),
                                      ALU.mult).then_inc(s_ss, 1)
                    at = CONST_COLS["mask_first"][0]
                    dve.tensor_tensor(sc[:, t % 2, P:P + SPAN], bank[t % 2][:, P:P + SPAN],
                                      cst[:, ds(at + g * SPAN, SPAN)], ALU.mult).then_inc(s_ss, 1)

                def step(g):
                    static = isinstance(g, int)
                    more = not static or g < GROUPS - 1
                    out = not static or 2 <= g < GROUPS + 2
                    if out:
                        dve.wait_ge(s_os, GT * (g - 1))
                        measure(dve, steps, lambda t: o_tile(g - 2, t), GT if more else 0)
                    if more or out:
                        steps.wait()
                        moments(dve, steps, GT * (more + out))
                    if more:
                        front(g + 1)
                    if out:
                        out_rows(g - 2, GT if more else 0)
                    if not static or 1 <= g <= GROUPS:
                        for t in range(2):
                            masked(g - 1, t)
                    if more:
                        left(g + 1)
                    if not static or 1 <= g <= GROUPS:
                        masked(g - 1, 2)
                    if not static or g < GROUPS - 2:
                        if static and g == 0:
                            dve.wait_ge(s_x2, 16 * (GROUPS - 2))
                        measure(dve, steps, x_rows(g + 2))
                    if not static or 1 <= g <= GROUPS:
                        masked(g - 1, 3)
                    if not static or g >= 3:
                        dve.wait_ge(s_res, 2 * (g - 2))
                        measure_x(dve, x_sb, g - 3, s_st)

                dve.wait_ge(s_x0, 16)
                measure(dve, steps, x_rows(0))
                steps.wait()
                moments(dve, steps, GT)
                front(0)
                dve.wait_ge(s_x1, 16)
                dve.wait_ge(s_w, 16 * 8)
                dve.wait_ge(s_whi, 1)
                dve.tensor_tensor(w_lo[:, :, :], w_sb[:, :, :], w_hi[:, :, :].bitcast(F32), ALU.subtract).then_inc(s_wlo, 1)
                left(0)
                measure(dve, steps, x_rows(1))
                step(0)
                step(1)
                start, per = steps.n, 2 * GT + MOMENT_STEPS
                step(2)
                with dve.Fori(3, GROUPS - 2) as g:
                    steps.base, steps.n = start + (g - 2) * per, 0
                    step(g)
                    assert steps.n == per
                steps.base, steps.n = 0, start + (GROUPS - 4) * per
                for g in range(GROUPS - 2, GROUPS + 3):
                    step(g)
                dve.wait_ge(s_st, TILES)

            @block.gpsimd
            def _(pool):
                pool.wait_ge(s_w, 16 * 8)

                def biases(g):
                    pool.wait_ge(s_rows, GT * g + GT)
                    x_g = x_sb[:, ds(g * GT, GT), :]
                    pool.tensor_tensor(x_g, x_g, lb[:, :].unsqueeze(1).to_broadcast([P, GT, D]), ALU.add).then_inc(s_xb, 1)
                    pool.wait_ge(s_va, 2 * g + 2)
                    v_g = v_sb[:, ds(g % 3, 1), :, :].rearrange("p a t n -> p (a t) n")
                    pool.tensor_tensor(v_g, v_g, bv_sb[:, :].unsqueeze(1).to_broadcast([P, GT, D]), ALU.add).then_inc(s_vs, 2)

                def residual(g):
                    pool.wait_ge(s_n, 2 * GT + GT * g + GT)
                    pool.tensor_tensor(n_sb[:, :, :], n_sb[:, :, :], lw[:, :].unsqueeze(1).to_broadcast([P, GT, D]),
                                       ALU.mult).then_inc(s_res, 1)
                    pool.wait_ge(s_res, 2 * g + 1)
                    pool.wait_ge(s_xb, g + 1)
                    x_g = x_sb[:, ds(g * GT, GT), :]
                    pool.tensor_tensor(x_g, x_g, n_sb[:, :, :], ALU.add).then_inc(s_res, 1)

                biases(0)
                biases(1)
                with pool.Fori(2, GROUPS) as g:
                    residual(g - 2)
                    biases(g)
                residual(GROUPS - 2)
                residual(GROUPS - 1)

            @block.tensor
            def _(pe):
                pe.wait_ge(s_w, 16 * 8)
                pe.wait_ge(s_zero, 3)

                def turn(g, p):
                    pe.wait_ge(s_rows, GT * (g + 1))
                    if not isinstance(g, int) or g >= 1:
                        pe.wait_ge(s_qks, 2 * KC * g)
                    transpose_rows(pe, rows, p, bank[2:4], s_xt)

                def nothing():
                    pass

                def project(g, p):
                    pe.wait_ge(s_xhi, KC * (g + 1))
                    pe.wait_ge(s_xlo, KC * (g + 1))
                    for m in range(2 * KC):
                        if m >= 2:
                            pe.wait_ge(s_qks, 2 * KC * g + m - 1)
                        cols = slice(m * P, (m + 1) * P)
                        multiply(pe, bank[2 + m % 2][:, :], lambda k: w_hi[:, k, cols], lambda k: w_lo[:, k, cols],
                                 lambda k: xn_hi[:, k, :], lambda k: xn_lo[:, k, :], KC, nothing, s_qk)
                    for h in range(2):
                        if not isinstance(g, int) or g >= 1:
                            pe.wait_ge(s_va, 2 * g + h - 1)
                        for t in (2 * h, 2 * h + 1):
                            rows_t = slice(t * P, (t + 1) * P)
                            multiply(pe, bank[4 + h][:, (t % 2) * D:(t % 2 + 1) * D],
                                     lambda k: xn_hi[:, k, rows_t], lambda k: xn_lo[:, k, rows_t],
                                     lambda k: w_hi[:, k, 2 * D:3 * D], lambda k: w_lo[:, k, 2 * D:3 * D], KC, nothing,
                                     s_v if t % 2 else None)

                def before(p, t):
                    return (p, t - 1) if t else ((p - 1) % 3, GT - 1)

                def scores(p, t):
                    for k in range(KC):
                        pe.matmul(bank[t % 2][:, 0:P], k_t[:, p, k, t * P:(t + 1) * P],
                                  q_t[:, p, k, t * P:(t + 1) * P], start=(k == 0), stop=(k == KC - 1))
                    pb, tb = before(p, t)
                    for k in range(KC):
                        mm = pe.matmul(bank[t % 2][:, P:P + SPAN], k_t[:, pb, k, tb * P:(tb + 1) * P],
                                       q_t[:, p, k, t * P:t * P + SPAN], start=(k == 0), stop=(k == KC - 1))
                    mm.then_inc(s_s, 1)

                def values(g, p, t):
                    pe.wait_ge(s_ss, 2 * (GT * g + t + 1))
                    if not isinstance(g, int) or GT * g + t >= 2:
                        pe.wait_ge(s_os, GT * g + t - 1 if t >= 2 else GT * g)
                    pb, tb = before(p, t)
                    pe.matmul(bank[6 + t % 2][:, 0:D], sc[:, t % 2, 0:P], v_sb[:, p, t, :], start=True, stop=False)
                    pe.matmul(bank[6 + t % 2][:, 0:D], sc[:, t % 2, P:2 * P], v_sb[:, pb, tb, :],
                              start=False, stop=True).then_inc(s_o, 1)

                def attend(g, p):
                    pe.wait_ge(s_qks, 2 * KC * (g + 1))
                    pe.wait_ge(s_vs, 2 * (g + 1))
                    scores(p, 0)
                    for t in range(1, GT):
                        scores(p, t)
                        values(g, p, t - 1)
                    values(g, p, GT - 1)

                def step(g, p):
                    if not isinstance(g, int) or g < GROUPS:
                        project(g, p)
                    if not isinstance(g, int) or g < GROUPS - 1:
                        turn(g + 1, (p + 1) % 3)
                    if not isinstance(g, int) or g >= 1:
                        attend(g - 1, (p - 1) % 3)

                turn(0, 0)
                pe.wait_ge(s_wlo, 1)
                over_groups(pe, step, 3)

    def mixture(n, total):
        with ExitStack() as c:
            b1_sb = sb(f"m{n}_b1", [P, EXPERTS, HID], c=c)
            b2_sb = sb(f"m{n}_b2", [P, EXPERTS, D], c=c)
            w1_lo = sb(f"m{n}_w1_lo", [P, EXPERTS, KC, HID], F32R, c=c)
            w2_lo = sb(f"m{n}_w2_lo", [P, EXPERTS, HC, D], F32R, c=c)
            idx = sb(f"m{n}_idx", [P, SLOT_TILES + 1], U32, c=c)
            expert = sb(f"m{n}_expert", [P, SLOT_TILES + 1], I32, c=c)
            with ExitStack() as c2:
                stage = sb(f"m{n}_stage", [P, 2, PIECE], c=c2)
                logit = sb(f"m{n}_logit", [P, TILES, EXPERTS], c=c2)
                mixture_rows(n, total, stage, w1_lo, logit)
                mixture_slots(n, logit, stage, w2_lo, b1_sb, b2_sb, idx, expert)
            mixture_experts(n, total, w1_lo, w2_lo, b1_sb, b2_sb, idx, expert)

    def left_by_rounding(eng, stage, w_lo, w_hi, s_stage, s_lo):
        with eng.Fori(0, EXPERTS // 2) as i:
            for p in range(2):
                eng.wait_ge(s_stage[p], 16 * i + 16)
                eng.tensor_tensor(of_expert(w_lo, 2 * i + p), stage[:, p, :], of_expert(w_hi, 2 * i + p).bitcast(F32),
                                  ALU.subtract).then_inc(s_lo, 1)

    def mixture_rows(n, x_dram, stage, w1_lo, logit):
        with ExitStack() as c:
            x_in = sb(f"m{n}_x_in", [P, 2, GT, D], c=c)
            rows = sb(f"m{n}_rows_sb", [P, 2, GT, D], c=c)
            turned = [sb(f"m{n}_turned{p}", [P, KC, GN], c=c) for p in range(2)]
            s_dve = sem(f"m{n}_dve_steps")
            s_x = [sem(f"m{n}_x{p}") for p in range(2)]
            s_rows = sem(f"m{n}_rows")
            s_xt, s_xts = sem(f"m{n}_xt_psum"), sem(f"m{n}_xt")
            lt_sb = sb(f"m{n}_logits_t", [EXPERTS, 2, GN], c=c)
            s_ltp, s_lt = sem(f"m{n}_logits_t_psum"), sem(f"m{n}_logits_t_ready")
            s_lg, s_lgs = sem(f"m{n}_logits_psum"), sem(f"m{n}_logits")
            s_out = [sem(f"m{n}_rows_out{p}") for p in range(2)]
            s_stage = [sem(f"m{n}_w1_staged{p}") for p in range(2)]
            s_lo = sem(f"m{n}_w1_left")

            block = c.enter_context(nc.Block())

            @block.sync
            def _(sp):
                def load(g, p):
                    sp.dma_start(x_in[:, p, :, :], tiled(x_dram, g, D)).then_inc(s_x[p], 16)

                def store(g, p):
                    sp.wait_ge(s_rows, GT * g + GT)
                    sp.dma_start(tiled(table, g, ROW)[:, :, 0:D], rows[:, p, :, :]).then_inc(s_out[p], 16)

                for p in range(2):
                    load(p, p)
                for p in range(2):
                    stage_weights(sp, stage, p, w1, p, s_stage[p])
                with sp.Fori(0, GROUPS // 2 - 1) as i:
                    for p in range(2):
                        store(2 * i + p, p)
                        load(2 * i + p + 2, p)
                        sp.wait_ge(s_lo, 2 * i + p + 1)
                        stage_weights(sp, stage, p, w1, 2 * i + p + 2, s_stage[p])
                for p in range(2):
                    store(GROUPS - 2 + p, p)
                for p in range(2):
                    sp.wait_ge(s_out[p], 16 * GROUPS // 2)

            @block.gpsimd
            def _(pool):
                left_by_rounding(pool, stage, w1_lo, w1_hi, s_stage, s_lo)

            @block.scalar
            def _(act):
                def copy_rows(g, p):
                    if not isinstance(g, int) or g >= 2:
                        act.wait_ge(s_ltp, g - 1)
                    act.wait_ge(s_xt, g + 1)
                    for k in range(KC):
                        act.activation(turned[p][:, k, :], bank[4 + 2 * p + k][:, :], ACT.Copy).then_inc(s_xts, 1)

                def copy_logits(g, p):
                    act.wait_ge(s_ltp, g + 1)
                    act.activation(lt_sb[:, p, :], bank[2 + p][0:EXPERTS, :], ACT.Copy).then_inc(s_lt, 1)

                def keep_logits(g, p):
                    act.wait_ge(s_lg, g + 1)
                    act.activation(logit[:, ds(g * GT, GT), :], bank[p][:, 0:GT * EXPERTS].rearrange("p (t e) -> p t e", t=GT),
                                   ACT.Copy).then_inc(s_lgs, 1)

                copy_rows(0, 0)
                copy_rows(1, 1)
                copy_logits(0, 0)
                with act.Fori(1, GROUPS // 2) as i:
                    copy_rows(2 * i, 0)
                    copy_logits(2 * i - 1, 1)
                    keep_logits(2 * i - 2, 0)
                    copy_rows(2 * i + 1, 1)
                    copy_logits(2 * i, 0)
                    keep_logits(2 * i - 1, 1)
                copy_logits(GROUPS - 1, 1)
                keep_logits(GROUPS - 2, 0)
                keep_logits(GROUPS - 1, 1)

            @block.vector
            def _(dve):
                moments(dve, Steps(dve, s_dve), TILES, of=st_x)

                def row_step(g, p, filled):
                    dve.wait_ge(s_x[p], 16 * filled)
                    normalise(dve, rows, p, lambda t: x_in[:, p, t, :], s_rows, g * GT)

                row_step(0, 0, 1)
                row_step(1, 1, 1)
                with dve.Fori(1, GROUPS // 2) as i:
                    for p in range(2):
                        dve.wait_ge(s_out[p], 16 * i)
                        dve.wait_ge(s_xt, 2 * i + p - 1)
                        row_step(2 * i + p, p, i + 1)

            @block.tensor
            def _(pe):
                def logits(g, p):
                    pe.wait_ge(s_xts, KC * (g + 1))
                    if not isinstance(g, int) or g >= 1:
                        pe.wait_ge(s_lt, g)
                    for k in range(KC):
                        mm = pe.matmul(bank[2 + p][0:EXPERTS, :], wg_sb[:, k, :], turned[p][:, k, :],
                                       start=(k == 0), stop=(k == KC - 1))
                    mm.then_inc(s_ltp, 1)

                def turn_logits(g, p):
                    for t in range(GT):
                        mm = pe.transpose(bank[p][:, t * EXPERTS:(t + 1) * EXPERTS], lt_sb[:, p, t * P:(t + 1) * P],
                                          ident[0:EXPERTS, 0:EXPERTS])
                    mm.then_inc(s_lg, 1)

                def turn_rows(g, p):
                    pe.wait_ge(s_rows, GT * (g + 1))
                    if not isinstance(g, int) or g >= 2:
                        pe.wait_ge(s_xts, KC * (g - 1))
                    transpose_rows(pe, rows, p, bank[4 + 2 * p:6 + 2 * p], s_xt)

                turn_rows(0, 0)
                turn_rows(1, 1)
                logits(0, 0)
                with pe.Fori(1, GROUPS // 2) as i:
                    turn_rows(2 * i, 0)
                    logits(2 * i - 1, 1)
                    turn_logits(2 * i - 2, 0)
                    turn_rows(2 * i + 1, 1)
                    logits(2 * i, 0)
                    turn_logits(2 * i - 1, 1)
                logits(GROUPS - 1, 1)
                turn_logits(GROUPS - 2, 0)
                pe.wait_ge(s_lt, GROUPS)
                turn_logits(GROUPS - 1, 1)

    def mixture_slots(n, logit, stage, w2_lo, b1_sb, b2_sb, idx, expert):
        NS1 = SLOT_TILES + 1
        PART = PAIRS // 4
        with ExitStack() as c:
            prob = sb(f"m{n}_prob", [P, TILES, EXPERTS], c=c)
            tmp = sb(f"m{n}_tmp", [P, TILES, EXPERTS], c=c)
            col = sb(f"m{n}_col", [P, 8, TILES], c=c)
            first = sb(f"m{n}_first", [P, TILES, EXPERTS], c=c)
            second = sb(f"m{n}_second", [P, TILES, EXPERTS], c=c)
            either = sb(f"m{n}_either", [P, TILES, EXPERTS], BF16, c=c)
            cb = sb(f"m{n}_cb", [P, 2 * P], BF16, c=c)
            tot = sb(f"m{n}_tot", [P, EXPERTS, TILES], c=c)
            inc = sb(f"m{n}_inc", [P, EXPERTS, TILES], c=c)
            pos = sb(f"m{n}_pos", [P, TILES, EXPERTS], c=c)
            e8 = sb(f"m{n}_e8", [P, 4, EXPERTS], c=c)
            e8i = sb(f"m{n}_e8i", [P, 2, EXPERTS], I32, c=c)
            slot = sb(f"m{n}_slot", [P, 3, PAIRS], c=c)
            sloti = sb(f"m{n}_sloti", [P, 3, PAIRS], I32, c=c)
            in_tile = sb(f"m{n}_in_tile", [P, 2, PART, P], BF16, c=c)
            in_slot_tile = sb(f"m{n}_in_slot_tile", [P, 2, PART, NS1], BF16, c=c)
            of_tile = sb(f"m{n}_of_tile", [P, 2, PART, 2, NS1], BF16, c=c)
            tile_e = sb(f"m{n}_tile_e", [P, NS1, EXPERTS], c=c)
            idxf = sb(f"m{n}_idxf", [P, 2, NS1], c=c)
            s_dve = sem(f"m{n}_slot_steps")
            s_either = sem(f"m{n}_chosen")
            s_gates = sem(f"m{n}_gates")
            s_mx, s_ex = sem(f"m{n}_shifted"), sem(f"m{n}_exp")
            s_gout = sem(f"m{n}_gates_out")
            s_bias = sem(f"m{n}_biases")
            s_base = sem(f"m{n}_onehot_of_tile")
            s_oft, s_ofp = sem(f"m{n}_tile_values"), sem(f"m{n}_place_values")
            s_cnt, s_onehot, s_inv = sem(f"m{n}_counted"), sem(f"m{n}_onehot"), sem(f"m{n}_tokens")
            s_idx = sem(f"m{n}_indices")
            s_stage = [sem(f"m{n}_w2_staged{p}") for p in range(2)]
            s_lo = sem(f"m{n}_w2_left")

            block = c.enter_context(nc.Block())

            @block.sync
            def _(sp):
                for p in range(2):
                    stage_weights(sp, stage, p, w2, p, s_stage[p])
                with sp.Fori(1, EXPERTS // 2) as i:
                    for p in range(2):
                        sp.wait_ge(s_lo, 2 * i + p - 1)
                        stage_weights(sp, stage, p, w2, 2 * i + p, s_stage[p])
                sp.dma_start(b1_sb[:, :, :], b1.partition_broadcast(P)).then_inc(s_bias, 16)
                sp.dma_start(b2_sb[:, :, :], b2.partition_broadcast(P)).then_inc(s_bias, 16)
                sp.wait_ge(s_gates, 1)
                sp.dma_start(table[0:TOKENS, D:ROW].rearrange("(t p) n -> p t n", p=P), tmp[:, :, :]).then_inc(s_gout, 16)
                sp.wait_ge(s_gout, 16)
                sp.wait_ge(s_bias, 32)

            @block.gpsimd
            def _(pool):
                left_by_rounding(pool, stage, w2_lo, w2_hi, s_stage, s_lo)
                for q in range(4):
                    pool.wait_ge(s_base, q + 1)
                    pool.tensor_tensor(of_tile[:, q % 2, :, 0, :], in_slot_tile[:, q % 2, :, :],
                                       const("tile1")[:, q * PART:(q + 1) * PART].unsqueeze(2).to_broadcast([P, PART, NS1]),
                                       ALU.mult).then_inc(s_oft, 1)

            @block.scalar
            def _(act):
                act.wait_ge(s_mx, 1)
                act.activation(prob[:, :, :], logit[:, :, :], ACT.Exp, scale=1.0 / TEMP).then_inc(s_ex, 1)
                for q in range(4):
                    act.wait_ge(s_base, q + 1)
                    act.activation(of_tile[:, q % 2, :, 1, :], in_slot_tile[:, q % 2, :, :], ACT.Copy,
                                   scale=const("place")).then_inc(s_ofp, 1)

            @block.vector
            def _(dve):
                steps = Steps(dve, s_dve)
                steps.did(dve.tensor_copy(cb[:, 0:P], const("before")))
                steps.did(dve.tensor_copy(cb[:, P:2 * P], const("ones")))

                def wide(c4):
                    return c4.unsqueeze(2).to_broadcast([P, TILES, EXPERTS])

                def by_expert(c8):
                    return c8.unsqueeze(1).to_broadcast([P, TILES, EXPERTS])

                steps.chain(dve.tensor_tensor(logit[:, :, :], logit[:, :, :], by_expert(bg_sb[:, :]), ALU.add))
                steps.chain(dve.tensor_reduce(col[:, 0, :], logit[:, :, :], AX.X, ALU.max))
                dve.tensor_tensor(logit[:, :, :], logit[:, :, :], wide(col[:, 0, :]), ALU.subtract).then_inc(s_mx, 1)
                dve.wait_ge(s_ex, 1)
                steps.chain(dve.tensor_reduce(col[:, 1, :], prob[:, :, :], AX.X, ALU.add))
                steps.chain(dve.reciprocal(col[:, 2, :], col[:, 1, :]))
                steps.chain(dve.tensor_tensor(prob[:, :, :], prob[:, :, :], wide(col[:, 2, :]), ALU.mult))
                for k, hot in ((0, first), (1, second)):
                    steps.chain(dve.tensor_reduce(col[:, 3 + k, :], prob[:, :, :], AX.X, ALU.max))
                    steps.chain(dve.tensor_tensor(tmp[:, :, :], prob[:, :, :], wide(col[:, 3 + k, :]), ALU.is_equal))
                    steps.chain(dve.tensor_tensor(tmp[:, :, :], tmp[:, :, :], by_expert(const("rank_e")), ALU.mult))
                    steps.chain(dve.tensor_reduce(col[:, 5, :], tmp[:, :, :], AX.X, ALU.max))
                    steps.chain(dve.tensor_tensor(hot[:, :, :], tmp[:, :, :], wide(col[:, 5, :]), ALU.is_equal))
                    if k == 0:
                        steps.chain(dve.scalar_tensor_tensor(prob[:, :, :], hot[:, :, :], -2.0, prob[:, :, :],
                                                             ALU.mult, ALU.add))
                dve.tensor_tensor(either[:, :, :], first[:, :, :], second[:, :, :], ALU.add).then_inc(s_either, 1)
                steps.chain(dve.scalar_tensor_tensor(col[:, 6, :], col[:, 3, :], GATE_EPS, col[:, 4, :], ALU.add, ALU.add))
                steps.chain(dve.reciprocal(col[:, 7, :], col[:, 6, :]))
                steps.chain(dve.tensor_tensor(col[:, 3:5, :], col[:, 3:5, :],
                                              col[:, 7:8, :].to_broadcast([P, 2, TILES]), ALU.mult))
                steps.did(dve.tensor_tensor(tmp[:, :, :], first[:, :, :], wide(col[:, 3, :]), ALU.mult))
                steps.chain(dve.tensor_tensor(prob[:, :, :], second[:, :, :], wide(col[:, 4, :]), ALU.mult))
                dve.tensor_tensor(tmp[:, :, :], tmp[:, :, :], prob[:, :, :], ALU.add).then_inc(s_gates, 1)

                dve.wait_ge(s_cnt, 1)
                steps.chain(dve.tensor_copy(tot[:, :, :], bank[1][:, 0:TILES * EXPERTS].rearrange("p (t e) -> p e t", t=TILES)))
                flat = lambda a: a[:, :, :].rearrange("p a b -> p (a b)")
                steps.chain(dve.tensor_tensor_scan(flat(inc), const("seg"), flat(tot), 0.0, ALU.mult, ALU.add))
                steps.chain(dve.tensor_scalar(e8i[:, 0, :], inc[:, :, TILES - 1], float(P - 1), None, ALU.add))
                steps.chain(dve.tensor_scalar(e8i[:, 1, :], e8i[:, 0, :], 7, None, ALU.logical_shift_right))
                steps.chain(dve.tensor_copy(e8[:, 0, :], e8i[:, 1, :]))
                steps.chain(dve.tensor_tensor_scan(e8[:, 1, :], const("ones")[:, 0:EXPERTS], e8[:, 0, :], 0.0, ALU.mult, ALU.add))
                steps.chain(dve.tensor_tensor(e8[:, 2, :], e8[:, 1, :], e8[:, 0, :], ALU.subtract))
                steps.chain(dve.tensor_scalar(e8[:, 3, :], e8[:, 2, :], float(P), None, ALU.mult))
                steps.chain(dve.tensor_tensor(inc[:, :, :], inc[:, :, :], tot[:, :, :], ALU.subtract))
                steps.chain(dve.tensor_tensor(inc[:, :, :], inc[:, :, :], e8[:, 3, :].unsqueeze(2).to_broadcast([P, EXPERTS, TILES]), ALU.add))
                steps.chain(dve.tensor_tensor(pos[:, :, :], bank[0][:, 0:TILES * EXPERTS].rearrange("p (t e) -> p t e", t=TILES),
                                              inc[:, :, :].rearrange("p e t -> p t e"), ALU.add))
                for k, hot in ((0, first), (1, second)):
                    steps.chain(dve.tensor_tensor(hot[:, :, :], hot[:, :, :], pos[:, :, :], ALU.mult))
                    steps.chain(dve.tensor_reduce(slot[:, 0, k * TILES:(k + 1) * TILES], hot[:, :, :], AX.X, ALU.add))
                steps.chain(dve.tensor_copy(sloti[:, 0, :], slot[:, 0, :]))
                steps.chain(dve.tensor_scalar(sloti[:, 1, :], sloti[:, 0, :], 7, None, ALU.logical_shift_right))
                steps.chain(dve.tensor_scalar(sloti[:, 2, :], sloti[:, 0, :], P - 1, None, ALU.bitwise_and))
                steps.chain(dve.tensor_copy(slot[:, 1:3, :], sloti[:, 1:3, :]))
                iota = const("iota")
                for q in range(4):
                    a, p = slice(q * PART, (q + 1) * PART), q % 2
                    if q >= 2:
                        dve.wait_ge(s_inv, q - 1)
                    dve.tensor_tensor(in_slot_tile[:, p, :, :], iota[:, 0:NS1].unsqueeze(1).to_broadcast([P, PART, NS1]),
                                      slot[:, 1, a].unsqueeze(2).to_broadcast([P, PART, NS1]), ALU.is_equal).then_inc(s_base, 1)
                    dve.tensor_tensor(in_tile[:, p, :, :], iota.unsqueeze(1).to_broadcast([P, PART, P]),
                                      slot[:, 2, a].unsqueeze(2).to_broadcast([P, PART, P]), ALU.is_equal).then_inc(s_onehot, 1)
                steps.chain(dve.tensor_tensor(tile_e[:, :, :], e8[:, 1, :].unsqueeze(1).to_broadcast([P, NS1, EXPERTS]),
                                              iota[:, 0:NS1].unsqueeze(2).to_broadcast([P, NS1, EXPERTS]), ALU.is_le))
                steps.chain(dve.tensor_reduce(idxf[:, 0, :], tile_e[:, :, :], AX.X, ALU.add))
                steps.chain(dve.tensor_scalar(expert[:, :], idxf[:, 0, :], float(EXPERTS - 1), None, ALU.min))
                dve.wait_ge(s_inv, 4)
                steps.chain(dve.tensor_scalar(idxf[:, 0, :], bank[3][:, 0:NS1], 0.0, const("spare1"), ALU.is_equal, ALU.mult))
                steps.chain(dve.scalar_tensor_tensor(idxf[:, 1, :], bank[3][:, 0:NS1], float(P), idxf[:, 0, :], ALU.mult, ALU.add))
                steps.chain(dve.scalar_tensor_tensor(idxf[:, 1, :], bank[3][:, NS1:2 * NS1], float(-P), idxf[:, 1, :], ALU.add, ALU.add))
                dve.tensor_copy(idx[:, :], idxf[:, 1, :]).then_inc(s_idx, 2)

            @block.tensor
            def _(pe):
                pe.wait_ge(s_dve, 2)
                pe.wait_ge(s_either, 1)
                flat = either[:, :, :].rearrange("p t e -> p (t e)")
                pe.matmul(bank[0][:, 0:TILES * EXPERTS], cb[:, 0:P], flat, start=True, stop=True)
                pe.matmul(bank[1][:, 0:TILES * EXPERTS], cb[:, P:2 * P], flat, start=True, stop=True).then_inc(s_cnt, 1)
                for q in range(4):
                    pe.wait_ge(s_onehot, q + 1)
                    pe.wait_ge(s_oft, q + 1)
                    pe.wait_ge(s_ofp, q + 1)
                    for a in range(PART):
                        mm = pe.matmul(bank[3][:, 0:2 * NS1], in_tile[:, q % 2, a, :], of_tile[:, q % 2, a, :, :],
                                       start=(q == 0 and a == 0), stop=(q == 3 and a == PART - 1))
                    mm.then_inc(s_inv, 1)

    def mixture_experts(n, total, w1_lo, w2_lo, b1_sb, b2_sb, idx, expert):
        with ExitStack() as c:
            gather_i = [sb(f"m{n}_gather_i{r}", [P, 1], U32, c=c) for r in range(RING)]
            sum_i = [sb(f"m{n}_sum_i{r}", [P, 1], U32, c=c) for r in range(RING)]
            xg = [sb(f"m{n}_xg{r}", [P, ROW], c=c) for r in range(RING)]
            y_sc = [sb(f"m{n}_y_sc{r}", [P, D], c=c) for r in range(RING)]
            xt_hi = sb(f"m{n}_xt_hi", [P, KC, P], F32R, c=c)
            xt_lo = sb(f"m{n}_xt_lo", [P, KC, P], F32R, c=c)
            h_sb = sb(f"m{n}_h", [P, HID], c=c)
            ht = sb(f"m{n}_ht", [P, HC, P], c=c)
            ht_hi = sb(f"m{n}_ht_hi", [P, HC, P], F32R, c=c)
            ht_lo = sb(f"m{n}_ht_lo", [P, HC, P], F32R, c=c)
            y_sb = sb(f"m{n}_y", [P, D], c=c)
            carry = sb(f"m{n}_carry", [P, 2 * RING + 1], c=c)
            s_carry = sem(f"m{n}_carry_zeroed")
            s_ib = sem(f"m{n}_index_copied")
            s_g = [sem(f"m{n}_gathered{r}") for r in range(RING)]
            s_sum = sem(f"m{n}_summed")
            f_xt, f_xhi, f_xlo = sem(f"m{n}_slot_xt_psum"), sem(f"m{n}_xt_hi_ready"), sem(f"m{n}_xt_lo_ready")
            f_h, f_hb = sem(f"m{n}_h_psum"), sem(f"m{n}_h_biased")
            f_ht = sem(f"m{n}_h_t_psum")
            f_ghi, f_gelu, f_glo = sem(f"m{n}_gelu_hi"), sem(f"m{n}_gelu"), sem(f"m{n}_gelu_lo")
            f_y, f_yb, f_ys = sem(f"m{n}_y_psum"), sem(f"m{n}_y_biased"), sem(f"m{n}_y_gated")

            block = c.enter_context(nc.Block())

            def over_slots(eng, step):
                def one(s, u):
                    step.first, step.last = u == 0, u == TURN - 1
                    step.filled = s // RING if isinstance(s, int) else (TURN // RING) * i + u // RING
                    step(s, u % RING)

                for s in range(TURN):
                    one(s, s)
                with eng.Fori(1, (SLOT_TILES - 1) // TURN) as i:
                    for u in range(TURN):
                        one(TURN * i + u, u)
                for u in range(2):
                    one(SLOT_TILES - 1 + u, u)

            def weights_of(w, e, k):
                return w[:, ds(e, 1), k, :].rearrange("p a n -> p (a n)")

            @block.gpsimd
            def _(pool):
                pool.memset(carry[:, :], 0.0).then_inc(s_carry, 1)
                pool.wait_ge(s_carry, 1)

                def carry_wait(place):
                    pool.tensor_tensor(carry[:, place:place + 1], carry[:, 2 * RING:], carry[:, 2 * RING:], ALU.add)

                def gather(s, r, copies):
                    pool.tensor_copy(gather_i[r][:, :], idx[:, ds(s, 1)]).then_inc(s_ib, 1)
                    pool.wait_ge(s_ib, copies)
                    carry_wait(r)
                    pool.indirect_dma_start(xg[r][:, :], None, table,
                                            bass.IndirectOffsetOnAxis(gather_i[r][:, 0:1], 0)).then_inc(s_g[r], 16)

                def step(s, r):
                    if isinstance(s, int) and s == SLOT_TILES:
                        return
                    ahead = not isinstance(s, int) or s + RING < SLOT_TILES
                    copies = (2 * s if not isinstance(s, int) or s + RING < SLOT_TILES else SLOT_TILES - RING + s) + RING
                    pool.tensor_copy(sum_i[r][:, :], idx[:, ds(s, 1)]).then_inc(s_ib, 1)
                    pool.wait_ge(s_ib, copies + 1)
                    pool.wait_ge(f_ys, s + 1)
                    if not isinstance(s, int) or s >= 1:
                        pool.wait_ge(s_sum, 16 * s)
                    carry_wait(RING + r)
                    pool.indirect_dma_start(total, bass.IndirectOffsetOnAxis(sum_i[r][:, 0:1], 0), y_sc[r][:, :], None,
                                            compute_op=ALU.add).then_inc(s_sum, 16)
                    if ahead:
                        gather(s + RING, r, copies + 2)

                for s in range(RING):
                    gather(s, s, s + 1)
                for s in range(RING):
                    step(s, s)
                with pool.Fori(1, (SLOT_TILES - 1) // RING - 1) as i:
                    for u in range(RING):
                        step(RING * i + u, u)
                for s in range(SLOT_TILES - 1 - RING, SLOT_TILES):
                    step(s, s % RING)
                pool.wait_ge(s_sum, 16 * SLOT_TILES)

            @block.scalar
            def _(act):
                def round_slots(s, r):
                    act.wait_ge(f_xt, s + 1)
                    if not isinstance(s, int) or s >= 1:
                        act.wait_ge(f_h, s)
                    act.activation(xt_hi[:, :, :], bank[0][:, 0:D].rearrange("p (c n) -> p c n", c=KC),
                                   ACT.Copy).then_inc(f_xhi, 1)

                def step(s, r):
                    if not isinstance(s, int) or s >= 1:
                        e = act.value_load(expert[0:1, ds(s - 1, 1)], min_val=0, max_val=EXPERTS - 1)
                    if not isinstance(s, int) or s < SLOT_TILES - 1:
                        round_slots(s + 1, (r + 1) % RING)
                    if not isinstance(s, int) or s < SLOT_TILES:
                        act.wait_ge(f_ht, s + 1)
                        if not isinstance(s, int) or s >= 1:
                            act.wait_ge(f_y, s)
                        in_bank = bank[2][:, :].rearrange("p (c n) -> p c n", c=HC)
                        act.activation(ht_hi[:, :, :], in_bank, ACT.Gelu).then_inc(f_ghi, 1)
                        act.activation(ht[:, :, :], in_bank, ACT.Gelu).then_inc(f_gelu, 1)
                    if not isinstance(s, int) or s >= 1:
                        if not isinstance(s, int) or s >= RING + 1:
                            act.wait_ge(s_sum, 16 * (s - RING))
                        q = (r - 1) % RING
                        act.wait_ge(f_yb, s)
                        act.activation(y_sc[q][:, :], y_sb[:, :], ACT.Copy,
                                       scale=xg[q][:, ds(e + D, 1)]).then_inc(f_ys, 1)

                round_slots(0, 0)
                over_slots(act, step)

            @block.vector
            def _(dve):
                def load(s):
                    return dve.value_load(expert[0:1, ds(s, 1)], min_val=0, max_val=EXPERTS - 1)

                def left(s):
                    dve.wait_ge(f_xhi, s + 1)
                    dve.tensor_tensor(xt_lo[:, :, :], bank[0][:, 0:D].rearrange("p (c n) -> p c n", c=KC),
                                      xt_hi[:, :, :].bitcast(F32), ALU.subtract).then_inc(f_xlo, 1)

                def step(s, r):
                    if step.first or step.now is None:
                        step.now = load(s) if not isinstance(s, int) or s < SLOT_TILES else None
                        step.before = load(s - 1) if not isinstance(s, int) or s >= 1 else None
                    now, before = step.now, step.before
                    if not isinstance(s, int) or s < SLOT_TILES:
                        dve.wait_ge(f_h, s + 1)
                        if not isinstance(s, int) or s >= 1:
                            dve.wait_ge(f_ht, s)
                        dve.tensor_tensor(h_sb[:, :], bank[1][:, :], b1_sb[:, ds(now, 1), :].rearrange("p a n -> p (a n)"), ALU.add).then_inc(f_hb, 1)
                    if not isinstance(s, int) or s < SLOT_TILES - 1:
                        left(s + 1)
                    if not isinstance(s, int) or s >= 1:
                        dve.wait_ge(f_y, s)
                        if not isinstance(s, int) or s >= 2:
                            dve.wait_ge(f_ys, s - 1)
                        dve.tensor_tensor(y_sb[:, :], bank[3][:, 0:D], b2_sb[:, ds(before, 1), :].rearrange("p a n -> p (a n)"), ALU.add).then_inc(f_yb, 1)
                    if not isinstance(s, int) or s < SLOT_TILES:
                        step.before = now
                        step.now = load(s + 1) if not step.last and (not isinstance(s, int) or s < SLOT_TILES - 1) else None
                        dve.wait_ge(f_gelu, s + 1)
                        dve.tensor_tensor(ht_lo[:, :, :], ht[:, :, :], ht_hi[:, :, :].bitcast(F32), ALU.subtract).then_inc(f_glo, 1)

                step.now = step.before = None
                left(0)
                over_slots(dve, step)

            @block.tensor
            def _(pe):
                def turn(s, r, filled):
                    pe.wait_ge(s_g[r], 16 * filled)
                    if not isinstance(s, int) or s >= 1:
                        pe.wait_ge(f_xlo, s)
                    for k in range(KC):
                        mm = pe.transpose(bank[0][:, k * P:(k + 1) * P], xg[r][:, k * P:(k + 1) * P], ident)
                    mm.then_inc(f_xt, 1)

                def product(to, hi, lo, w_hi, w_lo, e, chunks, s, lo_ready, done):
                    multiply(pe, to, lambda k: hi[:, k, :], lambda k: lo[:, k, :], lambda k: weights_of(w_hi, e, k),
                             lambda k: weights_of(w_lo, e, k), chunks, lambda: pe.wait_ge(lo_ready, s + 1), done)

                def load(s):
                    return pe.value_load(expert[0:1, ds(s, 1)], min_val=0, max_val=EXPERTS - 1)

                def step(s, r):
                    static = isinstance(s, int)
                    if not static or s < SLOT_TILES:
                        if step.first or step.now is None:
                            step.now = load(s)
                        pe.wait_ge(f_xhi, s + 1)
                        if not static or s >= 1:
                            pe.wait_ge(f_hb, s)
                        product(bank[1][:, :], xt_hi, xt_lo, w1_hi, w1_lo, step.now, KC, s, f_xlo, f_h)
                    if not static or s < SLOT_TILES - 1:
                        turn(s + 1, (r + 1) % RING, step.filled + (2 if r == RING - 1 else 1))
                    if not static or s >= 1:
                        if step.first or step.before is None:
                            step.before = load(s - 1)
                        pe.wait_ge(f_ghi, s)
                        if not static or s >= 2:
                            pe.wait_ge(f_yb, s - 1)
                        product(bank[3][:, 0:D], ht_hi, ht_lo, w2_hi, w2_lo, step.before, HC, s - 1, f_glo, f_y)
                    step.before = step.now
                    step.now = load(s + 1) if not step.last and (not static or s < SLOT_TILES - 1) else None
                    if not static or s < SLOT_TILES:
                        pe.wait_ge(f_hb, s + 1)
                        if not static or s >= 1:
                            pe.wait_ge(f_gelu, s)
                        for k in range(HC):
                            mm = pe.transpose(bank[2][:, k * P:(k + 1) * P], h_sb[:, k * P:(k + 1) * P], ident)
                        mm.then_inc(f_ht, 1)

                step.now = step.before = None
                turn(0, 0, 1)
                over_slots(pe, step)

    def linear_attention():
        with ExitStack() as c:
            x_sb = sb("b_x_sb", [P, TILES, D], c=c)
            rows = sb("b_rows_sb", [P, 2, GT, D], c=c)
            xn_hi, xn_lo = (sb(f"b_xn_{part}", [P, KC, GN], F32R, c=c) for part in ("hi", "lo"))
            w_hi, w_lo = (sb(f"b_w_{part}", [P, KC, 3 * D], F32R, c=c) for part in ("hi", "lo"))
            wo_sb = sb("wo_sb", [P, KC, D], c=c)
            bq_sb = sb("bq_sb", [P, KC], c=c)
            bk_sb = sb("bk_sb", [P, D], c=c)
            bv_sb = sb("bv2_sb", [P, D], c=c)
            bo_sb = sb("bo_sb", [P, D], c=c)
            q_t = sb("q2_t", [P, KC, BATCH, SEQ], c=c)
            q_flat = q_t[:, :, :, :].rearrange("p c b n -> p c (b n)")
            k_sb = sb("k2_sb", [P, 2, D], c=c)
            kf = sb("kf", [P, 2, GT, D], c=c)
            v1 = sb("v1", [P, 2, GT, KC, VW], c=c)
            part = sb("part", [P, GROUPS, KC, VW], c=c)
            kv = sb("kv", [P, KC, VW], c=c)
            kvm = sb("kvm", [P, BATCH, KC, NW], c=c)
            w_in = part[:, :, :, :].rearrange("p g c n -> p (g c n)")[:, 0:KC * 3 * D].rearrange("p (c n) -> p c n", c=KC)
            q_g = kf[:, :, :, :].rearrange("p a t n -> p a (t n)").rearrange("p a (c n) -> p a c n", c=KC)
            den = sb("den", [P, GT, KC, HG], c=c)
            rden = sb("rden", [P, GT, KC, HG], c=c)
            o_rows = rows
            o_t2 = v1[:, :, :, :, :].rearrange("p a t c n -> p (a t c n)")[:, 0:2 * KC * GN]
            o_t = [o_t2[:, p * KC * GN:(p + 1) * KC * GN].rearrange("p (c n) -> p c n", c=KC) for p in range(2)]

            s_w = sem("b_weights")
            s_x, s_xout = sem("b_x"), sem("b_x_out")
            s_st = sem("b_x_statistics")
            s_ones = sem("b_ones")
            s_dve = sem("b_dve_steps")
            s_bo = sem("b_x_biased")
            s_rows = sem("b_rows")
            s_whi, s_wlo = sem("b_w_hi_ready"), sem("b_w_lo_ready")
            s_xt, s_xhi, s_xlo = sem("b_xt_psum"), sem("b_xn_hi_ready"), sem("b_xn_lo_ready")
            s_kv, s_k, s_v = sem("b_kv_psum"), sem("b_k"), sem("b_v")
            s_kf = sem("b_kf")
            s_q, s_qs, s_qg = sem("b_q_psum"), sem("b_q"), sem("b_q_group")
            s_kvp, s_part = sem("b_part_psum"), sem("b_part")
            s_kvm = sem("b_kv_masked")
            s_od, s_os = sem("b_out_psum"), sem("b_out_rows")
            s_ot, s_ots = sem("b_out_t_psum"), sem("b_out_t")
            s_y, s_ys = sem("b_y_psum"), sem("b_y")

            def over_outputs(eng, step, steps=None, per_step=0):
                for g in range(3):
                    step(g, g % 2)
                start = steps.n if steps else 0
                with eng.Fori(1, GROUPS // 2 - 1) as i:
                    if steps:
                        steps.base, steps.n = start + (i - 1) * (2 * per_step), 0
                    step(2 * i + 1, 1)
                    step(2 * i + 2, 0)
                    assert not steps or steps.n == 2 * per_step
                if steps:
                    steps.base, steps.n = 0, start + (GROUPS - 4) * per_step
                for g in range(GROUPS - 1, GROUPS + 2):
                    step(g, g % 2)

            block = c.enter_context(nc.Block())

            @block.sync
            def _(sp):
                sp.dma_start(x_sb[:, 0:GT, :], tiled(acc1, 0, D)).then_inc(s_x, 16)
                with sp.Fori(1, GROUPS) as g:
                    sp.wait_ge(s_x, 16 * g)
                    sp.dma_start(x_sb[:, ds(g * GT, GT), :], tiled(acc1, g, D)).then_inc(s_x, 16)
                with sp.Fori(0, GROUPS) as g:
                    sp.wait_ge(s_ys, 2 * g + 2)
                    sp.dma_start(tiled(out, g, D), x_sb[:, ds(g * GT, GT), :]).then_inc(s_xout, 16)
                sp.wait_ge(s_xout, 16 * GROUPS)

            @block.scalar
            def _(act):
                for to, of in ((w_in[:, :, 0:D], wk_t), (w_in[:, :, D:2 * D], wv_t), (w_in[:, :, 2 * D:3 * D], wq_t), (wo_sb[:, :, :], wo_t)):
                    act.dma_start(to, of.rearrange("(c p) n -> p c n", p=P)).then_inc(s_w, 16)
                act.dma_start(bq_sb[:, :], bq_cols).then_inc(s_w, 16)
                for to, of in ((bk_sb, b_k), (bv_sb, b_v), (bo_sb, b_o)):
                    act.dma_start(to[:, :], of.partition_broadcast(P)).then_inc(s_w, 16)
                act.wait_ge(s_w, 16 * 8)

                def copy_rows(g):
                    if not isinstance(g, int) or g >= 1:
                        act.wait_ge(s_kv, GT * g)
                    act.wait_ge(s_xt, g + 1)
                    for k in range(KC):
                        act.activation(xn_hi[:, k, :], bank[k][:, :], ACT.Copy).then_inc(s_xhi, 1)

                def step(g, p):
                    static = isinstance(g, int)
                    if static and g == GROUPS:
                        return
                    if not static or g >= 2:
                        act.wait_ge(s_kvp, g - 1)
                    for t in range(GT):
                        act.wait_ge(s_k, GT * g + t + 1)
                        at = CONST_COLS["dec"][0]
                        tile = (g % (GROUPS // BATCH)) * GT + t
                        act.activation(kf[:, p, t, :], k_sb[:, t % 2, :], ACT.Relu,
                                       scale=cst[:, ds(at + tile, 1)]).then_inc(s_kf, 1)
                    for m in range(KC):
                        act.wait_ge(s_q, KC * g + m + 1)
                        act.activation(q_flat[:, m, ds(g * GN, GN)], bank[2 + m][:, :], ACT.Relu,
                                       bias=bq_sb[:, m:m + 1]).then_inc(s_qs, 1)
                    if not static or g < GROUPS - 1:
                        copy_rows(g + 1)

                act.activation(w_hi[:, :, :], w_in, ACT.Copy).then_inc(s_whi, 1)
                copy_rows(0)
                over_groups(act, step, 2)

                def copy_q(g, p):
                    if not isinstance(g, int) or g >= 2:
                        act.wait_ge(s_od, GT * (g - 1))
                    act.activation(q_g[:, p, :, :], q_flat[:, :, ds(g * GN, GN)], ACT.Copy).then_inc(s_qg, 1)

                def out_step(g, p):
                    if not isinstance(g, int) or g < GROUPS:
                        copy_q(g, p)
                    if not isinstance(g, int) or 1 <= g <= GROUPS:
                        act.wait_ge(s_ot, g)
                        if not isinstance(g, int) or g >= 3:
                            act.wait_ge(s_y, 2 * (g - 2))
                        for k in range(KC):
                            act.activation(o_t[1 - p][:, k, :], bank[4 + k][:, :], ACT.Copy).then_inc(s_ots, 1)

                act.wait_ge(s_qs, KC * GROUPS)
                act.wait_ge(s_kvp, GROUPS)
                over_outputs(act, out_step)

            @block.gpsimd
            def _(pool):
                pool.memset(v1[:, :, :, :, P:VW], 1.0).then_inc(s_ones, 1)
                pool.wait_ge(s_w, 16 * 8)
                with pool.Fori(0, GROUPS) as g:
                    pool.wait_ge(s_rows, GT * g + GT)
                    pool.tensor_tensor(x_sb[:, ds(g * GT, GT), :], x_sb[:, ds(g * GT, GT), :],
                                       bo_sb[:, :].unsqueeze(1).to_broadcast([P, GT, D]), ALU.add).then_inc(s_bo, 1)

            @block.vector
            def _(dve):
                steps = Steps(dve, s_dve)

                def front(g, p, between=()):
                    dve.wait_ge(s_x, 16 * g + 16)
                    measure(dve, steps, lambda t: tile_of(x_sb, g, t))
                    for w in between[0:1]:
                        w()
                    between = between[1:]
                    steps.wait()
                    moments(dve, steps, GT, between=between)
                    if not isinstance(g, int) or g >= 2:
                        dve.wait_ge(s_xt, g - 1)
                    normalise(dve, rows, p, lambda t: tile_of(x_sb, g, t), s_rows)

                def nothing():
                    pass

                def biased(g, p, t):
                    static = isinstance(g, int)
                    if t == 0 and (not static or g >= 2):
                        dve.wait_ge(s_kvp, g - 1)
                    dve.wait_ge(s_kv, GT * g + t + 1)
                    if static and GT * g + t >= 2 or not static:
                        dve.wait_ge(s_kf, GT * g + t - 1)
                    b = bank[4 + t % 2]
                    dve.tensor_tensor(k_sb[:, t % 2, :], b[:, 0:D], bk_sb[:, :], ALU.add).then_inc(s_k, 1)
                    dve.tensor_tensor(v1[:, p, t, :, 0:P], b[:, D:2 * D].rearrange("p (c n) -> p c n", c=KC),
                                      bv_sb[:, :].rearrange("p (c n) -> p c n", c=KC), ALU.add).then_inc(s_v, 1)

                def step(g, p):
                    static = isinstance(g, int)
                    if not static or g < GROUPS:
                        work = [lambda t=t: biased(g, p, t) for t in range(GT)]
                        if not static or g < GROUPS - 1:
                            front(g + 1, 1 - p, [work[0], work[1], nothing, nothing, nothing, nothing, work[2]])
                            work[3]()
                        else:
                            for w in work:
                                w()
                        if not static or g < GROUPS - 1:
                            left(g + 1)
                    if not static or g >= 1:
                        for k in range(KC):
                            dve.wait_ge(s_kvp, g)
                            dve.tensor_copy(part[:, ds(g - 1, 1), k, :].rearrange("p a n -> p (a n)"), bank[6 + k][:, 0:VW]).then_inc(s_part, 1)

                def left(g):
                    if not isinstance(g, int) or g >= 1:
                        dve.wait_ge(s_kv, GT * g)
                    for k in range(KC):
                        dve.wait_ge(s_xhi, KC * g + k + 1)
                        dve.tensor_tensor(xn_lo[:, k, :], bank[k][:, :], xn_hi[:, k, :].bitcast(F32),
                                          ALU.subtract).then_inc(s_xlo, 1)

                front(0, 0)
                dve.wait_ge(s_w, 16 * 8)
                dve.wait_ge(s_ones, 1)
                dve.wait_ge(s_whi, 1)
                dve.tensor_tensor(w_lo[:, :, :], w_in, w_hi[:, :, :].bitcast(F32), ALU.subtract).then_inc(s_wlo, 1)
                left(0)
                over_groups(dve, step, 2, steps, GT + MOMENT_STEPS)
                dve.wait_ge(s_part, KC * GROUPS)
                GB = GROUPS // BATCH
                block_mask = const("head_block")[:, 0:P].unsqueeze(1).to_broadcast([P, KC, P])
                head_mask = const("head_block")[:, P:NW].unsqueeze(1).to_broadcast([P, KC, HG])
                for b in range(BATCH):
                    steps.chain(dve.tensor_tensor(kv[:, :, :], part[:, b * GB, :, :], part[:, b * GB + 1, :, :], ALU.add))
                    for a in range(2, GB):
                        steps.chain(dve.tensor_tensor(kv[:, :, :], kv[:, :, :], part[:, b * GB + a, :, :], ALU.add))
                    dve.tensor_tensor(kvm[:, b, :, P:NW], kv[:, :, P:P + 1].to_broadcast([P, KC, HG]), head_mask,
                                      ALU.mult).then_inc(s_kvm, 1)
                    dve.tensor_tensor(kvm[:, b, :, 0:P], kv[:, :, 0:P], block_mask, ALU.mult).then_inc(s_kvm, 1)
                    dve.wait_ge(s_kvm, 2 * b + 2)

                def by_head(t):
                    return bank[t][:, 0:KC * NW].rearrange("p (k n) -> p k n", k=KC)

                def divide(g, p):
                    at = CONST_COLS["dec"][0] + (g % GB) * GT
                    for t in range(GT):
                        dve.wait_ge(s_od, GT * g + t + 1)
                        steps.did(dve.tensor_scalar(den[:, t, :, :], by_head(t)[:, :, P:NW], cst[:, ds(at + t, 1)], DEN_EPS,
                                                    ALU.mult, ALU.add))
                    steps.wait()
                    steps.chain(dve.reciprocal(rden[:, :, :, :], den[:, :, :, :]))
                    steps.chain(dve.tensor_tensor(rden[:, :, :, :].rearrange("p t k h -> p t (k h)"),
                                                  rden[:, :, :, :].rearrange("p t k h -> p t (k h)"),
                                                  cst[:, ds(at, GT)].unsqueeze(2).to_broadcast([P, GT, HEADS]), ALU.mult))
                    if not isinstance(g, int) or g >= 2:
                        dve.wait_ge(s_ot, g - 1)
                    for t in range(GT):
                        dve.tensor_tensor(o_rows[:, p, t, :].rearrange("p (k h n) -> p k h n", k=KC, h=HG),
                                          by_head(t)[:, :, 0:P].rearrange("p k (h n) -> p k h n", h=HG),
                                          rden[:, t, :, :].unsqueeze(3).to_broadcast([P, KC, HG, DK]), ALU.mult).then_inc(s_os, 1)

                DIVIDE_STEPS = GT + 2

                def residual(g):
                    for h in range(2):
                        dve.wait_ge(s_y, 2 * g + h + 1)
                        xs = x_sb[:, ds(g * GT + 2 * h, 2), :]
                        dve.tensor_tensor(xs, bank[6 + h][:, :].rearrange("p (t n) -> p t n", t=2), xs, ALU.add).then_inc(s_ys, 1)

                def out_step(g, p):
                    if not isinstance(g, int) or g < GROUPS:
                        divide(g, p)
                    if not isinstance(g, int) or g >= 2:
                        residual(g - 2)
                        dve.wait_ge(s_ys, 2 * (g - 1))
                        measure_x(dve, x_sb, g - 2, s_st)

                dve.wait_ge(s_bo, GROUPS)
                over_outputs(dve, out_step, steps, DIVIDE_STEPS)
                dve.wait_ge(s_st, TILES)

            @block.tensor
            def _(pe):

                def turn(g, p):
                    pe.wait_ge(s_rows, GT * (g + 1))
                    transpose_rows(pe, rows, p, bank[0:2], s_xt)

                def project(g, p):
                    static = isinstance(g, int)
                    pe.wait_ge(s_xhi, KC * (g + 1))

                    def lo_is_ready():
                        pe.wait_ge(s_xlo, KC * (g + 1))

                    def k_and_v(t):
                        if not static or GT * g + t >= 2:
                            pe.wait_ge(s_v, GT * g + t - 1)
                        rows_t = slice(t * P, (t + 1) * P)
                        multiply(pe, bank[4 + t % 2][:, :], lambda k: xn_hi[:, k, rows_t], lambda k: xn_lo[:, k, rows_t],
                                 lambda k: w_hi[:, k, 0:2 * D], lambda k: w_lo[:, k, 0:2 * D], KC, lo_is_ready, s_kv)

                    def q_chunk(m):
                        if not static or g >= 1:
                            pe.wait_ge(s_qs, KC * (g - 1) + m + 1)
                        cols = slice(2 * D + m * P, 2 * D + (m + 1) * P)
                        multiply(pe, bank[2 + m][:, :], lambda k: w_hi[:, k, cols], lambda k: w_lo[:, k, cols],
                                 lambda k: xn_hi[:, k, :], lambda k: xn_lo[:, k, :], KC, lo_is_ready, s_q)

                    k_and_v(0)
                    k_and_v(1)
                    q_chunk(0)
                    k_and_v(2)
                    q_chunk(1)
                    k_and_v(3)

                def parts(g, p):
                    static = isinstance(g, int)
                    pe.wait_ge(s_kf, GT * (g + 1))
                    pe.wait_ge(s_v, GT * (g + 1))
                    if not static or g >= 1:
                        pe.wait_ge(s_part, KC * g)
                    for k in range(KC):
                        for t in range(GT):
                            mm = pe.matmul(bank[6 + k][:, 0:VW], kf[:, p, t, k * P:(k + 1) * P], v1[:, p, t, k, :],
                                           start=(t == 0), stop=(t == GT - 1))
                    mm.then_inc(s_kvp, 1)

                def step(g, p):
                    if not isinstance(g, int) or g < GROUPS:
                        project(g, p)
                    if not isinstance(g, int) or g < GROUPS - 1:
                        turn(g + 1, 1 - p)
                    if not isinstance(g, int) or g >= 1:
                        parts(g - 1, 1 - p)

                turn(0, 0)
                pe.wait_ge(s_wlo, 1)
                over_groups(pe, step, 2)

                pe.wait_ge(s_kvm, 2 * BATCH)

                def outputs(g, p):
                    static = isinstance(g, int)
                    pe.wait_ge(s_qg, g + 1)
                    b = g // (GROUPS // BATCH)
                    for t in range(GT):
                        if not static or g >= 1:
                            pe.wait_ge(s_os, GT * (g - 1) + t + 1)
                        for k in range(KC):
                            of = kvm[:, ds(b, 1), k, :].rearrange("p a n -> p (a n)")
                            mm = pe.matmul(bank[t][:, k * NW:(k + 1) * NW], q_g[:, p, k, t * P:(t + 1) * P], of,
                                           start=True, stop=True)
                        mm.then_inc(s_od, 1)

                def turn_outputs(g, p):
                    static = isinstance(g, int)
                    pe.wait_ge(s_os, GT * (g + 1))
                    if not static or g >= 1:
                        pe.wait_ge(s_ots, KC * g)
                    transpose_rows(pe, rows, p, bank[4:6], s_ot)

                def mix(g, p):
                    static = isinstance(g, int)
                    pe.wait_ge(s_ots, KC * (g + 1))
                    for h in range(2):
                        if not static or g >= 1:
                            pe.wait_ge(s_ys, 2 * (g - 1) + h + 1)
                        for t in (2 * h, 2 * h + 1):
                            for k in range(KC):
                                mm = pe.matmul(bank[6 + h][:, (t % 2) * D:(t % 2 + 1) * D], o_t[p][:, k, t * P:(t + 1) * P],
                                               wo_sb[:, k, :], start=(k == 0), stop=(k == KC - 1))
                        mm.then_inc(s_y, 1)

                def out_step(g, p):
                    static = isinstance(g, int)
                    if not static or g < GROUPS:
                        outputs(g, p)
                    if not static or 1 <= g <= GROUPS:
                        turn_outputs(g - 1, 1 - p)
                    if not static or g >= 2:
                        mix(g - 2, p)

                over_outputs(pe, out_step)

    with nc.cleanup_on_exit():
        attention()
        mixture(1, acc1)
        linear_attention()
    mixture(2, out)


def constants():
    import numpy as np
    p = np.arange(P)[:, None]
    i = np.arange(P)[None, :]
    scale = 1.0 / np.sqrt(D * SPAN)
    own = ((p <= i) & (i - p < SPAN)) * scale
    prev = (p > i[:, 0:SPAN] + P - SPAN) * scale
    first = np.concatenate([prev * (g % (GROUPS // BATCH) != 0) for g in range(GROUPS)], axis=1)
    decay = np.exp(-(np.arange(SEQ) / SEQ))
    pair_tile = np.arange(PAIRS) % TILES
    parts = {
        "ident": p == i, "mask_own": own, "mask_prev": prev, "mask_first": first, "before": p < i, "ones": np.ones((P, P)),
        "dec": decay.reshape(SEQ // P, P).T, "rank_e": EXPERTS - np.arange(EXPERTS)[None, :] + 0 * p,
        "seg": (np.arange(EXPERTS * TILES) % TILES != 0)[None, :] + 0 * p, "iota": i + 0 * p,
        "tile1": pair_tile[None, :] + 1 + 0 * p, "place": p, "spare1": TOKENS + P + p, "head_block": np.concatenate([p // DK == i // DK, p // DK == i[:, 0:HG]], axis=1),
    }
    table = np.zeros((P, CONST_W), np.float32)
    for name, a in parts.items():
        at, n = CONST_COLS[name]
        table[:, at:at + n] = a
    return table


def kernel(L0_attn_a_x, L0_attn_a_W_qkv, L0_attn_a_b_qkv, L0_attn_a_ln_w, L0_attn_a_ln_b, L0_attn_b_W_q, L0_attn_b_b_q,
           L0_attn_b_W_k, L0_attn_b_b_k, L0_attn_b_W_v, L0_attn_b_b_v, L0_attn_b_W_o, L0_attn_b_b_o, L0_ffn_Wg, L0_ffn_bg,
           L0_ffn_W1, L0_ffn_b1, L0_ffn_W2, L0_ffn_b2):
    import numpy as np
    import concourse.bacc as bacc
    from concourse.bass_utils import run_bass_kernel_spmd

    table = constants()
    a = np.asarray
    arrays = {
        "x": a(L0_attn_a_x).reshape(TOKENS, D), "w_qkv": a(L0_attn_a_W_qkv), "bqkv_cols": a(L0_attn_a_b_qkv).reshape(3 * KC, P).T,
        "b_qkv": a(L0_attn_a_b_qkv),
        "ln_w": a(L0_attn_a_ln_w), "ln_b": a(L0_attn_a_ln_b),
        "wq_t": a(L0_attn_b_W_q).T, "bq_cols": a(L0_attn_b_b_q).reshape(KC, P).T, "wk_t": a(L0_attn_b_W_k).T, "b_k": a(L0_attn_b_b_k),
        "wv_t": a(L0_attn_b_W_v).T, "b_v": a(L0_attn_b_b_v), "wo_t": a(L0_attn_b_W_o).T, "b_o": a(L0_attn_b_b_o),
        "wg": a(L0_ffn_Wg), "bg": a(L0_ffn_bg), "w1": a(L0_ffn_W1), "b1": a(L0_ffn_b1), "w2": a(L0_ffn_W2),
        "b2": a(L0_ffn_b2), "consts": table,
    }
    arrays = {n: np.ascontiguousarray(v) for n, v in arrays.items()}
    nc = bacc.Bacc("TRN2", target_bir_lowering=False, num_devices=1)
    args = [nc.dram_tensor(f"in_{n}", v.shape, mybir.dt.from_np(v.dtype), kind="ExternalInput").ap()
            for n, v in arrays.items()]
    out = nc.dram_tensor("out_x", (TOKENS + SPARE, D), F32, kind="ExternalOutput").ap()
    program(nc, *args, out)
    r = run_bass_kernel_spmd(nc, [{f"in_{n}": v for n, v in arrays.items()}], core_ids=[0])
    return np.asarray(r.results[0]["out_x"])[0:TOKENS].reshape(BATCH, SEQ, D)
```
